# Optimizing a Trainium2 kernel written in Bass

```python
import numpy as np
import jax
import jax.numpy as jnp

def _softmax(x, axis=-1):
    return jax.nn.softmax(x, axis=axis)

def _gelu(x):
    return jax.nn.gelu(x, approximate=True)

def _silu(x):
    return jax.nn.silu(x)

def _sigmoid(x):
    return jax.nn.sigmoid(x)

def _layernorm(x, axis=-1, eps=1e-05):
    m = jnp.mean(x, axis=axis, keepdims=True)
    v = jnp.var(x, axis=axis, keepdims=True)
    return (x - m) / jnp.sqrt(v + eps)

def _scatter_add(tgt, idx, src, axis=0):
    return tgt.at[idx].add(src)

def _segment_sum(src, seg, n):
    return jax.ops.segment_sum(src, seg, n)
kernel_name = 'mk_xattn_ffn_d2_seqx_r8_23fccf'

def setup_inputs(seed: int=0):
    np.random.seed(seed)
    _w = jnp.asarray

    def _rec_inputs():
        import jax
        import jax.numpy as jnp
        _rk = jax.random.key(seed)
        x = -0.0002928 + 1 * jax.random.normal(jax.random.fold_in(_rk, 1), (16, 56, 128), jnp.float32)
        _lenS = 56 - jax.random.randint(jax.random.fold_in(_rk, 7), (16,), 0, max(1, 56 // 4) + 1, jnp.int32)
        _lenS2 = 1500 - jax.random.randint(jax.random.fold_in(_rk, 8), (16,), 0, max(1, 1500 // 4) + 1, jnp.int32)
        _ctx_512P = jax.random.normal(jax.random.fold_in(_rk, 11), (16, 16, 64), jnp.float32)
        _ctx_512c = jax.random.dirichlet(jax.random.fold_in(_rk, 511), 0.3 * jnp.ones((16,), jnp.float32), (16, 1500))
        _ctx_512t = jnp.einsum('bsk,bkd->bsd', _ctx_512c, _ctx_512P)
        _ctx_512t = _ctx_512t * jax.lax.rsqrt(jnp.mean(jnp.square(_ctx_512t)) + 1e-12) * 0.953939
        ctx_512 = 0.00222621 + 0.99962 * (_ctx_512t + 0.3 * jax.random.normal(jax.random.fold_in(_rk, 611), (16, 1500, 64), jnp.float32))
        return (x, ctx_512)
    x, ctx_512 = _rec_inputs()

    def _L0_xattn_setup():
        import jax, jax.numpy as jnp
        import numpy as np
        H, D, C1, C2, S, M, B, W = (16, 32, 128, 64, 256, 64, 2, 4)

        def _ln(x, g, b):
            m = jnp.mean(x, -1, keepdims=True)
            v = jnp.var(x, -1, keepdims=True)
            return (x - m) * jax.lax.rsqrt(v + 1e-05) * g + b

        def _mha(x, y, wq, wk, wv, li1_w, li1_b, lnx_g, lnx_b, lny_g, lny_b, ln3_g, ln3_b, li2_w, li2_b, li3_w, li3_b, causal):
            xn = _ln(x, lnx_g, lnx_b)
            yn = _ln(y, lny_g, lny_b)
            q = jnp.einsum('bsc,hcd->bhsd', xn, wq)
            k = jnp.einsum('btc,hcd->bhtd', yn, wk)
            v = jnp.einsum('btc,hcd->bhtd', yn, wv)
            a = jax.nn.softmax(jnp.einsum('bhsd,bhtd->bhst', q, k) * D ** (-0.5), axis=-1)
            if causal:
                s, t = (a.shape[-2], a.shape[-1])
                mask = (jnp.arange(t)[None, :] > jnp.arange(s)[:, None]).astype(a.dtype)
                a = a * mask
            o = jnp.einsum('bhst,bhtd->bhsd', a, v)
            o = o.transpose(0, 2, 1, 3).reshape(x.shape[0], x.shape[1], H * D)
            x_out = x + o @ li1_w + li1_b
            h = jax.nn.gelu(_ln(x_out, ln3_g, ln3_b) @ li2_w + li2_b, approximate=False)
            return x_out + h @ li3_w + li3_b
        key = jax.random.key(seed)
        ks = iter(jax.random.split(key, 64))

        def w(shape, scale=0.02):
            return jax.random.normal(next(ks), shape, jnp.float32) * scale
        inp = {'xx': jax.random.normal(next(ks), (B, S, C1), jnp.float32), 'ee': jax.random.normal(next(ks), (B, M, C2), jnp.float32), 'ln1_g': jnp.ones(C1, jnp.float32), 'ln1_b': jnp.zeros(C1, jnp.float32), 'ln2_g': jnp.ones(C1, jnp.float32), 'ln2_b': jnp.zeros(C1, jnp.float32)}
        for pfx, cy in (('a1', C1), ('a2', C2)):
            inp[pfx + '_wq'] = w((H, C1, D))
            inp[pfx + '_wk'] = w((H, cy, D))
            inp[pfx + '_wv'] = w((H, cy, D))
            inp[pfx + '_li1_w'] = w((H * D, C1))
            inp[pfx + '_li1_b'] = jnp.zeros(C1, jnp.float32)
            inp[pfx + '_lnx_g'] = jnp.ones(C1, jnp.float32)
            inp[pfx + '_lnx_b'] = jnp.zeros(C1, jnp.float32)
            inp[pfx + '_lny_g'] = jnp.ones(cy, jnp.float32)
            inp[pfx + '_lny_b'] = jnp.zeros(cy, jnp.float32)
            inp[pfx + '_ln3_g'] = jnp.ones(C1, jnp.float32)
            inp[pfx + '_ln3_b'] = jnp.zeros(C1, jnp.float32)
            inp[pfx + '_li2_w'] = w((C1, C1 * W))
            inp[pfx + '_li2_b'] = jnp.zeros(C1 * W, jnp.float32)
            inp[pfx + '_li3_w'] = w((C1 * W, C1))
            inp[pfx + '_li3_b'] = jnp.zeros(C1, jnp.float32)
        inp['training'] = 0
        return inp
    _L0_xattn_all = _L0_xattn_setup()
    _L0_xattn_in = {k: v for k, v in _L0_xattn_all.items() if k in ('ln1_g', 'ln1_b', 'ln2_g', 'ln2_b', 'a1_wq', 'a1_wk', 'a1_wv', 'a1_li1_w', 'a1_li1_b', 'a1_lnx_g', 'a1_lnx_b', 'a1_lny_g', 'a1_lny_b', 'a1_ln3_g', 'a1_ln3_b', 'a1_li2_w', 'a1_li2_b', 'a1_li3_w', 'a1_li3_b', 'a2_wq', 'a2_wk', 'a2_wv', 'a2_li1_w', 'a2_li1_b', 'a2_lnx_g', 'a2_lnx_b', 'a2_lny_g', 'a2_lny_b', 'a2_ln3_g', 'a2_ln3_b', 'a2_li2_w', 'a2_li2_b', 'a2_li3_w', 'a2_li3_b')}
    del _L0_xattn_all

    def _L0_ffn_setup():
        import jax, jax.numpy as jnp
        import numpy as np
        D_MODEL = 128
        N_EXPERTS = 8
        TOP_K = 2
        FFN_HIDDEN = 4 * D_MODEL
        key = jax.random.key(seed)
        ks = jax.random.split(key, 6)

        def xavier(k, shape):
            fan_in, fan_out = (shape[-2], shape[-1])
            lim = jnp.sqrt(6.0 / (fan_in + fan_out))
            return jax.random.uniform(k, shape, jnp.float32, -lim, lim)
        x = jax.random.normal(ks[0], (4, 256, D_MODEL), jnp.float32)
        w_gate = xavier(ks[1], (N_EXPERTS, D_MODEL))
        W1 = xavier(ks[2], (N_EXPERTS, D_MODEL, FFN_HIDDEN))
        b1 = jnp.zeros((N_EXPERTS, FFN_HIDDEN), jnp.float32)
        W2 = xavier(ks[3], (N_EXPERTS, FFN_HIDDEN, D_MODEL))
        b2 = jnp.zeros((N_EXPERTS, D_MODEL), jnp.float32)
        return {'x': x, 'w_gate': w_gate, 'W1': W1, 'b1': b1, 'W2': W2, 'b2': b2}
    _L0_ffn_all = _L0_ffn_setup()
    _L0_ffn_in = {k: v for k, v in _L0_ffn_all.items() if k in ('w_gate', 'W1', 'b1', 'W2', 'b2')}
    del _L0_ffn_all

    def _L1_xattn_setup():
        import jax, jax.numpy as jnp
        import numpy as np
        HEADS = 16
        D_MODEL = 128
        IMG_MODEL = 64
        D_K = D_MODEL // HEADS
        key = jax.random.key(seed)
        ks = jax.random.split(key, 12)
        B, LQ, LKV = (8, 256, 128)
        s_dm = 1.0 / np.sqrt(D_MODEL)
        s_im = 1.0 / np.sqrt(IMG_MODEL)
        return {'q': jax.random.normal(ks[0], (B, LQ, D_MODEL), jnp.float32), 'k': jax.random.normal(ks[1], (B, LKV, IMG_MODEL), jnp.float32), 'v': jax.random.normal(ks[2], (B, LKV, IMG_MODEL), jnp.float32), 'Wq': jax.random.normal(ks[3], (D_MODEL, D_MODEL), jnp.float32) * s_dm, 'bq': jnp.zeros((D_MODEL,), jnp.float32), 'Wk': jax.random.normal(ks[4], (IMG_MODEL, D_MODEL), jnp.float32) * s_im, 'bk': jnp.zeros((D_MODEL,), jnp.float32), 'Wv': jax.random.normal(ks[5], (IMG_MODEL, D_MODEL), jnp.float32) * s_im, 'bv': jnp.zeros((D_MODEL,), jnp.float32), 'Wo': jax.random.normal(ks[6], (D_MODEL, D_MODEL), jnp.float32) * s_dm, 'bo': jnp.zeros((D_MODEL,), jnp.float32)}
    _L1_xattn_all = _L1_xattn_setup()
    _L1_xattn_in = {k: v for k, v in _L1_xattn_all.items() if k in ('Wq', 'bq', 'Wk', 'bk', 'Wv', 'bv', 'Wo', 'bo')}
    del _L1_xattn_all

    def _L1_ffn_setup():
        import jax, jax.numpy as jnp
        import numpy as np
        B, S, D, DOUT, E = (2, 256, 128, 128, 8)
        DH = 4 * D
        key = jax.random.key(seed)
        ks = jax.random.split(key, 7)
        sc = lambda *sh: 1.0 / np.sqrt(sh[-2]) if len(sh) >= 2 else 0.02
        return {'x': jax.random.normal(ks[0], (B, S, D), jnp.float32), 'Wg': jax.random.normal(ks[1], (D, E), jnp.float32) / np.sqrt(D), 'bg': jnp.zeros((E,), jnp.float32), 'W1': jax.random.normal(ks[2], (E, D, DH), jnp.float32) / np.sqrt(D), 'b1': jax.random.normal(ks[3], (E, DH), jnp.float32) * 0.02, 'W2': jax.random.normal(ks[4], (E, DH, DOUT), jnp.float32) / np.sqrt(DH), 'b2': jax.random.normal(ks[5], (E, DOUT), jnp.float32) * 0.02}
    _L1_ffn_all = _L1_ffn_setup()
    _L1_ffn_in = {k: v for k, v in _L1_ffn_all.items() if k in ('Wg', 'bg', 'W1', 'b1', 'W2', 'b2')}
    del _L1_ffn_all
    return {'x': x, 'ctx_512': ctx_512, 'L0_xattn_ln1_g': _L0_xattn_in['ln1_g'], 'L0_xattn_ln1_b': _L0_xattn_in['ln1_b'], 'L0_xattn_ln2_g': _L0_xattn_in['ln2_g'], 'L0_xattn_ln2_b': _L0_xattn_in['ln2_b'], 'L0_xattn_a1_wq': _L0_xattn_in['a1_wq'], 'L0_xattn_a1_wk': _L0_xattn_in['a1_wk'], 'L0_xattn_a1_wv': _L0_xattn_in['a1_wv'], 'L0_xattn_a1_li1_w': _L0_xattn_in['a1_li1_w'], 'L0_xattn_a1_li1_b': _L0_xattn_in['a1_li1_b'], 'L0_xattn_a1_lnx_g': _L0_xattn_in['a1_lnx_g'], 'L0_xattn_a1_lnx_b': _L0_xattn_in['a1_lnx_b'], 'L0_xattn_a1_lny_g': _L0_xattn_in['a1_lny_g'], 'L0_xattn_a1_lny_b': _L0_xattn_in['a1_lny_b'], 'L0_xattn_a1_ln3_g': _L0_xattn_in['a1_ln3_g'], 'L0_xattn_a1_ln3_b': _L0_xattn_in['a1_ln3_b'], 'L0_xattn_a1_li2_w': _L0_xattn_in['a1_li2_w'], 'L0_xattn_a1_li2_b': _L0_xattn_in['a1_li2_b'], 'L0_xattn_a1_li3_w': _L0_xattn_in['a1_li3_w'], 'L0_xattn_a1_li3_b': _L0_xattn_in['a1_li3_b'], 'L0_xattn_a2_wq': _L0_xattn_in['a2_wq'], 'L0_xattn_a2_wk': _L0_xattn_in['a2_wk'], 'L0_xattn_a2_wv': _L0_xattn_in['a2_wv'], 'L0_xattn_a2_li1_w': _L0_xattn_in['a2_li1_w'], 'L0_xattn_a2_li1_b': _L0_xattn_in['a2_li1_b'], 'L0_xattn_a2_lnx_g': _L0_xattn_in['a2_lnx_g'], 'L0_xattn_a2_lnx_b': _L0_xattn_in['a2_lnx_b'], 'L0_xattn_a2_lny_g': _L0_xattn_in['a2_lny_g'], 'L0_xattn_a2_lny_b': _L0_xattn_in['a2_lny_b'], 'L0_xattn_a2_ln3_g': _L0_xattn_in['a2_ln3_g'], 'L0_xattn_a2_ln3_b': _L0_xattn_in['a2_ln3_b'], 'L0_xattn_a2_li2_w': _L0_xattn_in['a2_li2_w'], 'L0_xattn_a2_li2_b': _L0_xattn_in['a2_li2_b'], 'L0_xattn_a2_li3_w': _L0_xattn_in['a2_li3_w'], 'L0_xattn_a2_li3_b': _L0_xattn_in['a2_li3_b'], 'L0_ffn_w_gate': _L0_ffn_in['w_gate'], 'L0_ffn_W1': _L0_ffn_in['W1'], 'L0_ffn_b1': _L0_ffn_in['b1'], 'L0_ffn_W2': _L0_ffn_in['W2'], 'L0_ffn_b2': _L0_ffn_in['b2'], 'L1_xattn_Wq': _L1_xattn_in['Wq'], 'L1_xattn_bq': _L1_xattn_in['bq'], 'L1_xattn_Wk': _L1_xattn_in['Wk'], 'L1_xattn_bk': _L1_xattn_in['bk'], 'L1_xattn_Wv': _L1_xattn_in['Wv'], 'L1_xattn_bv': _L1_xattn_in['bv'], 'L1_xattn_Wo': _L1_xattn_in['Wo'], 'L1_xattn_bo': _L1_xattn_in['bo'], 'L1_ffn_Wg': _L1_ffn_in['Wg'], 'L1_ffn_bg': _L1_ffn_in['bg'], 'L1_ffn_W1': _L1_ffn_in['W1'], 'L1_ffn_b1': _L1_ffn_in['b1'], 'L1_ffn_W2': _L1_ffn_in['W2'], 'L1_ffn_b2': _L1_ffn_in['b2']}

def reference(x, ctx_512, L0_xattn_ln1_g, L0_xattn_ln1_b, L0_xattn_ln2_g, L0_xattn_ln2_b, L0_xattn_a1_wq, L0_xattn_a1_wk, L0_xattn_a1_wv, L0_xattn_a1_li1_w, L0_xattn_a1_li1_b, L0_xattn_a1_lnx_g, L0_xattn_a1_lnx_b, L0_xattn_a1_lny_g, L0_xattn_a1_lny_b, L0_xattn_a1_ln3_g, L0_xattn_a1_ln3_b, L0_xattn_a1_li2_w, L0_xattn_a1_li2_b, L0_xattn_a1_li3_w, L0_xattn_a1_li3_b, L0_xattn_a2_wq, L0_xattn_a2_wk, L0_xattn_a2_wv, L0_xattn_a2_li1_w, L0_xattn_a2_li1_b, L0_xattn_a2_lnx_g, L0_xattn_a2_lnx_b, L0_xattn_a2_lny_g, L0_xattn_a2_lny_b, L0_xattn_a2_ln3_g, L0_xattn_a2_ln3_b, L0_xattn_a2_li2_w, L0_xattn_a2_li2_b, L0_xattn_a2_li3_w, L0_xattn_a2_li3_b, L0_ffn_w_gate, L0_ffn_W1, L0_ffn_b1, L0_ffn_W2, L0_ffn_b2, L1_xattn_Wq, L1_xattn_bq, L1_xattn_Wk, L1_xattn_bk, L1_xattn_Wv, L1_xattn_bv, L1_xattn_Wo, L1_xattn_bo, L1_ffn_Wg, L1_ffn_bg, L1_ffn_W1, L1_ffn_b1, L1_ffn_W2, L1_ffn_b2):
    import jax
    import jax.numpy as jnp

    def _L0_xattn_ref(xx, ee, ln1_g, ln1_b, ln2_g, ln2_b, a1_wq, a1_wk, a1_wv, a1_li1_w, a1_li1_b, a1_lnx_g, a1_lnx_b, a1_lny_g, a1_lny_b, a1_ln3_g, a1_ln3_b, a1_li2_w, a1_li2_b, a1_li3_w, a1_li3_b, a2_wq, a2_wk, a2_wv, a2_li1_w, a2_li1_b, a2_lnx_g, a2_lnx_b, a2_lny_g, a2_lny_b, a2_ln3_g, a2_ln3_b, a2_li2_w, a2_li2_b, a2_li3_w, a2_li3_b, training):
        import jax, jax.numpy as jnp
        import numpy as np
        H, D, C1, C2, S, M, B, W = (16, 32, 128, 64, 256, 64, 2, 4)

        def _ln(x, g, b):
            m = jnp.mean(x, -1, keepdims=True)
            v = jnp.var(x, -1, keepdims=True)
            return (x - m) * jax.lax.rsqrt(v + 1e-05) * g + b

        def _mha(x, y, wq, wk, wv, li1_w, li1_b, lnx_g, lnx_b, lny_g, lny_b, ln3_g, ln3_b, li2_w, li2_b, li3_w, li3_b, causal):
            xn = _ln(x, lnx_g, lnx_b)
            yn = _ln(y, lny_g, lny_b)
            q = jnp.einsum('bsc,hcd->bhsd', xn, wq)
            k = jnp.einsum('btc,hcd->bhtd', yn, wk)
            v = jnp.einsum('btc,hcd->bhtd', yn, wv)
            a = jax.nn.softmax(jnp.einsum('bhsd,bhtd->bhst', q, k) * D ** (-0.5), axis=-1)
            if causal:
                s, t = (a.shape[-2], a.shape[-1])
                mask = (jnp.arange(t)[None, :] > jnp.arange(s)[:, None]).astype(a.dtype)
                a = a * mask
            o = jnp.einsum('bhst,bhtd->bhsd', a, v)
            o = o.transpose(0, 2, 1, 3).reshape(x.shape[0], x.shape[1], H * D)
            x_out = x + o @ li1_w + li1_b
            h = jax.nn.gelu(_ln(x_out, ln3_g, ln3_b) @ li2_w + li2_b, approximate=False)
            return x_out + h @ li3_w + li3_b
        x = _ln(xx, ln1_g, ln1_b)
        x = x + _mha(x, x, a1_wq, a1_wk, a1_wv, a1_li1_w, a1_li1_b, a1_lnx_g, a1_lnx_b, a1_lny_g, a1_lny_b, a1_ln3_g, a1_ln3_b, a1_li2_w, a1_li2_b, a1_li3_w, a1_li3_b, causal=True)
        x = _ln(x, ln2_g, ln2_b)
        return x + _mha(x, ee, a2_wq, a2_wk, a2_wv, a2_li1_w, a2_li1_b, a2_lnx_g, a2_lnx_b, a2_lny_g, a2_lny_b, a2_ln3_g, a2_ln3_b, a2_li2_w, a2_li2_b, a2_li3_w, a2_li3_b, causal=False)

    def _L0_ffn_ref(x, w_gate, W1, b1, W2, b2):
        import jax, jax.numpy as jnp
        import numpy as np
        D_MODEL = 128
        N_EXPERTS = 8
        TOP_K = 2
        FFN_HIDDEN = 4 * D_MODEL
        B, S, D = x.shape
        flat_x = x.reshape(-1, D)
        gate = jax.nn.softmax(flat_x @ w_gate.T, axis=-1)
        topk_scores, topk_idx = jax.lax.top_k(gate, TOP_K)
        cw = (jax.nn.one_hot(topk_idx, N_EXPERTS, dtype=flat_x.dtype) * topk_scores[..., None]).sum(axis=1)
        h = jax.nn.gelu(jnp.einsum('td,edh->teh', flat_x, W1) + b1, approximate=False)
        y = jnp.einsum('teh,ehd->ted', h, W2) + b2
        out = jnp.einsum('ted,te->td', y, cw)
        return out.reshape(B, S, D)

    def _L1_xattn_ref(q, k, v, Wq, bq, Wk, bk, Wv, bv, Wo, bo):
        import jax, jax.numpy as jnp
        import numpy as np
        HEADS = 16
        D_MODEL = 128
        IMG_MODEL = 64
        D_K = D_MODEL // HEADS
        B, LQ, _ = q.shape
        LKV = k.shape[1]
        qh = (q @ Wq + bq).reshape(B, LQ, HEADS, D_K).transpose(0, 2, 1, 3)
        kh = (k @ Wk + bk).reshape(B, LKV, HEADS, D_K).transpose(0, 2, 1, 3)
        vh = (v @ Wv + bv).reshape(B, LKV, HEADS, D_K).transpose(0, 2, 1, 3)
        scale = 1.0 / np.sqrt(D_K)
        scores = jnp.einsum('bhqd,bhkd->bhqk', qh, kh) * scale
        attn = jax.nn.softmax(scores, axis=-1)
        out = jnp.einsum('bhqk,bhkd->bhqd', attn, vh)
        concat = out.transpose(0, 2, 1, 3).reshape(B, LQ, D_MODEL)
        return concat @ Wo + bo

    def _L1_ffn_ref(x, Wg, bg, W1, b1, W2, b2):
        import jax, jax.numpy as jnp
        import numpy as np
        B, S, D, DOUT, E = (2, 256, 128, 128, 8)
        DH = 4 * D
        Bb, Ss, Dd = x.shape
        xt = x.reshape(-1, Dd)
        gates = jax.nn.softmax(xt @ Wg + bg, axis=-1)
        sel = jnp.argmax(gates, axis=-1)
        nE = W1.shape[0]
        out = jnp.zeros((xt.shape[0], W2.shape[-1]), x.dtype)
        for e in range(nE):
            h = jax.nn.gelu(xt @ W1[e] + b1[e], approximate=False)
            ye = h @ W2[e] + b2[e]
            out = jnp.where((sel == e)[:, None], ye, out)
        return out.reshape(Bb, Ss, -1)
    x = x + _L0_xattn_ref(_layernorm(x, axis=-1), ctx_512, L0_xattn_ln1_g, L0_xattn_ln1_b, L0_xattn_ln2_g, L0_xattn_ln2_b, L0_xattn_a1_wq, L0_xattn_a1_wk, L0_xattn_a1_wv, L0_xattn_a1_li1_w, L0_xattn_a1_li1_b, L0_xattn_a1_lnx_g, L0_xattn_a1_lnx_b, L0_xattn_a1_lny_g, L0_xattn_a1_lny_b, L0_xattn_a1_ln3_g, L0_xattn_a1_ln3_b, L0_xattn_a1_li2_w, L0_xattn_a1_li2_b, L0_xattn_a1_li3_w, L0_xattn_a1_li3_b, L0_xattn_a2_wq, L0_xattn_a2_wk, L0_xattn_a2_wv, L0_xattn_a2_li1_w, L0_xattn_a2_li1_b, L0_xattn_a2_lnx_g, L0_xattn_a2_lnx_b, L0_xattn_a2_lny_g, L0_xattn_a2_lny_b, L0_xattn_a2_ln3_g, L0_xattn_a2_ln3_b, L0_xattn_a2_li2_w, L0_xattn_a2_li2_b, L0_xattn_a2_li3_w, L0_xattn_a2_li3_b, 0)
    x = x + _L0_ffn_ref(_layernorm(x, axis=-1), L0_ffn_w_gate, L0_ffn_W1, L0_ffn_b1, L0_ffn_W2, L0_ffn_b2)
    x = x + _L1_xattn_ref(_layernorm(x, axis=-1), ctx_512, ctx_512, L1_xattn_Wq, L1_xattn_bq, L1_xattn_Wk, L1_xattn_bk, L1_xattn_Wv, L1_xattn_bv, L1_xattn_Wo, L1_xattn_bo)
    x = x + _L1_ffn_ref(_layernorm(x, axis=-1), L1_ffn_Wg, L1_ffn_bg, L1_ffn_W1, L1_ffn_b1, L1_ffn_W2, L1_ffn_b2)
    return x

_drawn_inputs = setup_inputs


def setup_inputs(seed=0):
    import zlib

    import numpy as np

    out = dict(_drawn_inputs(seed))
    spreads = {'L0_xattn_ln1_g': (1.0, 0.2),
     'L0_xattn_ln1_b': (0.0, 0.1),
     'L0_xattn_ln2_g': (1.0, 0.2),
     'L0_xattn_ln2_b': (0.0, 0.1),
     'L0_xattn_a1_li1_b': (0.0, 0.1),
     'L0_xattn_a1_lnx_g': (1.0, 0.6),
     'L0_xattn_a1_lnx_b': (0.0, 0.8),
     'L0_xattn_a1_lny_g': (1.0, 0.6),
     'L0_xattn_a1_lny_b': (0.0, 0.553),
     'L0_xattn_a1_ln3_g': (1.0, 0.6),
     'L0_xattn_a1_ln3_b': (0.0, 2.0),
     'L0_xattn_a1_li2_b': (0.0, 0.364),
     'L0_xattn_a1_li3_b': (0.0, 0.1),
     'L0_xattn_a2_li1_b': (0.0, 0.1),
     'L0_xattn_a2_lnx_g': (1.0, 0.6),
     'L0_xattn_a2_lnx_b': (0.0, 0.8),
     'L0_xattn_a2_lny_g': (1.0, 0.6),
     'L0_xattn_a2_lny_b': (0.0, 1.383),
     'L0_xattn_a2_ln3_g': (1.0, 0.6),
     'L0_xattn_a2_ln3_b': (0.0, 1.797),
     'L0_xattn_a2_li2_b': (0.0, 0.361),
     'L0_xattn_a2_li3_b': (0.0, 0.1),
     'L0_ffn_b1': (0.0, 0.1),
     'L0_ffn_b2': (0.0, 0.1),
     'L1_xattn_bq': (0.0, 0.393),
     'L1_xattn_bk': (0.0, 2.0),
     'L1_xattn_bv': (0.0, 0.1),
     'L1_xattn_bo': (0.0, 0.1),
     'L1_ffn_bg': (0.0, 0.1)}
    factors = {'L0_xattn_a1_wq': 8.0,
     'L0_xattn_a1_wk': 8.0,
     'L0_xattn_a1_wv': 5.136,
     'L0_xattn_a1_li1_w': 7.372,
     'L0_xattn_a2_wq': 8.0,
     'L0_xattn_a2_wk': 8.0,
     'L1_ffn_b1': 8.0,
     'L1_ffn_b2': 8.0}
    for name, (base, spread) in spreads.items():
        noise = np.random.default_rng([zlib.crc32(name.encode()), seed]).standard_normal(out[name].shape)
        drawn = base * np.exp(spread * noise) if base else spread * noise
        out[name] = jnp.asarray(drawn.astype(out[name].dtype))
    for name, factor in factors.items():
        out[name] = (out[name] * factor).astype(out[name].dtype)
    return out
```

```python
from contextlib import ExitStack

import concourse.bass as bass
from concourse import mybir

F32 = mybir.dt.float32
F32R = mybir.dt.float32r
ALU = mybir.AluOpType
ACT = mybir.ActivationFunctionType
AX = mybir.AxisListType

NB, SQ, CH = 16, 56, 128
NTOK = NB * SQ
TP = 112
NT = NTOK // TP
CTX_C = 64
NE, HID = 8, 512
NF = HID // 128
EPS = 1e-5


class Kit:

    def __init__(self, nc, ctx):
        self.nc, self.ctx = nc, ctx
        self.shared_sems, self.chains = {}, {}

    def sb(self, name, shape, dt=F32):
        return self.ctx.enter_context(self.nc.sbuf_tensor(name, shape, dt))

    def sem(self, name):
        return self.ctx.enter_context(self.nc.semaphore(name))

    def shared(self, name, adds):
        if name not in self.shared_sems:
            self.shared_sems[name] = [self.sem(name), 0]
        sem, base = self.shared_sems[name]
        self.shared_sems[name][1] += adds
        return sem, base

    def chain(self, eng, name):
        if name not in self.chains:
            self.chains[name] = [self.sem(name), 0]
        return Chain(eng, *self.chains[name], self.chains[name])


class Chain:

    def __init__(self, eng, sem, n=0, record=None):
        self.eng, self.sem, self.n, self.record = eng, sem, n, record

    def then(self, ins):
        self.n += 1
        if self.record is not None:
            self.record[1] = self.n
        ins.then_inc(self.sem, 1)
        self.eng.wait_ge(self.sem, self.n)


def row_tiles(x):
    return x.rearrange("(n p) c -> p n c", p=TP)


def over_tiles(v, n=NT):
    return v.unsqueeze(1).broadcast_to([v.shape[0], n, v.shape[1]])


def layer_norm(nc, K, name, X, XA, outs=(), affine=None, prefetch=None):
    stats, mv, rstd = K.ln_stats, K.ln_mv, K.ln_rstd
    var_ready, var0 = K.shared("ln_var", 1)
    rstd_ready, rstd0 = K.shared("ln_rstd", 1)
    xa_ready, xa0 = K.shared("ln_xa", 2)
    xt_ready, xt0 = K.shared("ln_xt", 2 * len(outs))
    with nc.Block() as block:
        if prefetch is not None:
            @block.sync
            def _(sp):
                prefetch(sp)

        @block.vector
        def _(dve):
            o = K.chain(dve, "ln_chain")
            for n in range(NT):
                last = nc.vector.bn_stats(stats[0:TP, n, :], X[0:TP, n, :])
            o.then(last)
            for n in range(NT):
                last = nc.vector.bn_aggr(mv[0:TP, n, :], stats[0:TP, n, :])
            o.then(last)
            nc.vector.tensor_scalar(rstd[0:TP, 0, :], mv[0:TP, :, 1], EPS, None, ALU.add).then_inc(var_ready, 1)
            dve.wait_ge(rstd_ready, rstd0 + 1)
            for n in range(NT):
                last = nc.vector.tensor_scalar(XA[0:TP, n, :], X[0:TP, n, :], mv[0:TP, n, 0:1],
                                               rstd[0:TP, 1, n:n + 1], ALU.subtract, ALU.mult)
                if n % 4 == 3:
                    last.then_inc(xa_ready, 1)
            if affine is not None:
                dst, gain, bias = affine
                dve.wait_ge(xa_ready, xa0 + 2)
                o.then(nc.vector.tensor_tensor(dst[0:TP, :, :], XA[0:TP, :, :], over_tiles(gain), ALU.mult))
                o.then(nc.vector.tensor_tensor(dst[0:TP, :, :], dst[0:TP, :, :], over_tiles(bias), ALU.add))
            for half in range(2 if outs else 0):
                dve.wait_ge(xt_ready, xt0 + half + 1)
                dst, gain, bias = outs[0]
                cols = slice(448 * half, 448 * half + 448)
                if gain is None:
                    nc.vector.tensor_copy(dst[:, cols], K.ps[:, half, 0:448])
                else:
                    nc.vector.tensor_scalar(dst[:, cols], K.ps[:, half, 0:448], gain, bias, ALU.mult, ALU.add)

        @block.gpsimd
        def _(pool):
            pool.wait_ge(var_ready, var0 + 1)
            nc.gpsimd.tensor_tensor(rstd[0:TP, 1, :], rstd[0:TP, 0, :], K.mhalf12[0:TP, 0:NT],
                                    ALU.pow).then_inc(rstd_ready, 1)

        if outs:
            @block.tensor
            def _(pe):
                for n in range(NT):
                    if n % 4 == 0:
                        pe.wait_ge(xa_ready, xa0 + n // 4 + 1)
                    last = nc.tensor.transpose(K.ps[:, n // 4, TP * (n % 4):TP * (n % 4) + TP],
                                               XA[0:TP, n, :], K.ident[0:TP, 0:TP])
                    if n % 4 == 3:
                        last.then_inc(xt_ready, 1)
                for n in range(NT if len(outs) > 1 else 0):
                    last = nc.tensor.transpose(K.ps[:, 2 + n // 4, TP * (n % 4):TP * (n % 4) + TP],
                                               XA[0:TP, n, :], K.ident[0:TP, 0:TP])
                    if n % 4 == 3:
                        last.then_inc(xt_ready, 1)

            @block.scalar
            def _(act):
                for dst, gain, bias in outs[1:]:
                    for half in range(2):
                        act.wait_ge(xt_ready, xt0 + 3 + half)
                        nc.scalar.activation(dst[:, 448 * half:448 * half + 448], K.ps[:, 2 + half, 0:448],
                                             ACT.Identity, scale=gain, bias=bias)


def fold_query_weights(nc, K, name, WQ, WK, nchunk, mask, M, WQT, WKM, bq=None, qbias=None):
    nh = 16 // nchunk
    wt_ready, wkm_ready = K.sem(f"{name}_wt"), K.sem(f"{name}_wkm")
    m_ready, m_copied, qb_ready = K.sem(f"{name}_m"), K.sem(f"{name}_mc"), K.sem(f"{name}_qb")
    with nc.Block() as block:
        @block.tensor
        def _(pe):
            for c in range(nchunk):
                if c:
                    pe.wait_ge(wkm_ready, c)
                nc.tensor.transpose(K.ps[:, 0, 0:128], WQ[:, 128 * c:128 * c + 128], K.ident[:, :])
                nc.tensor.transpose(K.ps[:, 0, 128:192], WK[0:64, 128 * c:128 * c + 128],
                                    K.ident[0:64, 0:64]).then_inc(wt_ready, 1)
                pe.wait_ge(wkm_ready, c + 1)
                if c:
                    pe.wait_ge(m_copied, c)
                for b in range(max(1, nh * 64 // 512)):
                    w = min(512, nh * 64)
                    last = nc.tensor.matmul(K.ps[:, 1 + b, 0:w], WQT[:, :],
                                            WKM[:, :, :].rearrange("p h c -> p (h c)")[:, w * b:w * b + w],
                                            start=True, stop=True)
                last.then_inc(m_ready, 1)
            if bq is not None:
                for h in range(16):
                    for half in range(2):
                        last = nc.tensor.matmul(K.ps[64 * half:64 * half + 64, 3, h:h + 1], WKM[:, h, :],
                                                bq, start=True, stop=True, skip_group_check=True)
                last.then_inc(qb_ready, 1)

        @block.vector
        def _(dve):
            o = K.chain(dve, "fold_chain")
            for c in range(nchunk):
                dve.wait_ge(wt_ready, c + 1)
                if c:
                    dve.wait_ge(m_ready, c)
                nc.vector.tensor_copy(WQT[:, :], K.ps[:, 0, 0:128])
                o.then(nc.vector.tensor_copy(K.wkt[:, :], K.ps[:, 0, 128:192]))
                nc.vector.tensor_tensor(WKM[:, :, :], over_tiles(K.wkt[:, :], nh),
                                        mask.unsqueeze(2).broadcast_to([128, nh, 64]),
                                        ALU.mult).then_inc(wkm_ready, 1)
                dve.wait_ge(wkm_ready, c + 1)
                dve.wait_ge(m_ready, c + 1)
                for b in range(max(1, nh * 64 // 512)):
                    w = min(512, nh * 64)
                    k = w // 64
                    for half in range(2):
                        last = nc.vector.tensor_copy(
                            M[:, nh * c + k * b:nh * c + k * b + k, 64 * half:64 * half + 64],
                            K.ps[:, 1 + b, 0:w].rearrange("p (h c) -> p h c", h=k))
                last.then_inc(m_copied, 1)
            if bq is not None:
                dve.wait_ge(qb_ready, 1)
                nc.vector.tensor_copy(qbias[:, :], K.ps[:, 3, 0:16])


def self_attention(nc, K, xT, yT, qT, kT, WQ, WK, WV, oT, bufs, scale):
    QS, KS, YS, VS, E, AT, MX, SM = bufs
    H, D = 16, 32
    proj_done, proj_copied = K.sem("sa_proj"), K.sem("sa_projc")
    with nc.Block() as block:
        @block.tensor
        def _(pe):
            k = 0
            for W, src in ((WQ, xT), (WK, yT)):
                for c in range(4):
                    for half in range(2):
                        if k >= 8:
                            pe.wait_ge(proj_copied, k - 7)
                        nc.tensor.matmul(K.ps[:, k % 8, 0:448], W[:, 128 * c:128 * c + 128],
                                         src[:, 448 * half:448 * half + 448],
                                         start=True, stop=True).then_inc(proj_done, 1)
                        k += 1

        @block.scalar
        def _(act):
            for k in range(16):
                dst, c, half = (qT, kT)[k // 8], k % 8 // 2, k % 2
                act.wait_ge(proj_done, k + 1)
                nc.scalar.copy(dst[:, c, 448 * half:448 * half + 448], K.ps[:, k % 8, 0:448]
                               ).then_inc(proj_copied, 1)

    q_sliced, y_sliced = K.sem("sa_qs"), K.sem("sa_ys")
    v_done, v_copied = K.sem("sa_v"), K.sem("sa_vc")
    sc_done = K.sem("sa_sc")
    mx_done, sub_done = K.sem("sa_mx"), K.sem("sa_sub")
    ex_done, sum_done, rec_done, mask_done, norm_done = (
        K.sem("sa_ex"), K.sem("sa_sum"), K.sem("sa_rec"), K.sem("sa_mask"), K.sem("sa_norm"))
    tr_done, tr_copied = K.sem("sa_tr"), K.sem("sa_trc")
    o_done, o_copied = K.sem("sa_o"), K.sem("sa_oc")

    def wait_from_second(eng, sem, p, value):
        if not isinstance(p, int) or value > 0:
            eng.wait_ge(sem, value)

    def pairs(eng, emit):
        emit(0, False, True)
        emit(1, True, True)
        with eng.Fori(2, NT) as p:
            emit(p, True, True)
        emit(NT, True, False)

    with nc.Block() as block:
        @block.gpsimd
        def _(pool):
            def emit(p, lag, cur):
                if cur:
                    pool.wait_ge(sum_done, p + 1)
                    nc.gpsimd.tensor_tensor(E[0:120, :, :], E[0:120, :, :], over_tiles(K.mask[0:120, :], H),
                                            ALU.mult).then_inc(mask_done, 1)
                    pool.wait_ge(mask_done, p + 1)
            pairs(pool, emit)

        @block.tensor
        def _(pe):
            def emit(p, lag, cur):
                if cur:
                    pe.wait_ge(q_sliced, p + 1)
                    if lag:
                        pe.wait_ge(sub_done, p)
                    for h in range(H):
                        j, c = h % 4, h // 4
                        for u in range(2):
                            last = nc.tensor.matmul(
                                K.ps[64 * u:64 * u + 64, j, SQ * c:SQ * c + SQ],
                                QS[32 * j:32 * j + 32, c, 64 * u:64 * u + 64],
                                KS[32 * j:32 * j + 32, c, SQ * u:SQ * u + SQ],
                                start=True, stop=True, skip_group_check=True)
                    last.then_inc(sc_done, 1)
                if lag:
                    pe.wait_ge(y_sliced, p)
                    for u in range(2):
                        wait_from_second(pe, v_copied, p, 2 * p - 2 + u)
                        nc.tensor.matmul(K.ps[0:SQ, 6, 0:512], YS[:, SQ * u:SQ * u + SQ], WV[:, :],
                                         start=True, stop=True).then_inc(v_done, 1)
                    for b in range(2):
                        pe.wait_ge(proj_copied, 16)
                        pe.wait_ge(norm_done, p)
                        wait_from_second(pe, tr_copied, p, 2 * p - 2 + b)
                        for h in range(8 * b, 8 * b + 8):
                            last = nc.tensor.transpose(
                                K.ps[0:SQ, 4 + h // 4 % 2, 120 * (h % 4):120 * (h % 4) + 120],
                                E[0:120, h, :], K.ident[0:120, 0:120])
                        last.then_inc(tr_done, 1)
                    for u in range(2):
                        pe.wait_ge(proj_copied, 16)
                        pe.wait_ge(tr_copied, 2 * p)
                        pe.wait_ge(v_copied, 2 * p)
                        wait_from_second(pe, o_copied, p, 2 * p - 2 + u)
                        for h in range(H):
                            j, c = h % 4, h // 4
                            last = nc.tensor.matmul(K.ps[32 * j:32 * j + 32, 7, SQ * c:SQ * c + SQ],
                                                    VS[0:SQ, u, 32 * h:32 * h + 32],
                                                    AT[0:SQ, h, 64 * u:64 * u + SQ],
                                                    start=True, stop=True, skip_group_check=True)
                        last.then_inc(o_done, 1)
            pairs(pe, emit)

        @block.vector
        def _(dve):
            def emit(p, lag, cur):
                if cur:
                    if lag:
                        dve.wait_ge(sc_done, p)
                    for u in range(2):
                        nc.vector.tensor_copy(QS[:, :, 64 * u:64 * u + 64],
                                              qT[:, :, bass.ds(TP * p + SQ * u, 64)])
                    nc.vector.tensor_copy(KS[:, :, :], kT[:, :, bass.ds(TP * p, TP)]).then_inc(q_sliced, 1)
                if lag:
                    wait_from_second(dve, v_done, p, 2 * p - 2)
                    nc.vector.tensor_copy(YS[:, :], yT[:, bass.ds(TP * (p - 1), TP)]).then_inc(y_sliced, 1)
                if not cur:
                    return
                dve.wait_ge(sc_done, p + 1)
                sc = K.ps[0:120, 0:4, 0:4 * SQ].rearrange("p j (c t) -> p j c t", c=4)
                mx = MX[0:120, :].rearrange("p (j c) -> p j c", j=4)
                nc.vector.tensor_reduce(mx, sc, axis=AX.X, op=ALU.max).then_inc(mx_done, 1)
                dve.wait_ge(mx_done, p + 1)
                if lag:
                    dve.wait_ge(tr_done, 2 * p)
                last = nc.vector.tensor_tensor(E[0:120, :, :].rearrange("p (c j) t -> p j c t", j=4), sc,
                                               mx.unsqueeze(3).broadcast_to([120, 4, 4, SQ]), ALU.subtract)
                last.then_inc(sub_done, 1)
                dve.wait_ge(ex_done, p + 1)
                nc.vector.tensor_reduce(SM[0:120, :], E[0:120, :, :], axis=AX.X, op=ALU.add).then_inc(sum_done, 1)
                dve.wait_ge(sum_done, p + 1)
                nc.vector.reciprocal(SM[0:120, :], SM[0:120, :]).then_inc(rec_done, 1)
                dve.wait_ge(rec_done, p + 1)
                dve.wait_ge(mask_done, p + 1)
                nc.vector.tensor_tensor(E[0:120, :, :], E[0:120, :, :],
                                        SM[0:120, :].unsqueeze(2).broadcast_to([120, H, SQ]),
                                        ALU.mult).then_inc(norm_done, 1)
            pairs(dve, emit)

        @block.scalar
        def _(act):
            def emit(p, lag, cur):
                if lag:
                    wait_from_second(act, o_done, p, 2 * p - 2)
                    for u in range(2):
                        act.wait_ge(v_done, 2 * p - 1 + u)
                        nc.scalar.copy(VS[0:SQ, u, :], K.ps[0:SQ, 6, 0:512]).then_inc(v_copied, 1)
                    for b in range(2):
                        act.wait_ge(tr_done, 2 * p - 1 + b)
                        for bb in range(2):
                            h = 8 * b + 4 * bb
                            last = nc.scalar.copy(AT[0:SQ, h:h + 4, :],
                                                  K.ps[0:SQ, 4 + bb, 0:480].rearrange("p (h s) -> p h s", h=4))
                        last.then_inc(tr_copied, 1)
                if cur:
                    act.wait_ge(sub_done, p + 1)
                    nc.scalar.activation(E[0:120, :, :], E[0:120, :, :], ACT.Exp, scale=scale).then_inc(ex_done, 1)
                if lag:
                    for u in range(2):
                        act.wait_ge(o_done, 2 * p - 1 + u)
                        nc.scalar.copy(oT[:, :, bass.ds(TP * (p - 1) + SQ * u, SQ)],
                                       K.ps[:, 7, 0:4 * SQ].rearrange("p (c s) -> p c s", c=4)).then_inc(o_copied, 1)
            pairs(act, emit)


def normalise_attention(nc, K, name, Zall, oT, sel, vbias, zt, rzt, prefetch=None):
    nchunk = oT.shape[1]
    rec_done, zt_done, zt_copied = K.sem(f"{name}_rec"), K.sem(f"{name}_zt"), K.sem(f"{name}_ztc")
    z_stored, z_loaded = K.sem(f"{name}_zst"), K.sem(f"{name}_zld")
    bc_done, bc_used = K.sem(f"{name}_bc"), K.sem(f"{name}_bcu")
    with nc.Block() as block:
        @block.sync
        def _(sp):
            if prefetch is not None:
                prefetch(sp)

        @block.scalar
        def _(act):
            act.wait_ge(zt_copied, 1)
            act.dma_start(K.z_dram, zt[0:112, :]).then_inc(z_stored, 16)
            act.wait_ge(z_stored, 16)
            act.dma_start(rzt[0:16, :, :], K.z_dram.rearrange("k p -> (k p)").rearrange(
                "(b h s) -> h b s", b=NB, h=16)).then_inc(z_loaded, 16)
            act.wait_ge(z_loaded, 16)

        @block.tensor
        def _(pe):
            pe.wait_ge(rec_done, 1)
            nc.tensor.transpose(K.ps[0:112, 0, 0:128], Zall[:, :], K.ident[:, :]).then_inc(zt_done, 1)
            pe.wait_ge(z_loaded, 16)
            for k in range(2 * nchunk):
                c, half = k // 2, k % 2
                if k >= 2:
                    pe.wait_ge(bc_used, k - 1)
                nc.tensor.matmul(K.ps[:, 1 + k % 2, 0:448], sel[0:16, c, :],
                                 rzt[0:16, 8 * half:8 * half + 8, :].rearrange("h b s -> h (b s)"),
                                 start=True, stop=True).then_inc(bc_done, 1)

        @block.vector
        def _(dve):
            nc.vector.reciprocal(Zall[:, :], Zall[:, :]).then_inc(rec_done, 1)
            dve.wait_ge(zt_done, 1)
            nc.vector.tensor_copy(zt[0:112, :], K.ps[0:112, 0, 0:128]).then_inc(zt_copied, 1)
            for k in range(2 * nchunk):
                c, half = k // 2, k % 2
                cols = slice(448 * half, 448 * half + 448)
                dve.wait_ge(bc_done, k + 1)
                nc.vector.tensor_tensor(oT[:, c, cols], oT[:, c, cols], K.ps[:, 1 + k % 2, 0:448],
                                        ALU.mult).then_inc(bc_used, 1)
                if vbias is not None:
                    dve.wait_ge(bc_used, k + 1)
                    nc.vector.tensor_scalar(oT[:, c, cols], oT[:, c, cols], vbias, None, ALU.add)


def project_and_add(nc, K, name, dst, terms, bias, srcT, W):
    nchunk = srcT.shape[1]
    base_done, base0 = K.shared("proj_base", len(terms))
    mm_done, mm0 = K.shared("proj_mm", 2)
    with nc.Block() as block:
        @block.gpsimd
        def _(pool):
            o = Chain(pool, base_done, base0)
            o.then(nc.gpsimd.tensor_tensor(dst[0:TP, :, :], terms[0][0:TP, :, :], over_tiles(bias), ALU.add))
            for t in terms[1:]:
                o.then(nc.gpsimd.tensor_tensor(dst[0:TP, :, :], dst[0:TP, :, :], t[0:TP, :, :], ALU.add))

        @block.tensor
        def _(pe):
            for n in range(NT):
                for c in range(nchunk):
                    last = nc.tensor.matmul(K.ps[0:TP, n // 4, 128 * (n % 4):128 * (n % 4) + 128],
                                            srcT[:, c, TP * n:TP * n + TP], W[:, c, :],
                                            start=c == 0, stop=c == nchunk - 1, skip_group_check=True)
                if n % 4 == 3:
                    last.then_inc(mm_done, 1)

        @block.vector
        def _(dve):
            dve.wait_ge(base_done, base0 + len(terms))
            for half in range(2):
                dve.wait_ge(mm_done, mm0 + half + 1)
                nc.vector.tensor_tensor(dst[0:TP, 4 * half:4 * half + 4, :], dst[0:TP, 4 * half:4 * half + 4, :],
                                        K.ps[0:TP, half, :].rearrange("p (n c) -> p n c", n=4), ALU.add)


def hidden_layer(nc, K, name, xT, W, bias, hT):
    h_done, h0 = K.shared("hidden_h", 2 * NF)
    with nc.Block() as block:
        @block.tensor
        def _(pe):
            for k in range(2 * NF):
                f, half = k % NF, k // NF
                nc.tensor.matmul(K.ps[:, k, 0:448], W[:, 128 * f:128 * f + 128],
                                 xT[:, 448 * half:448 * half + 448], start=True, stop=True).then_inc(h_done, 1)

        @block.scalar
        def _(act):
            for k in range(2 * NF):
                f, half = k % NF, k // NF
                act.wait_ge(h_done, h0 + k + 1)
                nc.scalar.activation(hT[:, f, 448 * half:448 * half + 448], K.ps[:, k, 0:448], ACT.Gelu,
                                     bias=bias[:, f:f + 1])


def expert_loader(nc, K, W1_dram, W2_dram, Wb1, Wb2, w_loaded):
    def load(sp, e, u):
        sp.dma_start(Wb1[:, u, :], W1_dram[bass.ds(e, 1), :, :].rearrange("e c h -> (e c) h")
                     ).then_inc(w_loaded[u], 16)
        sp.dma_start(Wb2[:, u, :, :], W2_dram[bass.ds(e, 1), :, :].rearrange("e (f p) d -> (e p) f d", p=128)
                     ).then_inc(w_loaded[u], 16)
    return load


def mixture(nc, K, name, X, xT, gate_w, gate_b, top, b1c, b2, load, Wb1, Wb2, w_loaded, hT, bufs):
    G, G2, EQ, SMALL, CW, CWT = bufs
    lg_done, k0 = K.shared("gate_lg", 1)
    sub_done, _ = K.shared("gate_sub", 1)
    ex_done, _ = K.shared("gate_ex", 1)
    cw_done, _ = K.shared("gate_cw", 1)
    cwt_done, _ = K.shared("gate_cwt", 1)
    cwt_copied, _ = K.shared("gate_cwtc", 1)
    b2_done, _ = K.shared("gate_b2", 1)
    with nc.Block() as block:
        @block.tensor
        def _(pe):
            for n in range(NT):
                last = nc.tensor.matmul(K.ps[0:TP, 0, NE * n:NE * n + NE], xT[:, TP * n:TP * n + TP], gate_w,
                                        start=True, stop=True, skip_group_check=True)
            last.then_inc(lg_done, 1)
            pe.wait_ge(cw_done, k0 + 1)
            for n in range(NT):
                last = nc.tensor.transpose(K.ps[0:NE, 1 + n // 4, TP * (n % 4):TP * (n % 4) + TP],
                                           CW[0:TP, n, :], K.ident[0:TP, 0:TP])
            last.then_inc(cwt_done, 1)
            pe.wait_ge(cwt_copied, k0 + 1)
            for n in range(NT):
                last = nc.tensor.matmul(K.ps[0:TP, 3 + n // 4, 128 * (n % 4):128 * (n % 4) + 128],
                                        CWT[0:NE, TP * n:TP * n + TP], b2, start=True, stop=True,
                                        skip_group_check=True)
            last.then_inc(b2_done, 1)

        @block.scalar
        def _(act):
            act.wait_ge(sub_done, k0 + 1)
            nc.scalar.activation(G[0:TP, :, :], G[0:TP, :, :], ACT.Exp).then_inc(ex_done, 1)

        @block.vector
        def _(dve):
            o = K.chain(dve, "gate_chain")
            g, g2, eq, cw = (t[0:TP, :, :] for t in (G, G2, EQ, CW))

            def bc(col):
                return SMALL[0:TP, col, :].unsqueeze(2).broadcast_to([TP, NT, NE])

            def first_largest(src, dst, col):
                o.then(nc.vector.tensor_reduce(SMALL[0:TP, col, :], src, axis=AX.X, op=ALU.max))
                o.then(nc.vector.tensor_tensor(dst, src, bc(col), ALU.is_ge))
                o.then(nc.vector.tensor_tensor(dst, dst, K.expert_m8[0:TP, :, :], ALU.mult))
                o.then(nc.vector.tensor_reduce(SMALL[0:TP, col, :], dst, axis=AX.X, op=ALU.min))
                o.then(nc.vector.tensor_tensor(dst, K.expert_m8[0:TP, :, :], bc(col), ALU.is_equal))

            dve.wait_ge(lg_done, k0 + 1)
            lg = K.ps[0:TP, 0, 0:NT * NE].rearrange("p (n e) -> p n e", e=NE)
            if gate_b is None:
                o.then(nc.vector.tensor_copy(g, lg))
            else:
                o.then(nc.vector.tensor_tensor(g, lg, over_tiles(gate_b), ALU.add))
            o.then(nc.vector.tensor_reduce(SMALL[0:TP, 0, :], g, axis=AX.X, op=ALU.max))
            nc.vector.tensor_tensor(g, g, bc(0), ALU.subtract).then_inc(sub_done, 1)
            dve.wait_ge(ex_done, k0 + 1)
            o.then(nc.vector.tensor_reduce(SMALL[0:TP, 1, :], g, axis=AX.X, op=ALU.add))
            o.then(nc.vector.reciprocal(SMALL[0:TP, 1, :], SMALL[0:TP, 1, :]))
            o.then(nc.vector.tensor_tensor(g, g, bc(1), ALU.mult))
            first_largest(g, eq, 2)
            if top == 1:
                nc.vector.tensor_copy(cw, eq).then_inc(cw_done, 1)
            else:
                o.then(nc.vector.scalar_tensor_tensor(g2, eq, -2.0, g, ALU.mult, ALU.add))
                first_largest(g2, cw, 3)
                o.then(nc.vector.tensor_tensor(cw, cw, eq, ALU.add))
                nc.vector.tensor_tensor(cw, cw, g, ALU.mult).then_inc(cw_done, 1)
            dve.wait_ge(cwt_done, k0 + 1)
            for half in range(2):
                last = nc.vector.tensor_copy(CWT[0:NE, 448 * half:448 * half + 448], K.ps[0:NE, 1 + half, 0:448])
            last.then_inc(cwt_copied, 1)
            dve.wait_ge(b2_done, k0 + 1)
            for half in range(2):
                nc.vector.tensor_tensor(X[0:TP, 4 * half:4 * half + 4, :], X[0:TP, 4 * half:4 * half + 4, :],
                                        K.ps[0:TP, 3 + half, :].rearrange("p (n c) -> p n c", n=4), ALU.add)

    h_done, g_done = K.sem(f"{name}_h"), K.sem(f"{name}_g")
    out_done, acc_done = K.sem(f"{name}_out"), K.sem(f"{name}_acc")
    col_done = K.sem(f"{name}_col")
    B1S, CWS = K.b1s, K.cws
    UNITS = 4

    with nc.Block() as block:
        @block.sync
        def _(sp):
            with sp.Fori(0, NE // 2 - 1) as t:
                for u in range(2):
                    sp.wait_ge(out_done, 4 * t + 2 * u + 2)
                    load(sp, 2 * t + 2 + u, u)

        @block.tensor
        def _(pe):
            def hidden(t, v):
                u, half = divmod(v, 2)
                if half == 0:
                    pe.wait_ge(w_loaded[u], 32 * t + 32)
                for f in range(NF):
                    if not (isinstance(t, int) and v == 0):
                        pe.wait_ge(g_done, 16 * t + 4 * v + f - 3)
                    nc.tensor.matmul(K.ps[:, f, 0:448], Wb1[:, u, 128 * f:128 * f + 128],
                                     xT[:, 448 * half:448 * half + 448], start=True, stop=True
                                     ).then_inc(h_done, 1)

            def output(t, v):
                u, half = divmod(v, 2)
                pe.wait_ge(g_done, 16 * t + 4 * v + 4)
                if not (isinstance(t, int) and v < 2):
                    pe.wait_ge(acc_done, 4 * t + v - 1)
                for i in range(4):
                    for f in range(NF):
                        last = nc.tensor.matmul(K.ps[0:TP, 4 + v % 2, 128 * i:128 * i + 128],
                                                hT[:, v % 2, f, TP * i:TP * i + TP], Wb2[:, u, f, :],
                                                start=f == 0, stop=f == NF - 1, skip_group_check=True)
                last.then_inc(out_done, 1)

            def turn(t):
                hidden(t, 0)
                for v in range(1, UNITS):
                    hidden(t, v)
                    output(t, v - 1)
                output(t, UNITS - 1)
            turn(0)
            with pe.Fori(1, NE // 2) as t:
                turn(t)

        @block.scalar
        def _(act):
            def turn(t):
                for v in range(UNITS):
                    u = v // 2
                    if v % 2 == 0:
                        act.wait_ge(col_done, 4 * t + 2 * u + 2)
                    if not (isinstance(t, int) and v < 2):
                        act.wait_ge(out_done, 4 * t + v - 1)
                    for f in range(NF):
                        act.wait_ge(h_done, 16 * t + 4 * v + f + 1)
                        nc.scalar.activation(hT[:, v % 2, f, :], K.ps[:, f, 0:448], ACT.Gelu,
                                             bias=B1S[:, u, f:f + 1]).then_inc(g_done, 1)
            turn(0)
            with act.Fori(1, NE // 2) as t:
                turn(t)

        @block.vector
        def _(dve):
            def columns(t, u):
                if not isinstance(t, int):
                    dve.wait_ge(g_done, 16 * t + 8 * u - 8)
                nc.vector.tensor_copy(B1S[:, u, :], b1c[:, bass.ds(8 * t + 4 * u, 4)]).then_inc(col_done, 1)
                nc.vector.tensor_copy(CWS[0:TP, u, :], CW[0:TP, :, bass.ds(2 * t + u, 1)].rearrange(
                    "p n e -> p (n e)")).then_inc(col_done, 1)

            def turn(t):
                columns(t, 0)
                for v in range(UNITS):
                    u, half = divmod(v, 2)
                    if v == 1:
                        columns(t, 1)
                    dve.wait_ge(out_done, 4 * t + v + 1)
                    if v % 2 == 0:
                        dve.wait_ge(col_done, 4 * t + 2 * u + 2)
                    if not (isinstance(t, int) and v < 2):
                        dve.wait_ge(acc_done, 4 * t + v - 1)
                    for i in range(4):
                        n = 4 * half + i
                        last = nc.vector.scalar_tensor_tensor(
                            X[0:TP, n, :], K.ps[0:TP, 4 + v % 2, 128 * i:128 * i + 128],
                            CWS[0:TP, u, n:n + 1], X[0:TP, n, :], ALU.mult, ALU.add)
                    last.then_inc(acc_done, 1)
            turn(0)
            with dve.Fori(1, NE // 2) as t:
                turn(t)
BLOCKS = 7
STEPS = 2 * BLOCKS
GROUPS = 3
GT = 4
TT = 125
NTT = 12
GC = GT * TT
HALF = 448
BANK_V = 7
Q_STEPS = (4, 5, 7, 11)
O_STEP = 6


def score_bank(m, g):
    return 2 if g == 2 else (m % 2) * 3 + g


def t_bank(slot):
    return 5 + slot % 2


def misc_at(m, lag, nxt):
    if m in (1, 2, 3):
        return ("y", 0, m - 1)
    if m in (8, 9, 10) and nxt:
        return ("y", 1, m - 8)
    if m in Q_STEPS and nxt:
        return ("q", 0, Q_STEPS.index(m))
    if m == O_STEP and lag:
        return ("o", 0, 0)
    return None


def cross_attention(nc, K, name, ctx_dram, xT, M, qbias, scale, wv, oT, Zall, with_ln,
                    g_bc=None, b_bc=None):
    nchunk = oT.shape[1]
    ps, ident = K.ps, K.ident
    PT, P, YH, YL, YF, yt, yv, yraw = K.PT, K.P, K.YH, K.YL, K.YF, K.yt, K.yv, K.yraw
    QF, Q, U, NM, MP, ZP = K.QF, K.Q, K.U, K.NM, K.MP, K.ZP
    LNS = K.LNS

    def sem(s):
        return K.sem(f"{name}_{s}")

    y_loaded = [sem("y_loaded0"), sem("y_loaded1")]
    y_sum1, y_cent, y_sq, y_sum2 = sem("y_sum1"), sem("y_cent"), sem("y_sq"), sem("y_sum2")
    yn_done = sem("yn_done")
    yv_done = sem("yv_done")
    yT_done, yT_copied = sem("yT_done"), sem("yT_copied")
    yh_done, yl_done = sem("yh_done"), sem("yl_done")
    q_done, q_copied = sem("q_done"), sem("q_copied")
    qh_done, ql_done = sem("qh_done"), sem("ql_done")
    sc_done = sem("sc_done")
    mxp_done, mx_done = sem("mxp_done"), sem("mx_done")
    ex_shared, ex_done = sem("ex_shared"), sem("ex_done")
    tr_done = sem("tr_done")
    cp = [sem(f"cp{g}") for g in range(GROUPS)]
    pv_done, u_done = sem("pv_done"), sem("u_done")
    o_done, o_copied = sem("o_done"), sem("o_copied")
    z_done = sem("z_done")
    pool_step = sem("pool_step")

    def for_pairs(eng, emit):
        emit(0, False, True, True)
        with eng.Fori(1, 7) as p:
            emit(p, True, True, True)
        emit(7, True, True, False)
        emit(8, True, False, False)

    def pe_free_t_bank(pe, p, m, g, misc, lag, cur, nxt):
        slot = 3 * m + g
        if misc:
            pm, pg = divmod(slot - 1, 3)
            blk = 14 * p + pm - 2
            if pm - 2 >= 0 or lag:
                pe.wait_ge(cp[pg], blk + 1)
            return
        before = misc_at(m - 1, lag, nxt) if g == 0 and m > 0 and cur else None
        if g == 0 and m > 0 and not cur:
            before = None
        if before:
            kind, par, k = before
            if kind == "y":
                pe.wait_ge(yT_copied, 6 * p + 3 * (par + 1) + k + 1)
            elif kind == "q":
                pe.wait_ge(q_copied, 4 * p + 4 + k + 1)
            else:
                pe.wait_ge(o_copied, p)
            return
        pm, pg = divmod(slot - 2, 3)
        if pm - 2 >= 0 or lag:
            pe.wait_ge(cp[pg], 14 * p + pm - 2 + 1)

    def pe_y_transposes(beta, par, g, bank):
        for j in range(GT):
            last = nc.tensor.transpose(ps[:, bank, TT * j:TT * j + TT], yt[:, par, GT * g + j, :],
                                       ident[0:TT, 0:TT])
        last.then_inc(yT_done, 1)

    def pe_q(p_next, k, bank):
        for h in range(4):
            last = nc.tensor.matmul(ps[:, bank, 112 * h:112 * h + 112], M[:, 4 * k + h, :],
                                    xT[:, bass.ds(112 * p_next, 112)], start=True, stop=True)
        last.then_inc(q_done, 1)

    def pe_o(bank):
        for h in range(16):
            if nchunk == 4:
                j, c, first, final = h % 4, h // 4, True, True
            else:
                j, c, first, final = h // 4, 0, h % 4 == 0, h % 4 == 3
            last = nc.tensor.matmul(ps[32 * j:32 * j + 32, bank, 112 * c:112 * c + 112],
                                    wv[:, h, :], U[:, h, :], start=first, stop=final,
                                    skip_group_check=True)
        last.then_inc(o_done, 1)

    def pe_sums(pe, beta, par, w, g):
        if g == 0 or not 6 <= w <= 11:
            return
        half, k = divmod(w - 6, 3)
        first_pair = k == 0 and g == 1
        if first_pair:
            for gg in range(GROUPS):
                pe.wait_ge(cp[gg], 7 * beta + (4 if half == 0 else 7))
            if half == 0:
                pe.wait_ge(yv_done, beta + 1)
        if first_pair and not (isinstance(beta, int) and beta == 0 and half == 0):
            pe.wait_ge(u_done, 2 * beta + half)
        for j in (4 * k + 2 * (g - 1), 4 * k + 2 * (g - 1) + 1):
            rows = slice(64 * (j % 2), 64 * (j % 2) + 64)
            last = nc.tensor.matmul(ps[rows, BANK_V, 0:HALF], yv[:, par, j, :],
                                    PT[0:TT, par, j, HALF * half:HALF * half + HALF],
                                    start=j < 2, stop=j >= NTT - 2, skip_group_check=True)
        if k == 2 and g == 2:
            last.then_inc(pv_done, 1)

    def pe_pair(pe):
        def emit(p, lag, cur, nxt):
            for m in range(STEPS if cur else BLOCKS):
                par, i = divmod(m, BLOCKS)
                n = 14 * p + m
                for g in range(GROUPS):
                    slot = 3 * m + g
                    if (lag and m < 2) or (cur and m >= 2):
                        pe_free_t_bank(pe, p, m, g, False, lag, cur, nxt)
                        if g == 0:
                            pe.wait_ge(ex_done, n - 1)
                        for j in range(GT):
                            last = nc.tensor.transpose(
                                ps[0:TT, t_bank(slot), 128 * j:128 * j + 128],
                                P[:, m % 2, GC * g + TT * j:GC * g + TT * j + TT], ident[:, :])
                        last.then_inc(tr_done, 1)
                    if cur:
                        if i == 0 and g == 0:
                            pe.wait_ge(ql_done, 2 * p + par + 1)
                            pe.wait_ge(yl_done, 2 * p + par + 1)
                        if g == 0 and (lag or m >= 2):
                            pe.wait_ge(ex_done, n - 1)
                        if g == 2 and (lag or m >= 1):
                            pe.wait_ge(ex_shared, n)
                        bank = score_bank(m, g)
                        rows = Q[:, par, 128 * i:128 * i + 128]
                        nc.tensor.matmul(ps[:, bank, 0:GC], rows, YH[:, par, GC * g:GC * g + GC],
                                         start=True, stop=False)
                        nc.tensor.matmul(ps[:, bank, 0:GC], rows, YL[:, par, GC * g:GC * g + GC],
                                         start=False, stop=True).then_inc(sc_done, 1)
                    if cur:
                        if 6 <= m <= 11:
                            pe_sums(pe, 2 * p, 0, m, g)
                        if m == 13:
                            pe_sums(pe, 2 * p + 1, 1, 6, g)
                    if lag and m <= 4:
                        pe_sums(pe, 2 * p - 1, 1, m + 7, g)
                misc = misc_at(m, lag, nxt)
                if misc and (cur or misc[0] == "o"):
                    kind, mp, k = misc
                    bank = t_bank(3 * m + 3)
                    pe_free_t_bank(pe, p, m, 2, True, lag, cur, nxt) if cur else pe.wait_ge(cp[2], 112)
                    if kind == "y":
                        beta = 2 * p + 1 + mp
                        if with_ln:
                            pe.wait_ge(yn_done, beta + 1)
                        else:
                            pe.wait_ge(y_loaded[(1 + mp) % 2], 16 * (beta - (1 + mp) % 2) + 32)
                        pe_y_transposes(beta, (1 + mp) % 2, k, bank)
                    elif kind == "q":
                        pe_q(p + 1, k, bank)
                    else:
                        pe.wait_ge(u_done, 4 * p)
                        pe_o(bank)
        return emit

    def copy_group(eng, copy, p, m, g, lag):
        slot = 3 * m + g
        n2 = 14 * p + m - 2
        par, i = divmod((m - 2) % STEPS, BLOCKS)
        eng.wait_ge(tr_done, 3 * n2 + g + 1)
        old = not (isinstance(p, int) and 2 * p + (m - 2) // BLOCKS < 2)
        if old:
            beta = 2 * p + (m - 2) // BLOCKS
            eng.wait_ge(pv_done, 2 * beta - 3 + (i >= 3))
        copy(PT[0:TT, par, GT * g:GT * g + GT, 128 * i:128 * i + 128],
             ps[0:TT, t_bank(slot), :].rearrange("p (j c) -> p j c", j=GT)).then_inc(cp[g], 1)

    def act_pair(act):
        def emit(p, lag, cur, nxt):
            for m in range(STEPS if cur else BLOCKS):
                n = 14 * p + m
                t_here = (lag and m < 2) or (cur and m >= 2)
                if t_here:
                    copy_group(act, nc.scalar.copy, p, m, 0, lag)
                if (cur and m >= 1) or (lag and m == 0):
                    pm = (m - 1) % STEPS
                    act.wait_ge(mx_done, n)
                    if lag or m >= 3:
                        act.wait_ge(tr_done, 3 * n - 6)
                    if pm % BLOCKS == 0 and lag:
                        act.wait_ge(z_done, 2 * p + pm // BLOCKS - 1)
                    nc.scalar.activation(P[:, pm % 2, 2 * GC:3 * GC], ps[:, 2, 0:GC], ACT.Exp,
                                         bias=NM[:, pm:pm + 1], scale=scale,
                                         accum_out=ZP[:, pm, 0:1]).then_inc(ex_shared, 1)
                    b = (pm % 2) * 3
                    nc.scalar.activation(P[:, pm % 2, 0:2 * GC].rearrange("p (a b) -> p a b", a=2),
                                         ps[:, b:b + 2, 0:GC], ACT.Exp, bias=NM[:, pm:pm + 1],
                                         scale=scale, accum_out=ZP[:, pm, 1:2]).then_inc(ex_done, 1)
                if t_here:
                    copy_group(act, nc.scalar.copy, p, m, 2, lag)
                for beta, par, w, live in ((2 * p, 0, m, cur), (2 * p - 1, 1, m + 7, lag)):
                    if live and w in (8, 11):
                        half = 0 if w == 8 else 1
                        act.wait_ge(pv_done, 2 * beta + half + 1)
                        nc.scalar.copy(U[:, 8 * half:8 * half + 8, 56 * par:56 * par + 56],
                                       ps[:, BANK_V, 0:HALF].rearrange("p (h s) -> p h s", h=8)
                                       ).then_inc(u_done, 1)
                misc = misc_at(m, lag, nxt)
                if misc and (cur or misc[0] == "o"):
                    kind, mp, k = misc
                    bank = t_bank(3 * m + 3)
                    if kind == "y":
                        act_y_copy(act, 2 * p + 1 + mp, k, bank, False)
                    elif kind == "q" and qbias is None:
                        act_q_copy(act, p + 1, k, bank, False)
                    elif kind == "o":
                        act.wait_ge(o_done, p)
                        nc.scalar.copy(oT[:, :, bass.ds(112 * (p - 1), 112)],
                                       ps[:, bank, 0:112 * nchunk].rearrange("p (c t) -> p c t", c=nchunk)
                                       ).then_inc(o_copied, 1)
        return emit

    def act_y_copy(act, beta, k, bank, first):
        act.wait_ge(yT_done, 3 * beta + k + 1)
        if not first:
            act.wait_ge(yl_done, beta)
        nc.scalar.copy(YF[:, GC * k:GC * k + GC], ps[:, bank, 0:GC]).then_inc(yT_copied, 1)

    def act_q_copy(act, p, k, bank, first):
        act.wait_ge(q_done, 4 * p + k + 1)
        if not first:
            act.wait_ge(ql_done, 2 * p)
        nc.scalar.copy(QF[:, 4 * k:4 * k + 4, :],
                       ps[:, bank, 0:448].rearrange("p (h t) -> p h t", h=4)).then_inc(q_copied, 1)

    def dve_q_copy(dve, p, k, bank, first):
        dve.wait_ge(q_done, 4 * p + k + 1)
        if not first:
            dve.wait_ge(ql_done, 2 * p)
        nc.vector.tensor_tensor(QF[:, 4 * k:4 * k + 4, :],
                                ps[:, bank, 0:448].rearrange("p (h t) -> p h t", h=4),
                                qbias[:, 4 * k:4 * k + 4].unsqueeze(2).broadcast_to([128, 4, 112]),
                                ALU.add).then_inc(q_copied, 1)

    def dve_q_high(dve, p, par, old):
        dve.wait_ge(q_copied, 4 * p + 4)
        if old:
            dve.wait_ge(sc_done, 42 * p + 21 * par - 21)
        nc.vector.tensor_copy(Q[:, par, :].rearrange("p (h s) -> p h s", h=16),
                              QF[:, :, 56 * par:56 * par + 56]).then_inc(qh_done, 1)

    def dve_y_high(dve, beta, par, old):
        dve.wait_ge(yT_copied, 3 * beta + 3)
        if old:
            dve.wait_ge(sc_done, 21 * (beta - 1))
        nc.vector.tensor_copy(YH[:, par, :], YF[:, :]).then_inc(yh_done, 1)

    def dve_y_sum1(dve, beta, par):
        dve.wait_ge(y_loaded[par], 8 * (beta - par) + 16)
        if not (isinstance(beta, int) and beta < 2):
            dve.wait_ge(yn_done, beta - 1)
        nc.vector.tensor_reduce(LNS[0:TT, par, 0, :], yraw[:, par, :, :], axis=AX.X,
                                op=ALU.add).then_inc(y_sum1, 1)

    def dve_y_sum2(dve, beta, par):
        dve.wait_ge(y_sq, beta + 1)
        nc.vector.tensor_reduce(LNS[0:TT, par, 1, :], yt[:, par, :, 0:64], axis=AX.X,
                                op=ALU.add).then_inc(y_sum2, 1)

    def dve_pair(dve):
        def emit(p, lag, cur, nxt):
            for m in range(STEPS if cur else BLOCKS):
                par, i = divmod(m, BLOCKS)
                n = 14 * p + m
                if cur and m == 0:
                    dve_q_high(dve, p, 1, lag)
                if nxt and m == 12:
                    dve_q_high(dve, p + 1, 0, True)
                if cur and m == 4:
                    dve_y_high(dve, 2 * p + 1, 1, lag)
                if nxt and m == 11:
                    dve_y_high(dve, 2 * p + 2, 0, True)
                if with_ln and nxt and i == 1:
                    dve_y_sum1(dve, 2 * p + par + 2, par)
                if with_ln and nxt and i == 3:
                    dve_y_sum2(dve, 2 * p + par + 2, par)
                if (lag and m < 2) or (cur and m >= 2):
                    copy_group(dve, nc.vector.tensor_copy, p, m, 1, lag)
                if cur:
                    b = (m % 2) * 3
                    dve.wait_ge(sc_done, 3 * n + 2)
                    nc.vector.tensor_reduce(MP[:, m, 0:1], ps[:, b:b + 2, 0:GC], axis=AX.XY, op=ALU.max)
                    dve.wait_ge(sc_done, 3 * n + 3)
                    nc.vector.tensor_reduce(MP[:, m, 1:2], ps[:, 2, 0:GC], axis=AX.X,
                                            op=ALU.max).then_inc(mxp_done, 1)
                    dve.wait_ge(mxp_done, n + 1)
                    nc.vector.tensor_scalar(NM[:, m:m + 1], MP[:, m, 0:1], MP[:, m, 1:2], -scale,
                                            ALU.max, ALU.mult).then_inc(mx_done, 1)
                misc = misc_at(m, lag, nxt)
                if misc and cur and misc[0] == "q" and qbias is not None:
                    dve_q_copy(dve, p + 1, misc[2], t_bank(3 * m + 3), False)
        return emit

    class PoolOrder:
        def __init__(self, pool, base):
            self.pool, self.base, self.k = pool, base, 0

        def then(self, ins, more=None):
            ins.then_inc(pool_step, 1)
            self.k += 1
            self.pool.wait_ge(pool_step, self.base + self.k)

    def pool_y_low(o, beta, par, old):
        o.pool.wait_ge(yh_done, beta + 1)
        if old:
            o.pool.wait_ge(sc_done, 21 * (beta - 1))
        nc.gpsimd.tensor_tensor(YL[:, par, :], YF[:, :], YH[:, par, :].bitcast(F32),
                                ALU.subtract).then_inc(yl_done, 1)
        o.pool.wait_ge(yl_done, beta + 1)

    def pool_q_low(o, beta, p, par):
        o.pool.wait_ge(qh_done, beta + 1)
        nc.gpsimd.tensor_tensor(Q[64:128, par, :].rearrange("p (h s) -> p h s", h=16),
                                QF[64:128, :, 56 * par:56 * par + 56],
                                Q[64:128, par, :].rearrange("p (h s) -> p h s", h=16).bitcast(F32),
                                ALU.subtract).then_inc(ql_done, 1)
        o.pool.wait_ge(ql_done, beta + 1)

    def pool_yv(o, beta, par, old):
        if with_ln:
            o.pool.wait_ge(yn_done, beta + 1)
        else:
            o.pool.wait_ge(y_loaded[par], 16 * (beta - par) + 32)
        if old:
            o.pool.wait_ge(pv_done, 2 * beta - 2)
        nc.gpsimd.tensor_tensor(yv[:, par, :, :], yt[:, par, :, 0:64], K.zero_bc, ALU.add).then_inc(yv_done, 1)
        o.pool.wait_ge(yv_done, beta + 1)

    def pool_z(o, beta, par):
        o.pool.wait_ge(ex_done, 7 * beta + 7)
        nc.gpsimd.tensor_tensor(Zall[:, bass.ds(7 * beta, 7)], ZP[:, 7 * par:7 * par + 7, 0],
                                ZP[:, 7 * par:7 * par + 7, 1], ALU.add).then_inc(z_done, 1)
        o.pool.wait_ge(z_done, beta + 1)

    def pool_ln1(o, beta, par):
        o.pool.wait_ge(y_sum1, beta + 1)
        ymean = LNS[0:TT, par, 0, :]
        o.then(nc.gpsimd.tensor_tensor(LNS[0:TT, par, 2, :], ymean, K.inv64, ALU.mult))
        nc.gpsimd.tensor_tensor(yraw[:, par, :, :], yraw[:, par, :, :],
                                LNS[0:TT, par, 2, :].unsqueeze(2).broadcast_to([TT, NTT, 64]),
                                ALU.subtract).then_inc(y_cent, 1)
        o.pool.wait_ge(y_cent, beta + 1)
        if not (isinstance(beta, int) and beta < 2):
            o.pool.wait_ge(yT_done, 3 * (beta - 2) + 3)
        nc.gpsimd.tensor_tensor(yt[:, par, :, 0:64], yraw[:, par, :, :], yraw[:, par, :, :],
                                ALU.mult).then_inc(y_sq, 1)
        o.pool.wait_ge(y_sq, beta + 1)

    def pool_ln2(o, beta, par):
        o.pool.wait_ge(y_sum2, beta + 1)
        o.then(nc.gpsimd.tensor_tensor(LNS[0:TT, par, 1, :], LNS[0:TT, par, 1, :], K.inv64, ALU.mult))
        o.then(nc.gpsimd.tensor_tensor(LNS[0:TT, par, 1, :], LNS[0:TT, par, 1, :], K.eps12, ALU.add))
        o.then(nc.gpsimd.tensor_tensor(LNS[0:TT, par, 1, :], LNS[0:TT, par, 1, :], K.mhalf12[0:TT, :], ALU.pow))
        o.then(nc.gpsimd.tensor_tensor(yraw[:, par, :, :], yraw[:, par, :, :],
                                       LNS[0:TT, par, 1, :].unsqueeze(2).broadcast_to([TT, NTT, 64]),
                                       ALU.mult))
        o.then(nc.gpsimd.tensor_tensor(yraw[:, par, :, :], yraw[:, par, :, :],
                                       g_bc.unsqueeze(1).broadcast_to([TT, NTT, 64]), ALU.mult))
        o.then(nc.gpsimd.tensor_tensor(yt[:, par, :, 0:64], yraw[:, par, :, :],
                                       b_bc.unsqueeze(1).broadcast_to([TT, NTT, 64]), ALU.add))
        nc.gpsimd.tensor_tensor(yt[:, par, :, 64:128], yraw[:, par, :, :],
                                b_bc.unsqueeze(1).broadcast_to([TT, NTT, 64]),
                                ALU.add).then_inc(yn_done, 1)
        o.pool.wait_ge(yn_done, beta + 1)

    LN_STEPS = 7
    PRE = 2 * LN_STEPS if with_ln else 0

    def pool_pair(pool):
        def emit(p, lag, cur, nxt):
            o = PoolOrder(pool, PRE + 2 * LN_STEPS * p)
            for par in range(2 if cur else 1):
                beta = 2 * p + par
                if cur and par == 0:
                    pool_q_low(o, beta + 1, p, 1)
                if cur:
                    pool_yv(o, beta, par, lag)
                if par == 1 or lag:
                    pool_z(o, beta - 1, (par + 1) % 2)
                if with_ln and nxt:
                    pool_ln1(o, beta + 2, par)
                if (par == 0 and cur) or nxt:
                    pool_y_low(o, beta + 1, (par + 1) % 2, lag or par == 1)
                if par == 1 and nxt:
                    pool_q_low(o, beta + 1, p + 1, 0)
                if with_ln and nxt:
                    pool_ln2(o, beta + 2, par)
        return emit

    ctx_v = ctx_dram.rearrange("b (r j) c -> b r j c", j=NTT)

    with nc.Block() as block:
        @block.sync
        def _(sp):
            def load(k, par):
                src = ctx_v[bass.ds(k, 1), :, :, :].rearrange("b r j c -> (b r) j c")
                if with_ln:
                    sp.dma_start(yraw[:, par, :, :], src).then_inc(y_loaded[par], 16)
                else:
                    for half in range(2):
                        sp.dma_start(yt[:, par, :, 64 * half:64 * half + 64], src).then_inc(y_loaded[par], 16)

            load(0, 0)
            load(1, 1)
            with sp.Fori(0, 7) as p:
                for par in range(2):
                    k = 2 * p + 2 + par
                    if with_ln:
                        sp.wait_ge(yn_done, k - 1)
                    else:
                        sp.wait_ge(yv_done, k - 1)
                        sp.wait_ge(yT_done, 3 * k - 3)
                    load(k, par)

        @block.tensor
        def _(pe):
            for k in range(4):
                if k >= 2:
                    pe.wait_ge(q_copied, k - 1)
                pe_q(0, k, 5 + k % 2)
            if with_ln:
                pe.wait_ge(yn_done, 1)
            else:
                pe.wait_ge(y_loaded[0], 32)
            for g in range(3):
                if g < 2:
                    pe.wait_ge(q_copied, 3 + g)
                else:
                    pe.wait_ge(yT_copied, 1)
                pe_y_transposes(0, 0, g, 5 + g % 2)
            pe.wait_ge(yT_copied, 3)
            for_pairs(pe, pe_pair(pe))

        @block.scalar
        def _(act):
            if qbias is None:
                for k in range(4):
                    act_q_copy(act, 0, k, 5 + k % 2, True)
            for g in range(3):
                act_y_copy(act, 0, g, 5 + g % 2, True)
            for_pairs(act, act_pair(act))

        @block.vector
        def _(dve):
            if qbias is not None:
                for k in range(4):
                    dve_q_copy(dve, 0, k, 5 + k % 2, True)
            if with_ln:
                dve_y_sum1(dve, 0, 0)
                dve_y_sum1(dve, 1, 1)
            dve_q_high(dve, 0, 0, False)
            if with_ln:
                dve_y_sum2(dve, 0, 0)
            dve_y_high(dve, 0, 0, False)
            if with_ln:
                dve_y_sum2(dve, 1, 1)
            for_pairs(dve, dve_pair(dve))

        @block.gpsimd
        def _(pool):
            o = PoolOrder(pool, 0)
            if with_ln:
                pool_ln1(o, 0, 0)
                pool_ln2(o, 0, 0)
            pool_q_low(o, 0, 0, 0)
            pool_y_low(o, 0, 0, False)
            if with_ln:
                pool_ln1(o, 1, 1)
                pool_ln2(o, 1, 1)
            for_pairs(pool, pool_pair(pool))


def block_selector(pool_order, nc, t, width, group):
    o = pool_order
    o.then(nc.gpsimd.memset(t, 1.0))
    o.then(nc.gpsimd.affine_select(t, t, pattern=[[1, width]], compare_op=ALU.is_ge, fill=0.0,
                                   base=0, channel_multiplier=-group))
    o.then(nc.gpsimd.affine_select(t, t, pattern=[[-1, width]], compare_op=ALU.is_ge, fill=0.0,
                                   base=group - 1, channel_multiplier=group))


def group_mask(pool_order, nc, t, heads, group):
    o = pool_order
    o.then(nc.gpsimd.memset(t, 1.0))
    o.then(nc.gpsimd.affine_select(t, t, pattern=[[-group, heads]], compare_op=ALU.is_ge, fill=0.0,
                                   base=0, channel_multiplier=1))
    o.then(nc.gpsimd.affine_select(t, t, pattern=[[group, heads]], compare_op=ALU.is_ge, fill=0.0,
                                   base=group - 1, channel_multiplier=-1))


class Arena:

    def __init__(self, flat):
        self.flat, self.at = flat, 0

    def take(self, *shape, parts=128):
        n = 1
        for s in shape:
            n *= s
        v = self.flat[0:parts, self.at:self.at + n]
        self.at += n
        assert self.at <= self.flat.shape[1]
        if len(shape) == 2:
            v = v.rearrange("p (a b) -> p a b", a=shape[0])
        elif len(shape) == 3:
            v = v.rearrange("p (a b c) -> p a b c", a=shape[0], b=shape[1])
        return v


def decoder_kernel(nc, d, out):
    with ExitStack() as ctx:
        build(nc, d, out, Kit(nc, ctx))


def build(nc, d, out, K):
    xin = d["x"].rearrange("b s c -> (b s) c")
    yout = out.rearrange("b s c -> (b s) c")

    K.ps = K.ctx.enter_context(nc.psum_tensor("ps", [128, 8, 512], F32))
    arena = K.sb("arena", [128, 2 * NTT * 896])
    K.PT = arena[:, :].rearrange("p (u j c) -> p u j c", u=2, j=NTT)
    K.P = K.sb("P", [128, 2, NTT * TT])
    K.YH, K.YL = K.sb("YH", [128, 2, NTT * TT], F32R), K.sb("YL", [128, 2, NTT * TT], F32R)
    K.YF = K.sb("YF", [128, NTT * TT])
    K.yt = K.sb("yt", [TT, 2, NTT, 128])
    K.yv, K.yraw = K.sb("yv", [TT, 2, NTT, 64]), K.sb("yraw", [TT, 2, NTT, 64])
    K.QF, K.Q = K.sb("QF", [128, 16, TP]), K.sb("Q", [128, 2, 16 * SQ], F32R)
    K.U = K.sb("U", [128, 16, TP])
    K.NM, K.MP, K.ZP = K.sb("NM", [128, STEPS]), K.sb("MP", [128, STEPS, 2]), K.sb("ZP", [128, STEPS, 2])
    K.LNS = K.sb("LNS", [128, 2, 3, NTT])
    K.b1s, K.cws = K.sb("b1s", [128, 2, NF]), K.sb("cws", [TP, 2, NT])
    K.ln_stats, K.ln_mv = K.sb("ln_stats", [TP, NT, 6]), K.sb("ln_mv", [TP, NT, 2])
    K.ln_rstd = K.sb("ln_rstd", [TP, 2, NT])
    X = K.sb("X", [TP, NT, CH])
    xnT = K.sb("xnT", [128, NTOK])
    oT = K.sb("oT", [128, 4, NTOK])
    Zall = K.sb("Zall", [128, BLOCKS * NB])
    M = K.sb("M", [128, 16, 128])
    wv = K.sb("wv", [128, 16, 32])
    qbias = K.sb("qbias", [128, 16])
    K.ident = K.sb("ident", [128, 128])
    K.mhalf12, inv64 = K.sb("mhalf12", [128, NTT]), K.sb("inv64", [TT, NTT])
    eps12, zero = K.sb("eps12", [TT, NTT]), K.sb("zero", [TT, 1])
    K.inv64, K.eps12 = inv64[:, :], eps12[:, :]
    K.zero_bc = zero[:, :].unsqueeze(2).broadcast_to([TT, NTT, CTX_C])
    K.expert_m8 = K.sb("expert_m8", [TP, NT, NE])
    hm0, hm1 = K.sb("hm0", [128, 4]), K.sb("hm1", [128, 16])
    lny = K.sb("lny", [TT, 2, CTX_C])
    VECS = ["L0_xattn_a1_lnx_g", "L0_xattn_a1_lnx_b", "L0_xattn_a1_lny_g", "L0_xattn_a1_lny_b",
            "L0_xattn_a1_ln3_g", "L0_xattn_a1_ln3_b", "L0_xattn_a2_lnx_g", "L0_xattn_a2_lnx_b",
            "L0_xattn_a2_ln3_g", "L0_xattn_a2_ln3_b", "L1_xattn_bq", "L1_xattn_bv"]
    MATS = [("L0_xattn_a1_li2_b", NF), ("L0_xattn_a2_li2_b", NF), ("L0_ffn_b1", NE * NF),
            ("L1_ffn_b1", NE * NF), ("L0_ffn_w_gate", NE)]
    at, ncols = {}, 0
    for v, n in [(v, 1) for v in VECS] + MATS:
        at[v] = (ncols, ncols + n)
        ncols += n
    cols = K.sb("cols", [128, ncols])

    def col(v):
        a, b = at[v]
        return cols[:, a:b]

    K.z_dram = nc.dram_tensor("z_scratch", [BLOCKS * NB, 128], F32).ap()

    A = Arena(arena)
    XA, XO = A.take(NT, CH), A.take(NT, CH)
    ynT = A.take(NTOK)
    qT_at = A.at
    qT, kT = A.take(4, NTOK + 8), A.take(4, NTOK)
    hT = arena[:, qT_at:qT_at + NF * NTOK].rearrange("p (f t) -> p f t", f=NF)
    a1 = {k: A.take(512) for k in ("wq", "wk", "wv")}
    li1, li2, li3 = A.take(4, CH), A.take(HID), A.take(NF, CH)
    QS, KS, YS, VS = A.take(4, CH), A.take(4, TP), A.take(TP), A.take(2, 512)
    E, AT, MX, SM = A.take(16, SQ), A.take(16, 120), A.take(16), A.take(16)
    K.wkt = A.take(CTX_C)
    WQ2, WK2 = A.take(512), A.take(512)
    WQT, WKM = A.take(CH), A.take(4, CTX_C)
    rows = {k: A.take(CH, parts=TP) for k in ("ln1_g", "ln1_b", "ln2_g", "ln2_b", "a1_li1_b", "a1_li3_b")}
    stage = A.take(CH)
    mask, mask_b = A.take(SQ), A.take(SQ)
    K.mask = mask

    x_loaded, rows_loaded, vecs_loaded = K.sem("x_loaded"), K.sem("rows_loaded"), K.sem("vecs_loaded")
    a1_loaded, a2_loaded = K.sem("a1_loaded"), K.sem("a2_loaded")
    const_step, const_dve = K.sem("const_step"), K.sem("const_dve")
    cols_done = K.sem("cols_done")

    def bcast(v, n=TP):
        return v.unsqueeze(0).broadcast_to([n, v.shape[0]])

    def by_head(w):
        return w.rearrange("h c d -> c h d")

    def heads_of(t, parts=128):
        return t[0:parts, :].rearrange("p (h d) -> p h d", h=16)

    with nc.Block() as block:
        @block.sync
        def _(sp):
            sp.dma_start(X[:, :, :], row_tiles(xin)).then_inc(x_loaded, 16)
            for k in rows:
                sp.dma_start(rows[k], bcast(d["L0_xattn_" + k])).then_inc(rows_loaded, 16)
            for v in VECS:
                sp.dma_start(stage[at[v][0]:at[v][1], :], d[v].unsqueeze(0)).then_inc(vecs_loaded, 16)
            for v, n in MATS:
                src = d[v]
                if len(src.shape) == 1:
                    src = src.rearrange("(f p) -> f p", p=128)
                elif src.shape[1] == HID:
                    src = src.rearrange("e (f p) -> (e f) p", p=128)
                sp.dma_start(stage[at[v][0]:at[v][1], :], src).then_inc(vecs_loaded, 16)
            for i, k in enumerate(("g", "b")):
                sp.dma_start(lny[:, i, :], bcast(d["L0_xattn_a2_lny_" + k], TT)).then_inc(a2_loaded, 16)
            sp.wait_ge(x_loaded, 16)

        @block.scalar
        def _(act):
            for k in ("wq", "wk", "wv"):
                act.dma_start(heads_of(a1[k]), by_head(d["L0_xattn_a1_" + k])).then_inc(a1_loaded, 16)
            act.dma_start(li1, d["L0_xattn_a1_li1_w"].rearrange("(c p) o -> p c o", p=128)).then_inc(a1_loaded, 16)
            act.dma_start(li2, d["L0_xattn_a1_li2_w"]).then_inc(a1_loaded, 16)
            act.dma_start(li3, d["L0_xattn_a1_li3_w"].rearrange("(c p) o -> p c o", p=128)).then_inc(a1_loaded, 16)
            act.dma_start(heads_of(WQ2), by_head(d["L0_xattn_a2_wq"])).then_inc(a2_loaded, 16)
            act.dma_start(heads_of(WK2, 64), by_head(d["L0_xattn_a2_wk"])).then_inc(a2_loaded, 16)
            for half in range(2):
                act.dma_start(wv[64 * half:64 * half + 64, :, :], by_head(d["L0_xattn_a2_wv"])
                              ).then_inc(a2_loaded, 16)

        @block.vector
        def _(dve):
            nc.vector.memset(K.mhalf12[:, :], -0.5)
            nc.vector.memset(inv64[:, :], 1.0 / CTX_C)
            nc.vector.memset(eps12[:, :], EPS)
            nc.vector.memset(zero[:, :], 0.0)
            nc.vector.memset(QS, 0.0)
            nc.vector.memset(qT[:, :, NTOK:NTOK + 8], 0.0)
            for e in range(NE):
                nc.vector.memset(K.expert_m8[:, :, e:e + 1], float(e - NE))

        @block.gpsimd
        def _(pool):
            o = Chain(pool, const_step)
            o.then(nc.gpsimd.memset(K.ident[:, :], 1.0))
            o.then(nc.gpsimd.affine_select(K.ident[:, :], K.ident[:, :], pattern=[[-1, 128]],
                                           compare_op=ALU.is_equal, fill=0.0, base=0, channel_multiplier=1))
            for t, base in ((mask, 0), (mask_b, 64)):
                o.then(nc.gpsimd.memset(t, 1.0))
                o.then(nc.gpsimd.affine_select(t, t, pattern=[[1, SQ]], compare_op=ALU.is_gt, fill=0.0,
                                               base=base, channel_multiplier=-1))
            o.then(nc.gpsimd.affine_select(mask_b, mask_b, pattern=[[0, SQ]], compare_op=ALU.is_ge, fill=0.0,
                                           base=-64, channel_multiplier=1))
            o.then(nc.gpsimd.tensor_tensor(mask, mask, mask_b, ALU.add))
            group_mask(o, nc, hm0[:, :], 4, 32)
            group_mask(o, nc, hm1[:, :], 16, 8)

    layer_norm(nc, K, "ln_in", X, XA, prefetch=lambda sp: sp.wait_ge(rows_loaded, 96))
    layer_norm(nc, K, "ln1", XA, XA, affine=(X, rows["ln1_g"], rows["ln1_b"]),
               prefetch=lambda sp: sp.wait_ge(vecs_loaded, 16 * (len(VECS) + len(MATS))))
    with nc.Block() as block:
        @block.tensor
        def _(pe):
            nc.tensor.transpose(K.ps[:, 0, 0:ncols], stage[0:ncols, :], K.ident[0:ncols, 0:ncols]
                                ).then_inc(cols_done, 1)

        @block.vector
        def _(dve):
            dve.wait_ge(cols_done, 1)
            nc.vector.tensor_copy(cols[:, :], K.ps[:, 0, 0:ncols])

    A1, A2 = "L0_xattn_a1_", "L0_xattn_a2_"
    layer_norm(nc, K, "ln_xy", X, XA,
               outs=[(xnT, col(A1 + "lnx_g"), col(A1 + "lnx_b")), (ynT, col(A1 + "lny_g"), col(A1 + "lny_b"))],
               prefetch=lambda sp: sp.wait_ge(a1_loaded, 96))
    self_attention(nc, K, xnT, ynT, qT, kT, a1["wq"], a1["wk"], a1["wv"], oT,
                   (QS, KS, YS, VS, E, AT, MX, SM), 32 ** -0.5)
    project_and_add(nc, K, "sa_out", XO, [X], rows["a1_li1_b"], oT, li1)
    layer_norm(nc, K, "ln3a", XO, XA, outs=[(xnT, col(A1 + "ln3_g"), col(A1 + "ln3_b"))])
    hidden_layer(nc, K, "ff1", xnT, li2, col(A1 + "li2_b"), hT)
    project_and_add(nc, K, "ff1_out", X, [X, XO], rows["a1_li3_b"], hT, li3)
    layer_norm(nc, K, "ln2", X, XA, affine=(X, rows["ln2_g"], rows["ln2_b"]))

    layer_norm(nc, K, "ln_x2", X, XA, outs=[(xnT, col(A2 + "lnx_g"), col(A2 + "lnx_b"))],
               prefetch=lambda sp: sp.wait_ge(a2_loaded, 96))
    fold_query_weights(nc, K, "fold0", WQ2, WK2, 4, hm0[:, :], M, WQT, WKM)
    cross_attention(nc, K, "xa0", d["ctx_512"], xnT, M, None, 32 ** -0.5, wv, oT, Zall, True,
                    g_bc=lny[:, 0, :], b_bc=lny[:, 1, :])

    B = Arena(arena)
    XA, XO, XI = B.take(NT, CH), B.take(NT, CH), B.take(NT, CH)
    hT = B.take(NF, NTOK)
    li1, li2, li3 = B.take(4, CH), B.take(HID), B.take(NF, CH)
    li1_b, li3_b = B.take(CH, parts=TP), B.take(CH, parts=TP)
    zt, rzt = B.take(CH), B.take(16, SQ)
    sel = B.take(4, CH)
    Wb1, Wb2, hM = B.take(2, HID), B.take(2, NF, CH), B.take(2, NF, 448)
    b2, gw, bg = B.take(CH, parts=NE), B.take(NE), B.take(NE, parts=TP)
    moe = (B.take(NT, NE), B.take(NT, NE), B.take(NT, NE), B.take(4, NT), B.take(NT, NE), B.take(NTOK, parts=NE))
    WQ1, WK1, Wo = B.take(CH), B.take(CH), B.take(1, CH)
    WQT1, WKM1, wkt1 = B.take(CH), B.take(16, CTX_C), B.take(CTX_C)

    def selector(name, nchunk, group):
        step = K.sem(name)
        with nc.Block() as block:
            @block.gpsimd
            def _(pool):
                block_selector(Chain(pool, step), nc, sel[0:16, 0:nchunk, :].rearrange("p c f -> p (c f)"),
                               128 * nchunk, group)

    post_loaded = K.sem("post_loaded")

    def load_post(sp):
        for dst, src in ((li1, d[A2 + "li1_w"].rearrange("(c p) o -> p c o", p=128)),
                         (li1_b, bcast(d[A2 + "li1_b"])), (li3_b, bcast(d[A2 + "li3_b"])),
                         (li2, d[A2 + "li2_w"]),
                         (li3, d[A2 + "li3_w"].rearrange("(c p) o -> p c o", p=128)),
                         (XI[0:TP, :, :], row_tiles(xin))):
            sp.dma_start(dst, src).then_inc(post_loaded, 16)
        sp.wait_ge(post_loaded, 96)

    selector("sel0", 4, 32)
    normalise_attention(nc, K, "nrm0", Zall, oT, sel, None, zt, rzt, prefetch=load_post)
    project_and_add(nc, K, "xa0_out", XO, [X], li1_b, oT, li1)
    layer_norm(nc, K, "ln3b", XO, XA, outs=[(xnT, col(A2 + "ln3_g"), col(A2 + "ln3_b"))])
    hidden_layer(nc, K, "ff2", xnT, li2, col(A2 + "li2_b"), hT)
    project_and_add(nc, K, "ff2_out", X, [X, XO, XI], li3_b, hT, li3)

    m0_loaded, m0_small = [K.sem("m0_w0"), K.sem("m0_w1")], K.sem("m0_small")
    load0 = expert_loader(nc, K, d["L0_ffn_W1"], d["L0_ffn_W2"], Wb1, Wb2, m0_loaded)

    def load_m0(sp):
        sp.dma_start(b2, d["L0_ffn_b2"]).then_inc(m0_small, 16)
        for u in range(2):
            load0(sp, u, u)
        sp.wait_ge(m0_small, 16)

    layer_norm(nc, K, "ln_m0", X, XA, outs=[(xnT, None, None)], prefetch=load_m0)
    mixture(nc, K, "moe0", X, xnT, col("L0_ffn_w_gate"), None, 2, col("L0_ffn_b1"), b2, load0,
            Wb1, Wb2, m0_loaded, hM, moe)

    l1_loaded, wv_zero = K.sem("l1_loaded"), K.sem("wv_zero")
    with nc.Block() as block:
        @block.vector
        def _(dve):
            nc.vector.memset(wv[:, :, :], 0.0).then_inc(wv_zero, 1)

        @block.sync
        def _(sp):
            sp.dma_start(WQ1, d["L1_xattn_Wq"]).then_inc(l1_loaded, 16)
            sp.dma_start(WK1[0:64, :], d["L1_xattn_Wk"]).then_inc(l1_loaded, 16)
            sp.wait_ge(wv_zero, 1)
            src = d["L1_xattn_Wv"].rearrange("c (a j k) -> c a j k", j=4, k=8)
            dst = wv[:, :, :].rearrange("p (a j) k -> p a j k", j=4)
            for half in range(2):
                for j in range(4):
                    sp.dma_start(dst[64 * half:64 * half + 64, :, j, 8 * j:8 * j + 8], src[:, :, j, :]
                                 ).then_inc(l1_loaded, 16)
    layer_norm(nc, K, "ln_x3", X, XA, outs=[(xnT, None, None)], prefetch=lambda sp: sp.wait_ge(l1_loaded, 160))
    K.wkt = wkt1
    fold_query_weights(nc, K, "fold1", WQ1, WK1, 1, hm1[:, :], M, WQT1, WKM1, bq=col("L1_xattn_bq"), qbias=qbias)
    oT1 = oT[:, 0:1, :]
    cross_attention(nc, K, "xa1", d["ctx_512"], xnT, M, qbias, 8 ** -0.5, wv, oT1, Zall, False)

    wo_loaded = K.sem("wo_loaded")

    def load_wo(sp):
        sp.dma_start(Wo[:, 0, :], d["L1_xattn_Wo"]).then_inc(wo_loaded, 16)
        sp.dma_start(li1_b, bcast(d["L1_xattn_bo"])).then_inc(wo_loaded, 16)
        sp.wait_ge(wo_loaded, 32)

    selector("sel1", 1, 8)
    normalise_attention(nc, K, "nrm1", Zall, oT1, sel, col("L1_xattn_bv"), zt, rzt, prefetch=load_wo)
    project_and_add(nc, K, "xa1_out", X, [X], li1_b, oT1, Wo)

    m1_loaded, m1_small = [K.sem("m1_w0"), K.sem("m1_w1")], K.sem("m1_small")
    load1 = expert_loader(nc, K, d["L1_ffn_W1"], d["L1_ffn_W2"], Wb1, Wb2, m1_loaded)

    def load_m1(sp):
        sp.dma_start(b2, d["L1_ffn_b2"]).then_inc(m1_small, 16)
        sp.dma_start(gw, d["L1_ffn_Wg"]).then_inc(m1_small, 16)
        sp.dma_start(bg, bcast(d["L1_ffn_bg"])).then_inc(m1_small, 16)
        for u in range(2):
            load1(sp, u, u)
        sp.wait_ge(m1_small, 48)

    layer_norm(nc, K, "ln_m1", X, XA, outs=[(xnT, None, None)], prefetch=load_m1)
    mixture(nc, K, "moe1", X, xnT, gw, bg, 1, col("L1_ffn_b1"), b2, load1, Wb1, Wb2, m1_loaded, hM, moe)

    out_stored = K.sem("out_stored")
    with nc.Block() as block:
        @block.sync
        def _(sp):
            sp.dma_start(row_tiles(yout), X[:, :, :]).then_inc(out_stored, 16)
            sp.wait_ge(out_stored, 16)


def kernel(**inputs):
    import numpy as _np
    import concourse.bacc as _bacc
    from concourse import mybir as _mybir
    from concourse.bass_utils import run_bass_kernel_spmd as _run

    nc = _bacc.Bacc("TRN2", target_bir_lowering=False, num_devices=1)
    arrays, d = {}, {}
    for name in inputs:
        a = _np.ascontiguousarray(inputs[name])
        arrays[f"in_{name}_dram"] = a
        d[name] = nc.dram_tensor(f"in_{name}_dram", a.shape, _mybir.dt.from_np(a.dtype), kind="ExternalInput").ap()
    out = nc.dram_tensor("out_0_dram", (NB, SQ, CH), _mybir.dt.float32, kind="ExternalOutput").ap()
    decoder_kernel(nc, d, out)
    r = _run(nc, [arrays], core_ids=[0])
    return r.results[0]["out_0_dram"]
```

```python
from contextlib import ExitStack

import concourse.bass as bass
from concourse import mybir

F32 = mybir.dt.float32
F32R = mybir.dt.float32r
ALU = mybir.AluOpType
ACT = mybir.ActivationFunctionType
AX = mybir.AxisListType

NB, SQ, CH = 16, 56, 128
NTOK = NB * SQ
TP = 112
NT = NTOK // TP
CTX_C = 64
NE, HID = 8, 512
NF = HID // 128
EPS = 1e-5


class Kit:

    def __init__(self, nc, ctx):
        self.nc, self.ctx = nc, ctx
        self.shared_sems, self.chains = {}, {}

    def sb(self, name, shape, dt=F32):
        return self.ctx.enter_context(self.nc.sbuf_tensor(name, shape, dt))

    def sem(self, name):
        return self.ctx.enter_context(self.nc.semaphore(name))

    def shared(self, name, adds):
        if name not in self.shared_sems:
            self.shared_sems[name] = [self.sem(name), 0]
        sem, base = self.shared_sems[name]
        self.shared_sems[name][1] += adds
        return sem, base

    def chain(self, eng, name):
        if name not in self.chains:
            self.chains[name] = [self.sem(name), 0]
        return Chain(eng, *self.chains[name], self.chains[name])


class Chain:

    def __init__(self, eng, sem, n=0, record=None):
        self.eng, self.sem, self.n, self.record = eng, sem, n, record

    def then(self, ins):
        self.n += 1
        if self.record is not None:
            self.record[1] = self.n
        ins.then_inc(self.sem, 1)
        self.eng.wait_ge(self.sem, self.n)


def row_tiles(x):
    return x.rearrange("(n p) c -> p n c", p=TP)


def over_tiles(v, n=NT):
    return v.unsqueeze(1).broadcast_to([v.shape[0], n, v.shape[1]])


def layer_norm(nc, K, name, X, XA, outs=(), affine=None, prefetch=None):
    stats, mv, rstd = K.ln_stats, K.ln_mv, K.ln_rstd
    st_done, st0 = K.shared("ln_st", 2)
    ag_done, ag0 = K.shared("ln_ag", 2)
    var_ready, var0 = K.shared("ln_var", 2)
    rstd_ready, rstd0 = K.shared("ln_rstd", 2)
    xa_ready, xa0 = K.shared("ln_xa", 4)
    xt_ready, xt0 = K.shared("ln_xt", 2 * len(outs))
    gain_done, g0 = K.shared("ln_gain", 2 if affine else 0)
    HT = NT // 2

    def copy_out(eng, out, half, bank):
        dst, gain, bias = out
        src, d = K.ps[:, bank + half, 0:448], dst[:, 448 * half:448 * half + 448]
        if eng is nc.vector:
            eng.tensor_scalar(d, src, gain, bias, ALU.mult, ALU.add)
        elif gain is None:
            eng.copy(d, src)
        else:
            eng.activation(d, src, ACT.Identity, scale=gain, bias=bias)

    with nc.Block() as block:
        if prefetch is not None:
            @block.sync
            def _(sp):
                prefetch(sp)

        @block.vector
        def _(dve):
            for half in range(2):
                t = slice(HT * half, HT * half + HT)
                for n in range(HT * half, HT * half + HT):
                    last = nc.vector.bn_stats(stats[0:TP, n, :], X[0:TP, n, :])
                last.then_inc(st_done, 1)
                dve.wait_ge(st_done, st0 + half + 1)
                for n in range(HT * half, HT * half + HT):
                    last = nc.vector.bn_aggr(mv[0:TP, n, :], stats[0:TP, n, :])
                last.then_inc(ag_done, 1)
                dve.wait_ge(ag_done, ag0 + half + 1)
                nc.vector.tensor_scalar(rstd[0:TP, 0, t], mv[0:TP, t, 1], EPS, None, ALU.add).then_inc(var_ready, 1)
            for half in range(2):
                dve.wait_ge(rstd_ready, rstd0 + half + 1)
                for n in range(HT * half, HT * half + HT):
                    last = nc.vector.tensor_scalar(XA[0:TP, n, :], X[0:TP, n, :], mv[0:TP, n, 0:1],
                                                   rstd[0:TP, 1, n:n + 1], ALU.subtract, ALU.mult)
                    if n % 2:
                        last.then_inc(xa_ready, 1)
            if affine is not None:
                dst, gain, bias = affine
                for half in range(2):
                    t = slice(HT * half, HT * half + HT)
                    dve.wait_ge(xa_ready, xa0 + 2 * half + 2)
                    nc.vector.tensor_tensor(dst[0:TP, t, :], XA[0:TP, t, :], over_tiles(gain, HT),
                                            ALU.mult).then_inc(gain_done, 1)
                for half in range(2):
                    t = slice(HT * half, HT * half + HT)
                    dve.wait_ge(gain_done, g0 + half + 1)
                    nc.vector.tensor_tensor(dst[0:TP, t, :], dst[0:TP, t, :], over_tiles(bias, HT), ALU.add)
            for half in range(2 if len(outs) > 1 else 0):
                dve.wait_ge(xt_ready, xt0 + 2 + half + 1)
                copy_out(nc.vector, outs[1], half, 2)

        @block.gpsimd
        def _(pool):
            for half in range(2):
                t = slice(HT * half, HT * half + HT)
                pool.wait_ge(var_ready, var0 + half + 1)
                nc.gpsimd.tensor_tensor(rstd[0:TP, 1, t], rstd[0:TP, 0, t], K.mhalf12[0:TP, 0:HT],
                                        ALU.pow).then_inc(rstd_ready, 1)
                pool.wait_ge(rstd_ready, rstd0 + half + 1)

        if outs:
            @block.tensor
            def _(pe):
                for o in range(len(outs)):
                    for n in range(NT):
                        if o == 0 and n % 2 == 0:
                            pe.wait_ge(xa_ready, xa0 + n // 2 + 1)
                        last = nc.tensor.transpose(K.ps[:, 2 * o + n // 4, TP * (n % 4):TP * (n % 4) + TP],
                                                   XA[0:TP, n, :], K.ident[0:TP, 0:TP])
                        if n % 4 == 3:
                            last.then_inc(xt_ready, 1)

            @block.scalar
            def _(act):
                for half in range(2):
                    act.wait_ge(xt_ready, xt0 + half + 1)
                    copy_out(nc.scalar, outs[0], half, 0)


def fold_query_weights(nc, K, name, WQ, WK, nchunk, mask, M, WQT, WKM, bq=None, qbias=None):
    nh = 16 // nchunk
    wt_ready, wkm_ready = K.sem(f"{name}_wt"), K.sem(f"{name}_wkm")
    m_ready, m_copied = K.sem(f"{name}_m"), K.sem(f"{name}_mc")
    qb_ready = K.sem(f"{name}_qb") if bq is not None else None
    with nc.Block() as block:
        @block.tensor
        def _(pe):
            for c in range(nchunk):
                if c:
                    pe.wait_ge(wkm_ready, c)
                nc.tensor.transpose(K.ps[:, 0, 0:128], WQ[:, 128 * c:128 * c + 128], K.ident[:, :])
                nc.tensor.transpose(K.ps[:, 0, 128:192], WK[0:64, 128 * c:128 * c + 128],
                                    K.ident[0:64, 0:64]).then_inc(wt_ready, 1)
                pe.wait_ge(wkm_ready, c + 1)
                if c:
                    pe.wait_ge(m_copied, c)
                for b in range(max(1, nh * 64 // 512)):
                    w = min(512, nh * 64)
                    last = nc.tensor.matmul(K.ps[:, 1 + b, 0:w], WQT[:, :],
                                            WKM[:, :, :].rearrange("p h c -> p (h c)")[:, w * b:w * b + w],
                                            start=True, stop=True)
                last.then_inc(m_ready, 1)
            if bq is not None:
                for h in range(16):
                    for half in range(2):
                        last = nc.tensor.matmul(K.ps[64 * half:64 * half + 64, 3, h:h + 1], WKM[:, h, :],
                                                bq, start=True, stop=True, skip_group_check=True)
                last.then_inc(qb_ready, 1)

        @block.vector
        def _(dve):
            o = K.chain(dve, "fold_chain")
            for c in range(nchunk):
                dve.wait_ge(wt_ready, c + 1)
                if c:
                    dve.wait_ge(m_ready, c)
                nc.vector.tensor_copy(WQT[:, :], K.ps[:, 0, 0:128])
                o.then(nc.vector.tensor_copy(K.wkt[:, :], K.ps[:, 0, 128:192]))
                nc.vector.tensor_tensor(WKM[:, :, :], over_tiles(K.wkt[:, :], nh),
                                        mask.unsqueeze(2).broadcast_to([128, nh, 64]),
                                        ALU.mult).then_inc(wkm_ready, 1)
                dve.wait_ge(wkm_ready, c + 1)
                dve.wait_ge(m_ready, c + 1)
                for b in range(max(1, nh * 64 // 512)):
                    w = min(512, nh * 64)
                    k = w // 64
                    for half in range(2):
                        last = nc.vector.tensor_copy(
                            M[:, nh * c + k * b:nh * c + k * b + k, 64 * half:64 * half + 64],
                            K.ps[:, 1 + b, 0:w].rearrange("p (h c) -> p h c", h=k))
                last.then_inc(m_copied, 1)
            if bq is not None:
                dve.wait_ge(qb_ready, 1)
                nc.vector.tensor_copy(qbias[:, :], K.ps[:, 3, 0:16])


def self_attention(nc, K, xT, yT, qT, kT, WQ, WK, WV, oT, bufs, scale):
    QS, KS, YS, VS, E, AT, MX, SM = bufs
    H, D = 16, 32
    proj_done, proj_copied = K.sem("sa_proj"), K.sem("sa_projc")
    with nc.Block() as block:
        @block.tensor
        def _(pe):
            k = 0
            for W, src in ((WQ, xT), (WK, yT)):
                for c in range(4):
                    for half in range(2):
                        if k >= 8:
                            pe.wait_ge(proj_copied, k - 7)
                        nc.tensor.matmul(K.ps[:, k % 8, 0:448], W[:, 128 * c:128 * c + 128],
                                         src[:, 448 * half:448 * half + 448],
                                         start=True, stop=True).then_inc(proj_done, 1)
                        k += 1

        @block.scalar
        def _(act):
            for k in range(16):
                dst, c, half = (qT, kT)[k // 8], k % 8 // 2, k % 2
                act.wait_ge(proj_done, k + 1)
                nc.scalar.copy(dst[:, c, 448 * half:448 * half + 448], K.ps[:, k % 8, 0:448]
                               ).then_inc(proj_copied, 1)

    q_sliced, y_sliced = K.sem("sa_qs"), K.sem("sa_ys")
    v_done, v_copied = K.sem("sa_v"), K.sem("sa_vc")
    sc_done = K.sem("sa_sc")
    mx_done, sub_done = K.sem("sa_mx"), K.sem("sa_sub")
    ex_done, sum_done, rec_done, mask_done, norm_done = (
        K.sem("sa_ex"), K.sem("sa_sum"), K.sem("sa_rec"), K.sem("sa_mask"), K.sem("sa_norm"))
    tr_done, tr_copied = K.sem("sa_tr"), K.sem("sa_trc")
    o_done, o_copied = K.sem("sa_o"), K.sem("sa_oc")

    def wait_from_second(eng, sem, p, value):
        if not isinstance(p, int) or value > 0:
            eng.wait_ge(sem, value)

    def pairs(eng, emit):
        emit(0, 0, False, True)
        emit(1, 1, True, True)
        with eng.Fori(1, NT // 2 - 1) as t:
            emit(2 * t, 0, True, True)
            emit(2 * t + 1, 1, True, True)
        emit(NT - 2, 0, True, True)
        emit(NT - 1, 1, True, True)
        emit(NT, 0, True, False)

    with nc.Block() as block:
        @block.gpsimd
        def _(pool):
            def emit(p, par, lag, cur):
                if cur:
                    e = E[par][0:120, :, 0:SQ]
                    pool.wait_ge(sum_done, p + 1)
                    nc.gpsimd.tensor_tensor(e, e, over_tiles(K.mask[0:120, :], H), ALU.mult).then_inc(mask_done, 1)
                    pool.wait_ge(mask_done, p + 1)
            pairs(pool, emit)

        @block.tensor
        def _(pe):
            def emit(p, par, lag, cur):
                if cur:
                    pe.wait_ge(q_sliced, p + 1)
                    if lag:
                        pe.wait_ge(sub_done, p)
                    for c in range(4):
                        for u in range(2):
                            last = nc.tensor.matmul(
                                K.ps[64 * u:64 * u + 64, c // 2, 4 * SQ * (c % 2):4 * SQ * (c % 2) + 4 * SQ],
                                QS[:, c, 64 * u:64 * u + 64],
                                KS[:, c, u, :], start=True, stop=True, skip_group_check=True)
                    last.then_inc(sc_done, 1)
                if lag:
                    pe.wait_ge(y_sliced, p)
                    for u in range(2):
                        wait_from_second(pe, v_copied, p, 2 * p - 3 + u)
                        nc.tensor.matmul(K.ps[0:120, (6, 2)[u], 0:512], YS[:, u, 0:120], WV[:, :],
                                         start=True, stop=True).then_inc(v_done, 1)
                    for b in range(2):
                        pe.wait_ge(proj_copied, 16)
                        pe.wait_ge(norm_done, p)
                        wait_from_second(pe, tr_copied, p, 2 * p - 2 + b)
                        for g in range(4 * b, 4 * b + 4):
                            last = nc.tensor.transpose(
                                K.ps[:, 4 + b, 120 * (g % 4):120 * (g % 4) + 120],
                                E[1 - par][0:120, 2 * g:2 * g + 2, :].rearrange("p h t -> p (h t)"),
                                K.ident[0:120, 0:120])
                        last.then_inc(tr_done, 1)
                    for u in range(2):
                        pe.wait_ge(proj_copied, 16)
                        pe.wait_ge(tr_copied, 2 * p)
                        pe.wait_ge(v_copied, 2 * p)
                        wait_from_second(pe, o_copied, p, 2 * p - 3 + u)
                        for h in range(H):
                            j, c, r = h % 4, h // 4, 64 * (h % 2)
                            last = nc.tensor.matmul(K.ps[32 * j:32 * j + 32, (7, 3)[u], SQ * c:SQ * c + SQ],
                                                    VS[r:r + SQ, u, 32 * h:32 * h + 32],
                                                    AT[r:r + SQ, h // 2, 64 * u:64 * u + SQ],
                                                    start=True, stop=True, skip_group_check=True)
                        last.then_inc(o_done, 1)
            pairs(pe, emit)

        @block.vector
        def _(dve):
            def slices(p):
                for u in range(2):
                    nc.vector.tensor_copy(QS[:, :, 64 * u:64 * u + 64],
                                          qT[:, :, bass.ds(TP * p + SQ * u, 64)])
                for j in range(4):
                    last = nc.vector.tensor_copy(
                        KS[32 * j:32 * j + 32, :, :, SQ * j:SQ * j + SQ],
                        kT[32 * j:32 * j + 32, :, bass.ds(TP * p, TP)].rearrange("p c (u t) -> p c u t", u=2))
                last.then_inc(q_sliced, 1)

            def emit(p, par, lag, cur):
                if lag:
                    wait_from_second(dve, v_done, p, 2 * p - 2)
                    for r in (0, 64):
                        last = nc.vector.tensor_copy(
                            YS[:, :, r:r + SQ], yT[:, bass.ds(TP * (p - 1), TP)].rearrange("p (u t) -> p u t", u=2))
                    last.then_inc(y_sliced, 1)
                if lag:
                    before = E[1 - par][0:120, :, 0:SQ]
                    dve.wait_ge(rec_done, p)
                    dve.wait_ge(mask_done, p)
                    nc.vector.tensor_tensor(before, before, SM[0:120, :].unsqueeze(2).broadcast_to([120, H, SQ]),
                                            ALU.mult).then_inc(norm_done, 1)
                if cur:
                    dve.wait_ge(sc_done, p + 1)
                    sc = K.ps[0:120, 0:2, 0:8 * SQ].rearrange("p b (h t) -> p b h t", h=8)
                    mx = MX[0:120, :].rearrange("p (b h) -> p b h", b=2)
                    nc.vector.tensor_reduce(mx, sc, axis=AX.X, op=ALU.max).then_inc(mx_done, 1)
                    dve.wait_ge(mx_done, p + 1)
                    wait_from_second(dve, tr_done, p, 2 * p - 2)
                    nc.vector.tensor_tensor(E[par][0:120, :, 0:SQ].rearrange("p (b h) t -> p b h t", b=2), sc,
                                            mx.unsqueeze(3).broadcast_to([120, 2, 8, SQ]),
                                            ALU.subtract).then_inc(sub_done, 1)
                    if not isinstance(p, int) or p + 1 < NT:
                        slices(p + 1)
                if cur:
                    dve.wait_ge(ex_done, p + 1)
                    if lag:
                        dve.wait_ge(norm_done, p)
                    nc.vector.tensor_reduce(SM[0:120, :], E[par][0:120, :, 0:SQ], axis=AX.X,
                                            op=ALU.add).then_inc(sum_done, 1)
                    dve.wait_ge(sum_done, p + 1)
                    nc.vector.reciprocal(SM[0:120, :], SM[0:120, :]).then_inc(rec_done, 1)

            slices(0)
            pairs(dve, emit)

        @block.scalar
        def _(act):
            def emit(p, par, lag, cur):
                if lag:
                    wait_from_second(act, o_done, p, 2 * p - 2)
                    for u in range(2):
                        act.wait_ge(v_done, 2 * p - 1 + u)
                        nc.scalar.copy(VS[0:120, u, :], K.ps[0:120, (6, 2)[u], 0:512]).then_inc(v_copied, 1)
                if cur:
                    act.wait_ge(sub_done, p + 1)
                    nc.scalar.activation(E[par][0:120, :, 0:SQ], E[par][0:120, :, 0:SQ], ACT.Exp,
                                         scale=scale).then_inc(ex_done, 1)
                if lag:
                    for b in range(2):
                        act.wait_ge(tr_done, 2 * p - 1 + b)
                        last = nc.scalar.copy(AT[:, 4 * b:4 * b + 4, :],
                                              K.ps[:, 4 + b, 0:480].rearrange("p (g s) -> p g s", g=4))
                        last.then_inc(tr_copied, 1)
                    for u in range(2):
                        act.wait_ge(o_done, 2 * p - 1 + u)
                        nc.scalar.copy(oT[:, :, bass.ds(TP * (p - 1) + SQ * u, SQ)],
                                       K.ps[:, (7, 3)[u], 0:4 * SQ].rearrange("p (c s) -> p c s", c=4)).then_inc(o_copied, 1)
            pairs(act, emit)


def normalise_attention(nc, K, name, Zall, oT, sel, vbias, zt, rzt, prefetch=None):
    nchunk = oT.shape[1]
    RH, RL = K.YH[0:16, 0, 0:NTOK], K.YH[0:16, 1, 0:NTOK]
    SEL = K.YL[0:16, 0, 0:128 * nchunk].rearrange("p (c f) -> p c f", c=nchunk)
    sel_done, k0 = K.shared("nrm_sel", 1)
    rh_done, _ = K.shared("nrm_rh", 1)
    rl_done, _ = K.shared("nrm_rl", 1)
    rec_done, _ = K.shared("nrm_rec", 1)
    zt_done, _ = K.shared("nrm_zt", 1)
    zt_copied, _ = K.shared("nrm_ztc", 1)
    z_stored, z0 = K.shared("nrm_zst", 16)
    z_loaded, _ = K.shared("nrm_zld", 16)
    bc_done, bc0 = K.shared("nrm_bc", 2 * nchunk)
    bc_used, _ = K.shared("nrm_bcu", 2 * nchunk)
    with nc.Block() as block:
        @block.sync
        def _(sp):
            if prefetch is not None:
                prefetch(sp)

        @block.scalar
        def _(act):
            act.wait_ge(zt_copied, k0 + 1)
            act.dma_start(K.z_dram, zt[0:112, :]).then_inc(z_stored, 16)
            act.wait_ge(z_stored, z0 + 16)
            act.dma_start(rzt[0:16, :, :], K.z_dram.rearrange("k p -> (k p)").rearrange(
                "(b h s) -> h b s", b=NB, h=16)).then_inc(z_loaded, 16)
            act.wait_ge(z_loaded, z0 + 16)

        @block.tensor
        def _(pe):
            pe.wait_ge(rec_done, k0 + 1)
            nc.tensor.transpose(K.ps[0:112, 0, 0:128], Zall[:, :], K.ident[:, :]).then_inc(zt_done, 1)
            pe.wait_ge(sel_done, k0 + 1)
            pe.wait_ge(rl_done, k0 + 1)
            for k in range(2 * nchunk):
                c, half = k // 2, k % 2
                if k >= 2:
                    pe.wait_ge(bc_used, bc0 + k - 1)
                nc.tensor.matmul(K.ps[:, 1 + k % 2, 0:448], SEL[:, c, :],
                                 RH[:, 448 * half:448 * half + 448], start=True, stop=False)
                nc.tensor.matmul(K.ps[:, 1 + k % 2, 0:448], SEL[:, c, :],
                                 RL[:, 448 * half:448 * half + 448], start=False, stop=True).then_inc(bc_done, 1)

        @block.vector
        def _(dve):
            nc.vector.reciprocal(Zall[:, :], Zall[:, :]).then_inc(rec_done, 1)
            dve.wait_ge(zt_done, k0 + 1)
            nc.vector.tensor_copy(zt[0:112, :], K.ps[0:112, 0, 0:128]).then_inc(zt_copied, 1)
            nc.vector.tensor_copy(SEL, sel[0:16, 0:nchunk, :]).then_inc(sel_done, 1)
            dve.wait_ge(z_loaded, z0 + 16)
            rz = rzt[0:16, :, :].rearrange("h b s -> h (b s)")
            nc.vector.tensor_copy(RH, rz).then_inc(rh_done, 1)
            dve.wait_ge(rh_done, k0 + 1)
            nc.vector.tensor_tensor(RL, rz, RH.bitcast(F32), ALU.subtract).then_inc(rl_done, 1)
            for k in range(2 * nchunk):
                c, half = k // 2, k % 2
                cols = slice(448 * half, 448 * half + 448)
                dve.wait_ge(bc_done, bc0 + k + 1)
                nc.vector.tensor_tensor(oT[:, c, cols], oT[:, c, cols], K.ps[:, 1 + k % 2, 0:448],
                                        ALU.mult).then_inc(bc_used, 1)
                if vbias is not None:
                    dve.wait_ge(bc_used, bc0 + k + 1)
                    nc.vector.tensor_scalar(oT[:, c, cols], oT[:, c, cols], vbias, None, ALU.add)


def project_and_add(nc, K, name, dst, terms, bias, srcT, W):
    nchunk = srcT.shape[1]
    base_done, base0 = K.shared("proj_base", len(terms))
    mm_done, mm0 = K.shared("proj_mm", 2)
    with nc.Block() as block:
        @block.gpsimd
        def _(pool):
            o = Chain(pool, base_done, base0)
            o.then(nc.gpsimd.tensor_tensor(dst[0:TP, :, :], terms[0][0:TP, :, :], over_tiles(bias), ALU.add))
            for t in terms[1:]:
                o.then(nc.gpsimd.tensor_tensor(dst[0:TP, :, :], dst[0:TP, :, :], t[0:TP, :, :], ALU.add))

        @block.tensor
        def _(pe):
            for n in range(NT):
                for c in range(nchunk):
                    last = nc.tensor.matmul(K.ps[0:TP, n // 4, 128 * (n % 4):128 * (n % 4) + 128],
                                            srcT[:, c, TP * n:TP * n + TP], W[:, c, :],
                                            start=c == 0, stop=c == nchunk - 1, skip_group_check=True)
                if n % 4 == 3:
                    last.then_inc(mm_done, 1)

        @block.vector
        def _(dve):
            dve.wait_ge(base_done, base0 + len(terms))
            for half in range(2):
                dve.wait_ge(mm_done, mm0 + half + 1)
                nc.vector.tensor_tensor(dst[0:TP, 4 * half:4 * half + 4, :], dst[0:TP, 4 * half:4 * half + 4, :],
                                        K.ps[0:TP, half, :].rearrange("p (n c) -> p n c", n=4), ALU.add)


def hidden_layer(nc, K, name, xT, W, bias, hT):
    h_done, h0 = K.shared("hidden_h", 2 * NF)
    with nc.Block() as block:
        @block.tensor
        def _(pe):
            for k in range(2 * NF):
                f, half = k % NF, k // NF
                nc.tensor.matmul(K.ps[:, k, 0:448], W[:, 128 * f:128 * f + 128],
                                 xT[:, 448 * half:448 * half + 448], start=True, stop=True).then_inc(h_done, 1)

        @block.scalar
        def _(act):
            for k in range(2 * NF):
                f, half = k % NF, k // NF
                act.wait_ge(h_done, h0 + k + 1)
                nc.scalar.activation(hT[:, f, 448 * half:448 * half + 448], K.ps[:, k, 0:448], ACT.Gelu,
                                     bias=bias[:, f:f + 1])


class ExpertLoader:

    def __init__(self, nc, W1_dram, W2_dram, Wb1, Wb2, w1_loaded, w2_loaded):
        self.W1, self.W2, self.Wb1, self.Wb2 = W1_dram, W2_dram, Wb1, Wb2
        self.w1_loaded, self.w2_loaded = w1_loaded, w2_loaded

    def first(self, sp, e, u):
        sp.dma_start(self.Wb1[:, u, :], self.W1[bass.ds(e, 1), :, :].rearrange("e c h -> (e c) h")
                     ).then_inc(self.w1_loaded[u], 16)

    def second(self, sp, e, u):
        sp.dma_start(self.Wb2[:, u, :, :], self.W2[bass.ds(e, 1), :, :].rearrange("e (f p) d -> (e p) f d", p=128)
                     ).then_inc(self.w2_loaded[u], 16)


def mixture(nc, K, name, X, xT, gate_w, gate_b, top, b1c, b2, load, Wb1, Wb2, hT, bufs):
    G, G2, EQ, SMALL, CW, CWT = bufs
    lg_done, k0 = K.shared("gate_lg", 1)
    sub_done, _ = K.shared("gate_sub", 1)
    ex_done, _ = K.shared("gate_ex", 1)
    cw_done, _ = K.shared("gate_cw", 1)
    cwt_done, _ = K.shared("gate_cwt", 1)
    cwt_copied, _ = K.shared("gate_cwtc", 1)
    b2_done, _ = K.shared("gate_b2", 1)
    xh_done, _ = K.shared("gate_xh", 1)
    XH, XL = K.YH[:, 0, 0:NTOK], K.YH[:, 1, 0:NTOK]
    W1H = K.YL[:, 0, 0:2 * HID].rearrange("p (u h) -> p u h", u=2)
    W1L = K.YL[:, 1, 0:2 * HID].rearrange("p (u h) -> p u h", u=2)
    with nc.Block() as block:
        @block.tensor
        def _(pe):
            for n in range(NT):
                last = nc.tensor.matmul(K.ps[0:TP, 0, NE * n:NE * n + NE], xT[:, TP * n:TP * n + TP], gate_w,
                                        start=True, stop=True, skip_group_check=True)
            last.then_inc(lg_done, 1)
            pe.wait_ge(cw_done, k0 + 1)
            for n in range(NT):
                last = nc.tensor.transpose(K.ps[0:NE, 1 + n // 4, TP * (n % 4):TP * (n % 4) + TP],
                                           CW[0:TP, n, :], K.ident[0:TP, 0:TP])
            last.then_inc(cwt_done, 1)
            pe.wait_ge(cwt_copied, k0 + 1)
            for n in range(NT):
                last = nc.tensor.matmul(K.ps[0:TP, 3 + n // 4, 128 * (n % 4):128 * (n % 4) + 128],
                                        CWT[0:NE, TP * n:TP * n + TP], b2, start=True, stop=True,
                                        skip_group_check=True)
            last.then_inc(b2_done, 1)

        @block.scalar
        def _(act):
            act.wait_ge(sub_done, k0 + 1)
            nc.scalar.activation(G[0:TP, :, :], G[0:TP, :, :], ACT.Exp).then_inc(ex_done, 1)

        @block.vector
        def _(dve):
            o = K.chain(dve, "gate_chain")
            g, g2, eq, cw = (t[0:TP, :, :] for t in (G, G2, EQ, CW))

            def bc(col):
                return SMALL[0:TP, col, :].unsqueeze(2).broadcast_to([TP, NT, NE])

            def first_largest(src, dst, col):
                o.then(nc.vector.tensor_reduce(SMALL[0:TP, col, :], src, axis=AX.X, op=ALU.max))
                o.then(nc.vector.tensor_tensor(dst, src, bc(col), ALU.is_ge))
                o.then(nc.vector.tensor_tensor(dst, dst, K.expert_m8[0:TP, :, :], ALU.mult))
                o.then(nc.vector.tensor_reduce(SMALL[0:TP, col, :], dst, axis=AX.X, op=ALU.min))
                o.then(nc.vector.tensor_tensor(dst, K.expert_m8[0:TP, :, :], bc(col), ALU.is_equal))

            nc.vector.tensor_copy(XH, xT[:, :]).then_inc(xh_done, 1)
            dve.wait_ge(xh_done, k0 + 1)
            nc.vector.tensor_tensor(XL, xT[:, :], XH.bitcast(F32), ALU.subtract)
            dve.wait_ge(lg_done, k0 + 1)
            lg = K.ps[0:TP, 0, 0:NT * NE].rearrange("p (n e) -> p n e", e=NE)
            if gate_b is None:
                o.then(nc.vector.tensor_copy(g, lg))
            else:
                o.then(nc.vector.tensor_tensor(g, lg, over_tiles(gate_b), ALU.add))
            o.then(nc.vector.tensor_reduce(SMALL[0:TP, 0, :], g, axis=AX.X, op=ALU.max))
            nc.vector.tensor_tensor(g, g, bc(0), ALU.subtract).then_inc(sub_done, 1)
            dve.wait_ge(ex_done, k0 + 1)
            o.then(nc.vector.tensor_reduce(SMALL[0:TP, 1, :], g, axis=AX.X, op=ALU.add))
            o.then(nc.vector.reciprocal(SMALL[0:TP, 1, :], SMALL[0:TP, 1, :]))
            o.then(nc.vector.tensor_tensor(g, g, bc(1), ALU.mult))
            first_largest(g, eq, 2)
            if top == 1:
                nc.vector.tensor_copy(cw, eq).then_inc(cw_done, 1)
            else:
                o.then(nc.vector.scalar_tensor_tensor(g2, eq, -2.0, g, ALU.mult, ALU.add))
                first_largest(g2, cw, 3)
                o.then(nc.vector.tensor_tensor(cw, cw, eq, ALU.add))
                nc.vector.tensor_tensor(cw, cw, g, ALU.mult).then_inc(cw_done, 1)
            dve.wait_ge(cwt_done, k0 + 1)
            for half in range(2):
                last = nc.vector.tensor_copy(CWT[0:NE, 448 * half:448 * half + 448], K.ps[0:NE, 1 + half, 0:448])
            last.then_inc(cwt_copied, 1)
            dve.wait_ge(b2_done, k0 + 1)
            for half in range(2):
                nc.vector.tensor_tensor(X[0:TP, 4 * half:4 * half + 4, :], X[0:TP, 4 * half:4 * half + 4, :],
                                        K.ps[0:TP, 3 + half, :].rearrange("p (n c) -> p n c", n=4), ALU.add)

    h_done, g_done = K.sem(f"{name}_h"), K.sem(f"{name}_g")
    out_done, acc_done = K.sem(f"{name}_out"), K.sem(f"{name}_acc")
    col_done = K.sem(f"{name}_col")
    wh_done = K.sem(f"{name}_wh")
    split_done = K.sem(f"{name}_split")
    B1S, CWS = K.b1s, K.cws
    UNITS = 4

    with nc.Block() as block:
        @block.sync
        def _(sp):
            with sp.Fori(0, NE // 2 - 1) as t:
                for u in range(2):
                    sp.wait_ge(split_done, 2 * t + u + 1)
                    load.first(sp, 2 * t + 2 + u, u)
                for u in range(2):
                    sp.wait_ge(out_done, 4 * t + 2 * u + 2)
                    load.second(sp, 2 * t + 2 + u, u)

        @block.tensor
        def _(pe):
            def hidden(t, v):
                u, half = divmod(v, 2)
                if half == 0:
                    pe.wait_ge(split_done, 2 * t + u + 1)
                for f in range(NF):
                    if not (isinstance(t, int) and v == 0):
                        pe.wait_ge(g_done, 16 * t + 4 * v + f - 3)
                    for k, (w, x) in enumerate(((W1H, XH), (W1H, XL), (W1L, XH))):
                        last = nc.tensor.matmul(K.ps[:, f, 0:448], w[:, u, 128 * f:128 * f + 128],
                                                x[:, 448 * half:448 * half + 448], start=k == 0, stop=k == 2)
                    last.then_inc(h_done, 1)

            def output(t, v):
                u, half = divmod(v, 2)
                pe.wait_ge(g_done, 16 * t + 4 * v + 4)
                if half == 0:
                    pe.wait_ge(load.w2_loaded[u], 16 * t + 16)
                if not (isinstance(t, int) and v < 2):
                    pe.wait_ge(acc_done, 4 * t + v - 1)
                for i in range(4):
                    for f in range(NF):
                        last = nc.tensor.matmul(K.ps[0:TP, 4 + v % 2, 128 * i:128 * i + 128],
                                                hT[:, v % 2, f, TP * i:TP * i + TP], Wb2[:, u, f, :],
                                                start=f == 0, stop=f == NF - 1, skip_group_check=True)
                last.then_inc(out_done, 1)

            def turn(t):
                hidden(t, 0)
                for v in range(1, UNITS):
                    hidden(t, v)
                    output(t, v - 1)
                output(t, UNITS - 1)
            turn(0)
            with pe.Fori(1, NE // 2) as t:
                turn(t)

        @block.scalar
        def _(act):
            def turn(t):
                for v in range(UNITS):
                    u = v // 2
                    if v % 2 == 0:
                        act.wait_ge(col_done, 4 * t + 2 * u + 2)
                    if not (isinstance(t, int) and v < 2):
                        act.wait_ge(out_done, 4 * t + v - 1)
                    for f in range(NF):
                        act.wait_ge(h_done, 16 * t + 4 * v + f + 1)
                        nc.scalar.activation(hT[:, v % 2, f, :], K.ps[:, f, 0:448], ACT.Gelu,
                                             bias=B1S[:, u, f:f + 1]).then_inc(g_done, 1)
            turn(0)
            with act.Fori(1, NE // 2) as t:
                turn(t)

        @block.vector
        def _(dve):
            def columns(t, u):
                if not isinstance(t, int) or t > 0:
                    dve.wait_ge(g_done, 16 * t + 8 * u - 8)
                    dve.wait_ge(acc_done, 4 * t + 2 * u - 2)
                nc.vector.tensor_copy(B1S[:, u, :], b1c[:, bass.ds(8 * t + 4 * u, 4)]).then_inc(col_done, 1)
                nc.vector.tensor_copy(CWS[0:TP, u, :], CW[0:TP, :, bass.ds(2 * t + u, 1)].rearrange(
                    "p n e -> p (n e)")).then_inc(col_done, 1)
                dve.wait_ge(load.w1_loaded[u], 16 * t + 16)
                nc.vector.tensor_copy(W1H[:, u, :], Wb1[:, u, :]).then_inc(wh_done, 1)
                dve.wait_ge(wh_done, 2 * t + u + 1)
                nc.vector.tensor_tensor(W1L[:, u, :], Wb1[:, u, :], W1H[:, u, :].bitcast(F32),
                                        ALU.subtract).then_inc(split_done, 1)

            def turn(t, last_turn=False):
                for v in range(UNITS):
                    u, half = divmod(v, 2)
                    if v == 0:
                        columns(t, 1)
                    if v == 3 and not last_turn:
                        columns(t + 1, 0)
                    dve.wait_ge(out_done, 4 * t + v + 1)
                    if v % 2 == 0:
                        dve.wait_ge(col_done, 4 * t + 2 * u + 2)
                    if not (isinstance(t, int) and v < 2):
                        dve.wait_ge(acc_done, 4 * t + v - 1)
                    for i in range(4):
                        n = 4 * half + i
                        last = nc.vector.scalar_tensor_tensor(
                            X[0:TP, n, :], K.ps[0:TP, 4 + v % 2, 128 * i:128 * i + 128],
                            CWS[0:TP, u, n:n + 1], X[0:TP, n, :], ALU.mult, ALU.add)
                    last.then_inc(acc_done, 1)
            columns(0, 0)
            turn(0)
            with dve.Fori(1, NE // 2 - 1) as t:
                turn(t)
            turn(NE // 2 - 1, True)
BLOCKS = 7
STEPS = 2 * BLOCKS
GROUPS = 3
GT = 4
TT = 125
NTT = 12
GC = GT * TT
HALF = 448
BANK_V = 7
Q_STEPS = (4, 5, 7, 11)
O_STEP = 6


def score_bank(m, g):
    return 2 if g == 2 else (m % 2) * 3 + g


def t_bank(slot):
    return 5 + slot % 2


def misc_at(m, lag, nxt):
    if m in (1, 2, 3):
        return ("y", 0, m - 1)
    if m in (8, 9, 10) and nxt:
        return ("y", 1, m - 8)
    if m in Q_STEPS and nxt:
        return ("q", 0, Q_STEPS.index(m))
    if m == O_STEP and lag:
        return ("o", 0, 0)
    return None


def cross_attention(nc, K, name, ctx_dram, xT, M, qbias, scale, wv, oT, Zall, with_ln,
                    g_bc=None, b_bc=None):
    nchunk = oT.shape[1]
    ps, ident = K.ps, K.ident
    PT, P, YH, YL, YF, yt, yv, yraw = K.PT, K.P, K.YH, K.YL, K.YF, K.yt, K.yv, K.yraw
    QF, Q, U, NM, MP, ZP = K.QF, K.Q, K.U, K.NM, K.MP, K.ZP
    LNS = K.LNS

    def sem(s):
        return K.sem(f"{name}_{s}")

    y_loaded = [sem("y_loaded0"), sem("y_loaded1")]
    y_sum1, y_cent, y_sq, y_sum2 = sem("y_sum1"), sem("y_cent"), sem("y_sq"), sem("y_sum2")
    yn_done = sem("yn_done")
    yv_done = sem("yv_done")
    yT_done, yT_copied = sem("yT_done"), sem("yT_copied")
    yh_done, yl_done = sem("yh_done"), sem("yl_done")
    q_done, q_copied = sem("q_done"), sem("q_copied")
    qh_done, ql_done = sem("qh_done"), sem("ql_done")
    sc_done = sem("sc_done")
    mxp_done, mx_done = sem("mxp_done"), sem("mx_done")
    ex_shared, ex_done = sem("ex_shared"), sem("ex_done")
    tr_done = sem("tr_done")
    cp = [sem(f"cp{g}") for g in range(GROUPS)]
    pv_done, u_done = sem("pv_done"), sem("u_done")
    o_done, o_copied = sem("o_done"), sem("o_copied")
    z_done = sem("z_done")
    pool_step = sem("pool_step")

    def for_pairs(eng, emit):
        emit(0, False, True, True)
        with eng.Fori(1, 7) as p:
            emit(p, True, True, True)
        emit(7, True, True, False)
        emit(8, True, False, False)

    def pe_free_t_bank(pe, p, m, g, misc, lag, cur, nxt):
        slot = 3 * m + g
        if misc:
            pm, pg = divmod(slot - 1, 3)
            blk = 14 * p + pm - 2
            if pm - 2 >= 0 or lag:
                pe.wait_ge(cp[pg], blk + 1)
            return
        before = misc_at(m - 1, lag, nxt) if g == 0 and m > 0 and cur else None
        if g == 0 and m > 0 and not cur:
            before = None
        if before:
            kind, par, k = before
            if kind == "y":
                pe.wait_ge(yT_copied, 6 * p + 3 * (par + 1) + k + 1)
            elif kind == "q":
                pe.wait_ge(q_copied, 4 * p + 4 + k + 1)
            else:
                pe.wait_ge(o_copied, p)
            return
        pm, pg = divmod(slot - 2, 3)
        if pm - 2 >= 0 or lag:
            pe.wait_ge(cp[pg], 14 * p + pm - 2 + 1)

    def pe_y_transposes(beta, par, g, bank):
        for j in range(GT):
            last = nc.tensor.transpose(ps[:, bank, TT * j:TT * j + TT], yt[:, par, GT * g + j, :],
                                       ident[0:TT, 0:TT])
        last.then_inc(yT_done, 1)

    def pe_q(p_next, k, bank):
        for h in range(4):
            last = nc.tensor.matmul(ps[:, bank, 112 * h:112 * h + 112], M[:, 4 * k + h, :],
                                    xT[:, bass.ds(112 * p_next, 112)], start=True, stop=True)
        last.then_inc(q_done, 1)

    def pe_o(bank):
        for h in range(16):
            if nchunk == 4:
                j, c, first, final = h % 4, h // 4, True, True
            else:
                j, c, first, final = h // 4, 0, h % 4 == 0, h % 4 == 3
            last = nc.tensor.matmul(ps[32 * j:32 * j + 32, bank, 112 * c:112 * c + 112],
                                    wv[:, h, :], U[:, h, :], start=first, stop=final,
                                    skip_group_check=True)
        last.then_inc(o_done, 1)

    def pe_sums(pe, beta, par, w, g):
        if g == 0 or not 6 <= w <= 11:
            return
        half, k = divmod(w - 6, 3)
        first_pair = k == 0 and g == 1
        if first_pair:
            for gg in range(GROUPS):
                pe.wait_ge(cp[gg], 7 * beta + (4 if half == 0 else 7))
            if half == 0:
                pe.wait_ge(yv_done, beta + 1)
        if first_pair and not (isinstance(beta, int) and beta == 0 and half == 0):
            pe.wait_ge(u_done, 2 * beta + half)
        for j in (4 * k + 2 * (g - 1), 4 * k + 2 * (g - 1) + 1):
            rows = slice(64 * (j % 2), 64 * (j % 2) + 64)
            last = nc.tensor.matmul(ps[rows, BANK_V, 0:HALF], yv[:, par, j, :],
                                    PT[0:TT, par, j, HALF * half:HALF * half + HALF],
                                    start=j < 2, stop=j >= NTT - 2, skip_group_check=True)
        if k == 2 and g == 2:
            last.then_inc(pv_done, 1)

    def pe_pair(pe):
        def emit(p, lag, cur, nxt):
            for m in range(STEPS if cur else BLOCKS):
                par, i = divmod(m, BLOCKS)
                n = 14 * p + m
                for g in range(GROUPS):
                    slot = 3 * m + g
                    if (lag and m < 2) or (cur and m >= 2):
                        pe_free_t_bank(pe, p, m, g, False, lag, cur, nxt)
                        if g == 0:
                            pe.wait_ge(ex_done, n - 1)
                        for j in range(GT):
                            last = nc.tensor.transpose(
                                ps[0:TT, t_bank(slot), 128 * j:128 * j + 128],
                                P[:, m % 2, GC * g + TT * j:GC * g + TT * j + TT], ident[:, :])
                        last.then_inc(tr_done, 1)
                    if g == 2:
                        misc = misc_at(m, lag, nxt)
                        if misc and (cur or misc[0] == "o"):
                            kind, mp, k = misc
                            bank = t_bank(3 * m + 3)
                            pe_free_t_bank(pe, p, m, 2, True, lag, cur, nxt) if cur else pe.wait_ge(cp[2], 112)
                            if kind == "y":
                                beta = 2 * p + 1 + mp
                                if with_ln:
                                    pe.wait_ge(yn_done, beta + 1)
                                else:
                                    pe.wait_ge(y_loaded[(1 + mp) % 2], 16 * (beta - (1 + mp) % 2) + 32)
                                pe_y_transposes(beta, (1 + mp) % 2, k, bank)
                            elif kind == "q":
                                pe_q(p + 1, k, bank)
                            else:
                                pe.wait_ge(u_done, 4 * p)
                                pe_o(bank)
                    if cur:
                        if i == 0 and g == 0:
                            pe.wait_ge(ql_done, 2 * p + par + 1)
                            pe.wait_ge(yl_done, 2 * p + par + 1)
                        if g == 0 and (lag or m >= 2):
                            pe.wait_ge(ex_done, n - 1)
                        if g == 2 and (lag or m >= 1):
                            pe.wait_ge(ex_shared, n)
                        bank = score_bank(m, g)
                        rows = Q[:, par, 128 * i:128 * i + 128]
                        nc.tensor.matmul(ps[:, bank, 0:GC], rows, YH[:, par, GC * g:GC * g + GC],
                                         start=True, stop=False)
                        nc.tensor.matmul(ps[:, bank, 0:GC], rows, YL[:, par, GC * g:GC * g + GC],
                                         start=False, stop=True).then_inc(sc_done, 1)
                    if cur:
                        if 6 <= m <= 11:
                            pe_sums(pe, 2 * p, 0, m, g)
                        if m == 13:
                            pe_sums(pe, 2 * p + 1, 1, 6, g)
                    if lag and m <= 4:
                        pe_sums(pe, 2 * p - 1, 1, m + 7, g)
        return emit

    def copy_group(eng, copy, p, m, g, lag):
        slot = 3 * m + g
        n2 = 14 * p + m - 2
        par, i = divmod((m - 2) % STEPS, BLOCKS)
        eng.wait_ge(tr_done, 3 * n2 + g + 1)
        old = not (isinstance(p, int) and 2 * p + (m - 2) // BLOCKS < 2)
        if old:
            beta = 2 * p + (m - 2) // BLOCKS
            eng.wait_ge(pv_done, 2 * beta - 3 + (i >= 3))
        copy(PT[0:TT, par, GT * g:GT * g + GT, 128 * i:128 * i + 128],
             ps[0:TT, t_bank(slot), :].rearrange("p (j c) -> p j c", j=GT)).then_inc(cp[g], 1)

    def act_pair(act):
        def emit(p, lag, cur, nxt):
            for m in range(STEPS if cur else BLOCKS):
                n = 14 * p + m
                t_here = (lag and m < 2) or (cur and m >= 2)
                if t_here:
                    copy_group(act, nc.scalar.copy, p, m, 0, lag)
                if (cur and m >= 1) or (lag and m == 0):
                    pm = (m - 1) % STEPS
                    act.wait_ge(mx_done, n)
                    if lag or m >= 3:
                        act.wait_ge(tr_done, 3 * n - 6)
                    if pm % BLOCKS == 0 and lag:
                        act.wait_ge(z_done, 2 * p + pm // BLOCKS - 1)
                    nc.scalar.activation(P[:, pm % 2, 2 * GC:3 * GC], ps[:, 2, 0:GC], ACT.Exp,
                                         bias=NM[:, pm:pm + 1], scale=scale,
                                         accum_out=ZP[:, pm, 0:1]).then_inc(ex_shared, 1)
                    b = (pm % 2) * 3
                    nc.scalar.activation(P[:, pm % 2, 0:2 * GC].rearrange("p (a b) -> p a b", a=2),
                                         ps[:, b:b + 2, 0:GC], ACT.Exp, bias=NM[:, pm:pm + 1],
                                         scale=scale, accum_out=ZP[:, pm, 1:2]).then_inc(ex_done, 1)
                if t_here:
                    copy_group(act, nc.scalar.copy, p, m, 2, lag)
                misc = misc_at(m, lag, nxt)
                if misc and (cur or misc[0] == "o"):
                    kind, mp, k = misc
                    bank = t_bank(3 * m + 3)
                    if kind == "y":
                        act_y_copy(act, 2 * p + 1 + mp, k, bank, False)
                    elif kind == "q" and qbias is None:
                        act_q_copy(act, p + 1, k, bank, False)
                    elif kind == "o":
                        act.wait_ge(o_done, p)
                        nc.scalar.copy(oT[:, :, bass.ds(112 * (p - 1), 112)],
                                       ps[:, bank, 0:112 * nchunk].rearrange("p (c t) -> p c t", c=nchunk)
                                       ).then_inc(o_copied, 1)
                for beta, par, w, live in ((2 * p, 0, m, cur), (2 * p - 1, 1, m + 7, lag)):
                    if live and w in (8, 11):
                        half = 0 if w == 8 else 1
                        act.wait_ge(pv_done, 2 * beta + half + 1)
                        nc.scalar.copy(U[:, 8 * half:8 * half + 8, 56 * par:56 * par + 56],
                                       ps[:, BANK_V, 0:HALF].rearrange("p (h s) -> p h s", h=8)
                                       ).then_inc(u_done, 1)
        return emit

    def act_y_copy(act, beta, k, bank, first):
        act.wait_ge(yT_done, 3 * beta + k + 1)
        if not first:
            act.wait_ge(yl_done, beta)
        nc.scalar.copy(YF[:, GC * k:GC * k + GC], ps[:, bank, 0:GC]).then_inc(yT_copied, 1)

    def act_q_copy(act, p, k, bank, first):
        act.wait_ge(q_done, 4 * p + k + 1)
        if not first:
            act.wait_ge(ql_done, 2 * p)
        nc.scalar.copy(QF[:, 4 * k:4 * k + 4, :],
                       ps[:, bank, 0:448].rearrange("p (h t) -> p h t", h=4)).then_inc(q_copied, 1)

    def dve_q_copy(dve, p, k, bank, first):
        dve.wait_ge(q_done, 4 * p + k + 1)
        if not first:
            dve.wait_ge(ql_done, 2 * p)
        nc.vector.tensor_tensor(QF[:, 4 * k:4 * k + 4, :],
                                ps[:, bank, 0:448].rearrange("p (h t) -> p h t", h=4),
                                qbias[:, 4 * k:4 * k + 4].unsqueeze(2).broadcast_to([128, 4, 112]),
                                ALU.add).then_inc(q_copied, 1)

    def dve_q_high(dve, p, par, old):
        dve.wait_ge(q_copied, 4 * p + 4)
        if old:
            dve.wait_ge(sc_done, 42 * p + 21 * par - 21)
        nc.vector.tensor_copy(Q[:, par, :].rearrange("p (h s) -> p h s", h=16),
                              QF[:, :, 56 * par:56 * par + 56]).then_inc(qh_done, 1)

    def dve_y_high(dve, beta, par, old):
        dve.wait_ge(yT_copied, 3 * beta + 3)
        if old:
            dve.wait_ge(sc_done, 21 * (beta - 1))
        nc.vector.tensor_copy(YH[:, par, :], YF[:, :]).then_inc(yh_done, 1)

    def dve_y_sum1(dve, beta, par):
        dve.wait_ge(y_loaded[par], 8 * (beta - par) + 16)
        if not (isinstance(beta, int) and beta < 2):
            dve.wait_ge(yn_done, beta - 1)
        nc.vector.tensor_reduce(LNS[0:TT, par, 0, :], yraw[:, par, :, :], axis=AX.X,
                                op=ALU.add).then_inc(y_sum1, 1)

    def dve_y_sum2(dve, beta, par):
        dve.wait_ge(y_sq, beta + 1)
        nc.vector.tensor_reduce(LNS[0:TT, par, 1, :], yt[:, par, :, 0:64], axis=AX.X,
                                op=ALU.add).then_inc(y_sum2, 1)

    def dve_pair(dve):
        def emit(p, lag, cur, nxt):
            for m in range(STEPS if cur else BLOCKS):
                par, i = divmod(m, BLOCKS)
                n = 14 * p + m
                if cur and m == 0:
                    dve_q_high(dve, p, 1, lag)
                if nxt and m == 12:
                    dve_q_high(dve, p + 1, 0, True)
                if cur and m == 4:
                    dve_y_high(dve, 2 * p + 1, 1, lag)
                if nxt and m == 11:
                    dve_y_high(dve, 2 * p + 2, 0, True)
                if with_ln and nxt and i == 1:
                    dve_y_sum1(dve, 2 * p + par + 2, par)
                if with_ln and nxt and i == 3:
                    dve_y_sum2(dve, 2 * p + par + 2, par)
                if (lag and m < 2) or (cur and m >= 2):
                    copy_group(dve, nc.vector.tensor_copy, p, m, 1, lag)
                if cur:
                    b = (m % 2) * 3
                    dve.wait_ge(sc_done, 3 * n + 2)
                    nc.vector.tensor_reduce(MP[:, m, 0:1], ps[:, b:b + 2, 0:GC], axis=AX.XY, op=ALU.max)
                    dve.wait_ge(sc_done, 3 * n + 3)
                    nc.vector.tensor_reduce(MP[:, m, 1:2], ps[:, 2, 0:GC], axis=AX.X,
                                            op=ALU.max).then_inc(mxp_done, 1)
                    dve.wait_ge(mxp_done, n + 1)
                    nc.vector.tensor_scalar(NM[:, m:m + 1], MP[:, m, 0:1], MP[:, m, 1:2], -scale,
                                            ALU.max, ALU.mult).then_inc(mx_done, 1)
                misc = misc_at(m, lag, nxt)
                if misc and cur and misc[0] == "q" and qbias is not None:
                    dve_q_copy(dve, p + 1, misc[2], t_bank(3 * m + 3), False)
        return emit

    class PoolOrder:
        def __init__(self, pool, base):
            self.pool, self.base, self.k = pool, base, 0

        def then(self, ins, more=None):
            ins.then_inc(pool_step, 1)
            self.k += 1
            self.pool.wait_ge(pool_step, self.base + self.k)

    def pool_y_low(o, beta, par, old):
        o.pool.wait_ge(yh_done, beta + 1)
        if old:
            o.pool.wait_ge(sc_done, 21 * (beta - 1))
        nc.gpsimd.tensor_tensor(YL[:, par, :], YF[:, :], YH[:, par, :].bitcast(F32),
                                ALU.subtract).then_inc(yl_done, 1)
        o.pool.wait_ge(yl_done, beta + 1)

    def pool_q_low(o, beta, p, par):
        o.pool.wait_ge(qh_done, beta + 1)
        nc.gpsimd.tensor_tensor(Q[64:128, par, :].rearrange("p (h s) -> p h s", h=16),
                                QF[64:128, :, 56 * par:56 * par + 56],
                                Q[64:128, par, :].rearrange("p (h s) -> p h s", h=16).bitcast(F32),
                                ALU.subtract).then_inc(ql_done, 1)
        o.pool.wait_ge(ql_done, beta + 1)

    def pool_yv(o, beta, par, old):
        if with_ln:
            o.pool.wait_ge(yn_done, beta + 1)
        else:
            o.pool.wait_ge(y_loaded[par], 16 * (beta - par) + 32)
        if old:
            o.pool.wait_ge(pv_done, 2 * beta - 2)
        nc.gpsimd.tensor_tensor(yv[:, par, :, :], yt[:, par, :, 0:64], K.zero_bc, ALU.add).then_inc(yv_done, 1)
        o.pool.wait_ge(yv_done, beta + 1)

    def pool_z(o, beta, par):
        o.pool.wait_ge(ex_done, 7 * beta + 7)
        nc.gpsimd.tensor_tensor(Zall[:, bass.ds(7 * beta, 7)], ZP[:, 7 * par:7 * par + 7, 0],
                                ZP[:, 7 * par:7 * par + 7, 1], ALU.add).then_inc(z_done, 1)
        o.pool.wait_ge(z_done, beta + 1)

    def pool_ln1(o, beta, par):
        o.pool.wait_ge(y_sum1, beta + 1)
        ymean = LNS[0:TT, par, 0, :]
        o.then(nc.gpsimd.tensor_tensor(LNS[0:TT, par, 2, :], ymean, K.inv64, ALU.mult))
        nc.gpsimd.tensor_tensor(yraw[:, par, :, :], yraw[:, par, :, :],
                                LNS[0:TT, par, 2, :].unsqueeze(2).broadcast_to([TT, NTT, 64]),
                                ALU.subtract).then_inc(y_cent, 1)
        o.pool.wait_ge(y_cent, beta + 1)
        if not (isinstance(beta, int) and beta < 2):
            o.pool.wait_ge(yT_done, 3 * (beta - 2) + 3)
        nc.gpsimd.tensor_tensor(yt[:, par, :, 0:64], yraw[:, par, :, :], yraw[:, par, :, :],
                                ALU.mult).then_inc(y_sq, 1)
        o.pool.wait_ge(y_sq, beta + 1)

    def pool_ln2(o, beta, par):
        o.pool.wait_ge(y_sum2, beta + 1)
        o.then(nc.gpsimd.tensor_tensor(LNS[0:TT, par, 1, :], LNS[0:TT, par, 1, :], K.inv64, ALU.mult))
        o.then(nc.gpsimd.tensor_tensor(LNS[0:TT, par, 1, :], LNS[0:TT, par, 1, :], K.eps12, ALU.add))
        o.then(nc.gpsimd.tensor_tensor(LNS[0:TT, par, 1, :], LNS[0:TT, par, 1, :], K.mhalf12[0:TT, :], ALU.pow))
        o.then(nc.gpsimd.tensor_tensor(yraw[:, par, :, :], yraw[:, par, :, :],
                                       LNS[0:TT, par, 1, :].unsqueeze(2).broadcast_to([TT, NTT, 64]),
                                       ALU.mult))
        o.then(nc.gpsimd.tensor_tensor(yraw[:, par, :, :], yraw[:, par, :, :],
                                       g_bc.unsqueeze(1).broadcast_to([TT, NTT, 64]), ALU.mult))
        o.then(nc.gpsimd.tensor_tensor(yt[:, par, :, 0:64], yraw[:, par, :, :],
                                       b_bc.unsqueeze(1).broadcast_to([TT, NTT, 64]), ALU.add))
        nc.gpsimd.tensor_tensor(yt[:, par, :, 64:128], yraw[:, par, :, :],
                                b_bc.unsqueeze(1).broadcast_to([TT, NTT, 64]),
                                ALU.add).then_inc(yn_done, 1)
        o.pool.wait_ge(yn_done, beta + 1)

    LN_STEPS = 7
    PRE = 2 * LN_STEPS if with_ln else 0

    def pool_pair(pool):
        def emit(p, lag, cur, nxt):
            o = PoolOrder(pool, PRE + 2 * LN_STEPS * p)
            for par in range(2 if cur else 1):
                beta = 2 * p + par
                if cur and par == 0:
                    pool_q_low(o, beta + 1, p, 1)
                if cur:
                    pool_yv(o, beta, par, lag)
                if par == 1 or lag:
                    pool_z(o, beta - 1, (par + 1) % 2)
                if with_ln and nxt:
                    pool_ln1(o, beta + 2, par)
                if (par == 0 and cur) or nxt:
                    pool_y_low(o, beta + 1, (par + 1) % 2, lag or par == 1)
                if par == 1 and nxt:
                    pool_q_low(o, beta + 1, p + 1, 0)
                if with_ln and nxt:
                    pool_ln2(o, beta + 2, par)
        return emit

    ctx_v = ctx_dram.rearrange("b (r j) c -> b r j c", j=NTT)

    with nc.Block() as block:
        @block.sync
        def _(sp):
            def load(k, par):
                src = ctx_v[bass.ds(k, 1), :, :, :].rearrange("b r j c -> (b r) j c")
                if with_ln:
                    sp.dma_start(yraw[:, par, :, :], src).then_inc(y_loaded[par], 16)
                else:
                    for half in range(2):
                        sp.dma_start(yt[:, par, :, 64 * half:64 * half + 64], src).then_inc(y_loaded[par], 16)

            load(0, 0)
            load(1, 1)
            with sp.Fori(0, 7) as p:
                for par in range(2):
                    k = 2 * p + 2 + par
                    if with_ln:
                        sp.wait_ge(yn_done, k - 1)
                    else:
                        sp.wait_ge(yv_done, k - 1)
                        sp.wait_ge(yT_done, 3 * k - 3)
                    load(k, par)

        @block.tensor
        def _(pe):
            for k in range(4):
                if k >= 2:
                    pe.wait_ge(q_copied, k - 1)
                pe_q(0, k, 5 + k % 2)
            if with_ln:
                pe.wait_ge(yn_done, 1)
            else:
                pe.wait_ge(y_loaded[0], 32)
            for g in range(3):
                if g < 2:
                    pe.wait_ge(q_copied, 3 + g)
                else:
                    pe.wait_ge(yT_copied, 1)
                pe_y_transposes(0, 0, g, 5 + g % 2)
            pe.wait_ge(yT_copied, 3)
            for_pairs(pe, pe_pair(pe))

        @block.scalar
        def _(act):
            if qbias is None:
                for k in range(4):
                    act_q_copy(act, 0, k, 5 + k % 2, True)
            for g in range(3):
                act_y_copy(act, 0, g, 5 + g % 2, True)
            for_pairs(act, act_pair(act))

        @block.vector
        def _(dve):
            if qbias is not None:
                for k in range(4):
                    dve_q_copy(dve, 0, k, 5 + k % 2, True)
            if with_ln:
                dve_y_sum1(dve, 0, 0)
                dve_y_sum1(dve, 1, 1)
            dve_q_high(dve, 0, 0, False)
            if with_ln:
                dve_y_sum2(dve, 0, 0)
            dve_y_high(dve, 0, 0, False)
            if with_ln:
                dve_y_sum2(dve, 1, 1)
            for_pairs(dve, dve_pair(dve))

        @block.gpsimd
        def _(pool):
            o = PoolOrder(pool, 0)
            if with_ln:
                pool_ln1(o, 0, 0)
                pool_ln2(o, 0, 0)
            pool_q_low(o, 0, 0, 0)
            pool_y_low(o, 0, 0, False)
            if with_ln:
                pool_ln1(o, 1, 1)
                pool_ln2(o, 1, 1)
            for_pairs(pool, pool_pair(pool))


def block_selector(pool_order, nc, t, width, group):
    o = pool_order
    o.then(nc.gpsimd.memset(t, 1.0))
    o.then(nc.gpsimd.affine_select(t, t, pattern=[[1, width]], compare_op=ALU.is_ge, fill=0.0,
                                   base=0, channel_multiplier=-group))
    o.then(nc.gpsimd.affine_select(t, t, pattern=[[-1, width]], compare_op=ALU.is_ge, fill=0.0,
                                   base=group - 1, channel_multiplier=group))


def group_mask(pool_order, nc, t, heads, group):
    o = pool_order
    o.then(nc.gpsimd.memset(t, 1.0))
    o.then(nc.gpsimd.affine_select(t, t, pattern=[[-group, heads]], compare_op=ALU.is_ge, fill=0.0,
                                   base=0, channel_multiplier=1))
    o.then(nc.gpsimd.affine_select(t, t, pattern=[[group, heads]], compare_op=ALU.is_ge, fill=0.0,
                                   base=group - 1, channel_multiplier=-1))


class Arena:

    def __init__(self, flat):
        self.flat, self.at = flat, 0

    def take(self, *shape, parts=128):
        n = 1
        for s in shape:
            n *= s
        v = self.flat[0:parts, self.at:self.at + n]
        self.at += n
        assert self.at <= self.flat.shape[1]
        if len(shape) == 2:
            v = v.rearrange("p (a b) -> p a b", a=shape[0])
        elif len(shape) == 3:
            v = v.rearrange("p (a b c) -> p a b c", a=shape[0], b=shape[1])
        return v


def decoder_kernel(nc, d, out):
    with ExitStack() as ctx:
        build(nc, d, out, Kit(nc, ctx))


def build(nc, d, out, K):
    xin = d["x"].rearrange("b s c -> (b s) c")
    yout = out.rearrange("b s c -> (b s) c")

    K.ps = K.ctx.enter_context(nc.psum_tensor("ps", [128, 8, 512], F32))
    arena = K.sb("arena", [128, 2 * NTT * 896])
    K.PT = arena[:, :].rearrange("p (u j c) -> p u j c", u=2, j=NTT)
    K.P = K.sb("P", [128, 2, NTT * TT])
    K.YH, K.YL = K.sb("YH", [128, 2, NTT * TT], F32R), K.sb("YL", [128, 2, NTT * TT], F32R)
    K.YF = K.sb("YF", [128, NTT * TT])
    K.yt = K.sb("yt", [TT, 2, NTT, 128])
    K.yv, K.yraw = K.sb("yv", [TT, 2, NTT, 64]), K.sb("yraw", [TT, 2, NTT, 64])
    K.QF, K.Q = K.sb("QF", [128, 16, TP]), K.sb("Q", [128, 2, 16 * SQ], F32R)
    K.U = K.sb("U", [128, 16, TP])
    K.NM, K.MP, K.ZP = K.sb("NM", [128, STEPS]), K.sb("MP", [128, STEPS, 2]), K.sb("ZP", [128, STEPS, 2])
    K.LNS = K.sb("LNS", [128, 2, 3, NTT])
    K.b1s, K.cws = K.sb("b1s", [128, 2, NF]), K.sb("cws", [TP, 2, NT])
    K.ln_stats, K.ln_mv = K.sb("ln_stats", [TP, NT, 6]), K.sb("ln_mv", [TP, NT, 2])
    K.ln_rstd = K.sb("ln_rstd", [TP, 2, NT])
    X = K.sb("X", [TP, NT, CH])
    xnT = K.sb("xnT", [128, NTOK])
    oT = K.sb("oT", [128, 4, NTOK])
    Zall = K.sb("Zall", [128, BLOCKS * NB])
    M = K.sb("M", [128, 16, 128])
    wv = K.sb("wv", [128, 16, 32])
    qbias = K.sb("qbias", [128, 16])
    K.ident = K.sb("ident", [128, 128])
    K.mhalf12, inv64 = K.sb("mhalf12", [128, NTT]), K.sb("inv64", [TT, NTT])
    eps12, zero = K.sb("eps12", [TT, NTT]), K.sb("zero", [TT, 1])
    K.inv64, K.eps12 = inv64[:, :], eps12[:, :]
    K.zero_bc = zero[:, :].unsqueeze(2).broadcast_to([TT, NTT, CTX_C])
    K.expert_m8 = K.sb("expert_m8", [TP, NT, NE])
    hm0, hm1 = K.sb("hm0", [128, 4]), K.sb("hm1", [128, 16])
    lny = K.sb("lny", [TT, 2, CTX_C])
    VECS = ["L0_xattn_a1_lnx_g", "L0_xattn_a1_lnx_b", "L0_xattn_a1_lny_g", "L0_xattn_a1_lny_b",
            "L0_xattn_a1_ln3_g", "L0_xattn_a1_ln3_b", "L0_xattn_a2_lnx_g", "L0_xattn_a2_lnx_b",
            "L0_xattn_a2_ln3_g", "L0_xattn_a2_ln3_b", "L1_xattn_bq", "L1_xattn_bv"]
    MATS = [("L0_xattn_a1_li2_b", NF), ("L0_xattn_a2_li2_b", NF), ("L0_ffn_b1", NE * NF),
            ("L1_ffn_b1", NE * NF), ("L0_ffn_w_gate", NE)]
    at, ncols = {}, 0
    for v, n in [(v, 1) for v in VECS] + MATS:
        at[v] = (ncols, ncols + n)
        ncols += n
    cols = K.sb("cols", [128, ncols])

    def col(v):
        a, b = at[v]
        return cols[:, a:b]

    K.z_dram = nc.dram_tensor("z_scratch", [BLOCKS * NB, 128], F32).ap()

    A = Arena(arena)
    XA, XO = A.take(NT, CH), A.take(NT, CH)
    ynT = A.take(NTOK)
    qT_at = A.at
    qT, kT = A.take(4, NTOK + 8), A.take(4, NTOK)
    hT = arena[:, qT_at:qT_at + NF * NTOK].rearrange("p (f t) -> p f t", f=NF)
    a1 = {k: A.take(512) for k in ("wq", "wk", "wv")}
    li1, li2, li3 = A.take(4, CH), A.take(HID), A.take(NF, CH)
    QS, KS, YS, VS = A.take(4, CH), A.take(4, 2, 4 * SQ), A.take(2, CH), A.take(2, 512)
    E, AT, MX, SM = A.take(16, 64), A.take(8, 120), A.take(16), A.take(16)
    E2 = arena[:, NT * CH:NT * CH + 16 * 64].rearrange("p (h s) -> p h s", h=16)
    K.wkt = A.take(CTX_C)
    WQ2, WK2 = A.take(512), A.take(512)
    WQT, WKM = A.take(CH), A.take(4, CTX_C)
    rows = {k: A.take(CH, parts=TP) for k in ("ln1_g", "ln1_b", "ln2_g", "ln2_b", "a1_li1_b", "a1_li3_b")}
    stage = A.take(CH)
    mask, mask_b = A.take(SQ), A.take(SQ)
    K.mask = mask

    A1, A2 = "L0_xattn_a1_", "L0_xattn_a2_"
    x_loaded, rows_loaded, vecs_loaded = K.sem("x_loaded"), K.sem("rows_loaded"), K.sem("vecs_loaded")
    a1_loaded, a2_loaded = K.sem("a1_loaded"), K.sem("a2_loaded")
    const_step = K.sem("const_step")
    cols_done = K.sem("cols_done")

    def bcast(v, n=TP):
        return v.unsqueeze(0).broadcast_to([n, v.shape[0]])

    def by_head(w):
        return w.rearrange("h c d -> c h d")

    def heads_of(t, parts=128):
        return t[0:parts, :].rearrange("p (h d) -> p h d", h=16)

    def load_vectors(sp):
        for v in VECS:
            sp.dma_start(stage[at[v][0]:at[v][1], :], d[v].unsqueeze(0)).then_inc(vecs_loaded, 16)
        for v, n in MATS:
            src = d[v]
            if len(src.shape) == 1:
                src = src.rearrange("(f p) -> f p", p=128)
            elif src.shape[1] == HID:
                src = src.rearrange("e (f p) -> (e f) p", p=128)
            sp.dma_start(stage[at[v][0]:at[v][1], :], src).then_inc(vecs_loaded, 16)
        sp.wait_ge(rows_loaded, 32)

    def load_a1(sp):
        for k in ("wq", "wk", "wv"):
            sp.dma_start(heads_of(a1[k]), by_head(d[A1 + k])).then_inc(a1_loaded, 16)
        sp.dma_start(li1, d[A1 + "li1_w"].rearrange("(c p) o -> p c o", p=128)).then_inc(a1_loaded, 16)
        sp.dma_start(li2, d[A1 + "li2_w"]).then_inc(a1_loaded, 16)
        sp.dma_start(li3, d[A1 + "li3_w"].rearrange("(c p) o -> p c o", p=128)).then_inc(a1_loaded, 16)
        sp.wait_ge(vecs_loaded, 16 * (len(VECS) + len(MATS)))

    def load_a2(sp):
        for k in ("ln2_g", "ln2_b", "a1_li1_b", "a1_li3_b"):
            sp.dma_start(rows[k], bcast(d["L0_xattn_" + k])).then_inc(rows_loaded, 16)
        for i, k in enumerate(("g", "b")):
            sp.dma_start(lny[:, i, :], bcast(d[A2 + "lny_" + k], TT)).then_inc(a2_loaded, 16)
        sp.dma_start(heads_of(WQ2), by_head(d[A2 + "wq"])).then_inc(a2_loaded, 16)
        sp.dma_start(heads_of(WK2, 64), by_head(d[A2 + "wk"])).then_inc(a2_loaded, 16)
        for half in range(2):
            sp.dma_start(wv[64 * half:64 * half + 64, :, :], by_head(d[A2 + "wv"])).then_inc(a2_loaded, 16)
        sp.wait_ge(a1_loaded, 96)
        sp.wait_ge(rows_loaded, 96)

    with nc.Block() as block:
        @block.sync
        def _(sp):
            sp.dma_start(X[:, :, :], row_tiles(xin)).then_inc(x_loaded, 16)
            for k in ("ln1_g", "ln1_b"):
                sp.dma_start(rows[k], bcast(d["L0_xattn_" + k])).then_inc(rows_loaded, 16)
            sp.wait_ge(x_loaded, 16)

        @block.vector
        def _(dve):
            nc.vector.memset(K.mhalf12[:, :], -0.5)
            nc.vector.memset(inv64[:, :], 1.0 / CTX_C)
            nc.vector.memset(eps12[:, :], EPS)
            nc.vector.memset(zero[:, :], 0.0)
            nc.vector.memset(QS, 0.0)
            nc.vector.memset(KS, 0.0)
            nc.vector.memset(YS, 0.0)
            nc.vector.memset(E, 0.0)
            nc.vector.memset(E2, 0.0)
            nc.vector.memset(qT[:, :, NTOK:NTOK + 8], 0.0)
            for e in range(NE):
                nc.vector.memset(K.expert_m8[:, :, e:e + 1], float(e - NE))

        @block.gpsimd
        def _(pool):
            o = Chain(pool, const_step)
            o.then(nc.gpsimd.memset(K.ident[:, :], 1.0))
            o.then(nc.gpsimd.affine_select(K.ident[:, :], K.ident[:, :], pattern=[[-1, 128]],
                                           compare_op=ALU.is_equal, fill=0.0, base=0, channel_multiplier=1))
            for t, base in ((mask, 0), (mask_b, 64)):
                o.then(nc.gpsimd.memset(t, 1.0))
                o.then(nc.gpsimd.affine_select(t, t, pattern=[[1, SQ]], compare_op=ALU.is_gt, fill=0.0,
                                               base=base, channel_multiplier=-1))
            o.then(nc.gpsimd.affine_select(mask_b, mask_b, pattern=[[0, SQ]], compare_op=ALU.is_ge, fill=0.0,
                                           base=-64, channel_multiplier=1))
            o.then(nc.gpsimd.tensor_tensor(mask, mask, mask_b, ALU.add))
            group_mask(o, nc, hm0[:, :], 4, 32)
            group_mask(o, nc, hm1[:, :], 16, 8)

    layer_norm(nc, K, "ln_in", X, XA, prefetch=load_vectors)
    layer_norm(nc, K, "ln1", XA, XA, affine=(X, rows["ln1_g"], rows["ln1_b"]),
               prefetch=load_a1)
    with nc.Block() as block:
        @block.tensor
        def _(pe):
            nc.tensor.transpose(K.ps[:, 0, 0:ncols], stage[0:ncols, :], K.ident[0:ncols, 0:ncols]
                                ).then_inc(cols_done, 1)

        @block.vector
        def _(dve):
            dve.wait_ge(cols_done, 1)
            nc.vector.tensor_copy(cols[:, :], K.ps[:, 0, 0:ncols])

    layer_norm(nc, K, "ln_xy", X, XA,
               outs=[(xnT, col(A1 + "lnx_g"), col(A1 + "lnx_b")), (ynT, col(A1 + "lny_g"), col(A1 + "lny_b"))],
               prefetch=load_a2)
    self_attention(nc, K, xnT, ynT, qT, kT, a1["wq"], a1["wk"], a1["wv"], oT,
                   (QS, KS, YS, VS, (E, E2), AT, MX, SM), 32 ** -0.5)
    project_and_add(nc, K, "sa_out", XO, [X], rows["a1_li1_b"], oT, li1)
    layer_norm(nc, K, "ln3a", XO, XA, outs=[(xnT, col(A1 + "ln3_g"), col(A1 + "ln3_b"))])
    hidden_layer(nc, K, "ff1", xnT, li2, col(A1 + "li2_b"), hT)
    project_and_add(nc, K, "ff1_out", X, [X, XO], rows["a1_li3_b"], hT, li3)
    layer_norm(nc, K, "ln2", X, XA, affine=(X, rows["ln2_g"], rows["ln2_b"]))

    layer_norm(nc, K, "ln_x2", X, XA, outs=[(xnT, col(A2 + "lnx_g"), col(A2 + "lnx_b"))],
               prefetch=lambda sp: sp.wait_ge(a2_loaded, 96))
    fold_query_weights(nc, K, "fold0", WQ2, WK2, 4, hm0[:, :], M, WQT, WKM)
    cross_attention(nc, K, "xa0", d["ctx_512"], xnT, M, None, 32 ** -0.5, wv, oT, Zall, True,
                    g_bc=lny[:, 0, :], b_bc=lny[:, 1, :])

    B = Arena(arena)
    XA, XO, XI = B.take(NT, CH), B.take(NT, CH), B.take(NT, CH)
    hT = B.take(NF, NTOK)
    li1, li2, li3 = B.take(4, CH), B.take(HID), B.take(NF, CH)
    li1_b, li3_b = B.take(CH, parts=TP), B.take(CH, parts=TP)
    zt, rzt = B.take(CH), B.take(16, SQ)
    sel = B.take(4, CH)
    Wb1, Wb2, hM = B.take(2, HID), B.take(2, NF, CH), B.take(2, NF, 448)
    b2, gw, bg = B.take(CH, parts=NE), B.take(NE), B.take(NE, parts=TP)
    moe = (B.take(NT, NE), B.take(NT, NE), B.take(NT, NE), B.take(4, NT), B.take(NT, NE), B.take(NTOK, parts=NE))
    WQ1, WK1, Wo = B.take(CH), B.take(CH), B.take(1, CH)
    WQT1, WKM1, wkt1 = B.take(CH), B.take(16, CTX_C), B.take(CTX_C)

    def selector(name, nchunk, group):
        with nc.Block() as block:
            @block.gpsimd
            def _(pool):
                block_selector(K.chain(pool, "sel_chain"), nc, sel[0:16, 0:nchunk, :].rearrange("p c f -> p (c f)"),
                               128 * nchunk, group)

    post_loaded = K.sem("post_loaded")

    def load_post(sp):
        for dst, src in ((li1, d[A2 + "li1_w"].rearrange("(c p) o -> p c o", p=128)),
                         (li1_b, bcast(d[A2 + "li1_b"])), (li3_b, bcast(d[A2 + "li3_b"])),
                         (li2, d[A2 + "li2_w"]),
                         (li3, d[A2 + "li3_w"].rearrange("(c p) o -> p c o", p=128)),
                         (XI[0:TP, :, :], row_tiles(xin))):
            sp.dma_start(dst, src).then_inc(post_loaded, 16)
        sp.wait_ge(post_loaded, 96)

    selector("sel0", 4, 32)
    normalise_attention(nc, K, "nrm0", Zall, oT, sel, None, zt, rzt, prefetch=load_post)
    project_and_add(nc, K, "xa0_out", XO, [X], li1_b, oT, li1)
    layer_norm(nc, K, "ln3b", XO, XA, outs=[(xnT, col(A2 + "ln3_g"), col(A2 + "ln3_b"))])
    hidden_layer(nc, K, "ff2", xnT, li2, col(A2 + "li2_b"), hT)
    project_and_add(nc, K, "ff2_out", X, [X, XO, XI], li3_b, hT, li3)

    m0_small, small0 = K.shared("small_loaded", 16)
    load0 = ExpertLoader(nc, d["L0_ffn_W1"], d["L0_ffn_W2"], Wb1, Wb2,
                         [K.sem("m0_w1_even"), K.sem("m0_w1_odd")], [K.sem("m0_w2_even"), K.sem("m0_w2_odd")])

    def load_m0(sp):
        sp.dma_start(b2, d["L0_ffn_b2"]).then_inc(m0_small, 16)
        for u in range(2):
            load0.first(sp, u, u)
            load0.second(sp, u, u)
        sp.wait_ge(m0_small, 16)

    layer_norm(nc, K, "ln_m0", X, XA, outs=[(xnT, None, None)], prefetch=load_m0)
    mixture(nc, K, "moe0", X, xnT, col("L0_ffn_w_gate"), None, 2, col("L0_ffn_b1"), b2, load0,
            Wb1, Wb2, hM, moe)

    l1_loaded, wv_zero = K.sem("l1_loaded"), K.sem("wv_zero")
    with nc.Block() as block:
        @block.vector
        def _(dve):
            nc.vector.memset(wv[:, :, :], 0.0).then_inc(wv_zero, 1)

        @block.sync
        def _(sp):
            sp.dma_start(WQ1, d["L1_xattn_Wq"]).then_inc(l1_loaded, 16)
            sp.dma_start(WK1[0:64, :], d["L1_xattn_Wk"]).then_inc(l1_loaded, 16)
            sp.wait_ge(wv_zero, 1)
            src = d["L1_xattn_Wv"].rearrange("c (a j k) -> c a j k", j=4, k=8)
            dst = wv[:, :, :].rearrange("p (a j) k -> p a j k", j=4)
            for half in range(2):
                for j in range(4):
                    sp.dma_start(dst[64 * half:64 * half + 64, :, j, 8 * j:8 * j + 8], src[:, :, j, :]
                                 ).then_inc(l1_loaded, 16)
    layer_norm(nc, K, "ln_x3", X, XA, outs=[(xnT, None, None)], prefetch=lambda sp: sp.wait_ge(l1_loaded, 160))
    K.wkt = wkt1
    fold_query_weights(nc, K, "fold1", WQ1, WK1, 1, hm1[:, :], M, WQT1, WKM1, bq=col("L1_xattn_bq"), qbias=qbias)
    oT1 = oT[:, 0:1, :]
    cross_attention(nc, K, "xa1", d["ctx_512"], xnT, M, qbias, 8 ** -0.5, wv, oT1, Zall, False)

    wo_loaded = K.sem("wo_loaded")

    def load_wo(sp):
        sp.dma_start(Wo[:, 0, :], d["L1_xattn_Wo"]).then_inc(wo_loaded, 16)
        sp.dma_start(li1_b, bcast(d["L1_xattn_bo"])).then_inc(wo_loaded, 16)
        sp.wait_ge(wo_loaded, 32)

    selector("sel1", 1, 8)
    normalise_attention(nc, K, "nrm1", Zall, oT1, sel, col("L1_xattn_bv"), zt, rzt, prefetch=load_wo)
    project_and_add(nc, K, "xa1_out", X, [X], li1_b, oT1, Wo)

    m1_small, small0 = K.shared("small_loaded", 48)
    load1 = ExpertLoader(nc, d["L1_ffn_W1"], d["L1_ffn_W2"], Wb1, Wb2,
                         [K.sem("m1_w1_even"), K.sem("m1_w1_odd")], [K.sem("m1_w2_even"), K.sem("m1_w2_odd")])

    def load_m1(sp):
        sp.dma_start(b2, d["L1_ffn_b2"]).then_inc(m1_small, 16)
        sp.dma_start(gw, d["L1_ffn_Wg"]).then_inc(m1_small, 16)
        sp.dma_start(bg, bcast(d["L1_ffn_bg"])).then_inc(m1_small, 16)
        for u in range(2):
            load1.first(sp, u, u)
            load1.second(sp, u, u)
        sp.wait_ge(m1_small, small0 + 48)

    layer_norm(nc, K, "ln_m1", X, XA, outs=[(xnT, None, None)], prefetch=load_m1)
    mixture(nc, K, "moe1", X, xnT, gw, bg, 1, col("L1_ffn_b1"), b2, load1, Wb1, Wb2, hM, moe)

    out_stored = K.sem("out_stored")
    with nc.Block() as block:
        @block.sync
        def _(sp):
            sp.dma_start(row_tiles(yout), X[:, :, :]).then_inc(out_stored, 16)
            sp.wait_ge(out_stored, 16)


def kernel(**inputs):
    import numpy as _np
    import concourse.bacc as _bacc
    from concourse import mybir as _mybir
    from concourse.bass_utils import run_bass_kernel_spmd as _run

    nc = _bacc.Bacc("TRN2", target_bir_lowering=False, num_devices=1)
    arrays, d = {}, {}
    for name in inputs:
        a = _np.ascontiguousarray(inputs[name])
        arrays[f"in_{name}_dram"] = a
        d[name] = nc.dram_tensor(f"in_{name}_dram", a.shape, _mybir.dt.from_np(a.dtype), kind="ExternalInput").ap()
    out = nc.dram_tensor("out_0_dram", (NB, SQ, CH), _mybir.dt.float32, kind="ExternalOutput").ap()
    decoder_kernel(nc, d, out)
    r = _run(nc, [arrays], core_ids=[0])
    return r.results[0]["out_0_dram"]
```

```python
from contextlib import ExitStack

import concourse.bass as bass
from concourse import mybir

F32 = mybir.dt.float32
F32R = mybir.dt.float32r
ALU = mybir.AluOpType
ACT = mybir.ActivationFunctionType
AX = mybir.AxisListType

NB, SQ, CH = 16, 56, 128
NTOK = NB * SQ
TP = 112
NT = NTOK // TP
CTX_C = 64
NE, HID = 8, 512
NF = HID // 128
EPS = 1e-5


class Kit:

    def __init__(self, nc, ctx):
        self.nc, self.ctx = nc, ctx
        self.shared_sems, self.chains = {}, {}

    def sb(self, name, shape, dt=F32):
        return self.ctx.enter_context(self.nc.sbuf_tensor(name, shape, dt))

    def sem(self, name):
        return self.ctx.enter_context(self.nc.semaphore(name))

    def shared(self, name, adds):
        if name not in self.shared_sems:
            self.shared_sems[name] = [self.sem(name), 0]
        sem, base = self.shared_sems[name]
        self.shared_sems[name][1] += adds
        return sem, base

    def chain(self, eng, name):
        if name not in self.chains:
            self.chains[name] = [self.sem(name), 0]
        return Chain(eng, *self.chains[name], self.chains[name])


class Chain:

    def __init__(self, eng, sem, n=0, record=None):
        self.eng, self.sem, self.n, self.record = eng, sem, n, record

    def then(self, ins):
        self.n += 1
        if self.record is not None:
            self.record[1] = self.n
        ins.then_inc(self.sem, 1)
        self.eng.wait_ge(self.sem, self.n)


def row_tiles(x):
    return x.rearrange("(n p) c -> p n c", p=TP)


def over_tiles(v, n=NT):
    return v.unsqueeze(1).broadcast_to([v.shape[0], n, v.shape[1]])


def layer_norm(nc, K, name, X, XA, outs=(), affine=None, prefetch=None):
    stats, mv, rstd = K.ln_stats, K.ln_mv, K.ln_rstd
    st_done, st0 = K.shared("ln_st", 2)
    ag_done, ag0 = K.shared("ln_ag", 2)
    var_ready, var0 = K.shared("ln_var", 2)
    rstd_ready, rstd0 = K.shared("ln_rstd", 2)
    xa_ready, xa0 = K.shared("ln_xa", 4)
    xt_ready, xt0 = K.shared("ln_xt", 2 * len(outs))
    gain_done, g0 = K.shared("ln_gain", 2 if affine else 0)
    HT = NT // 2

    def copy_out(eng, out, half, bank):
        dst, gain, bias = out
        src, d = K.ps[:, bank + half, 0:448], dst[:, 448 * half:448 * half + 448]
        if eng is nc.vector:
            eng.tensor_scalar(d, src, gain, bias, ALU.mult, ALU.add)
        elif gain is None:
            eng.copy(d, src)
        else:
            eng.activation(d, src, ACT.Identity, scale=gain, bias=bias)

    with nc.Block() as block:
        if prefetch is not None:
            @block.sync
            def _(sp):
                prefetch(sp)

        @block.vector
        def _(dve):
            for half in range(2):
                t = slice(HT * half, HT * half + HT)
                for n in range(HT * half, HT * half + HT):
                    last = nc.vector.bn_stats(stats[0:TP, n, :], X[0:TP, n, :])
                last.then_inc(st_done, 1)
                dve.wait_ge(st_done, st0 + half + 1)
                for n in range(HT * half, HT * half + HT):
                    last = nc.vector.bn_aggr(mv[0:TP, n, :], stats[0:TP, n, :])
                last.then_inc(ag_done, 1)
                dve.wait_ge(ag_done, ag0 + half + 1)
                nc.vector.tensor_scalar(rstd[0:TP, 0, t], mv[0:TP, t, 1], EPS, None, ALU.add).then_inc(var_ready, 1)
            for half in range(2):
                dve.wait_ge(rstd_ready, rstd0 + half + 1)
                for n in range(HT * half, HT * half + HT):
                    last = nc.vector.tensor_scalar(XA[0:TP, n, :], X[0:TP, n, :], mv[0:TP, n, 0:1],
                                                   rstd[0:TP, 1, n:n + 1], ALU.subtract, ALU.mult)
                    if n % 2:
                        last.then_inc(xa_ready, 1)
            if affine is not None:
                dst, gain, bias = affine
                for half in range(2):
                    t = slice(HT * half, HT * half + HT)
                    dve.wait_ge(xa_ready, xa0 + 2 * half + 2)
                    nc.vector.tensor_tensor(dst[0:TP, t, :], XA[0:TP, t, :], over_tiles(gain, HT),
                                            ALU.mult).then_inc(gain_done, 1)
                for half in range(2):
                    t = slice(HT * half, HT * half + HT)
                    dve.wait_ge(gain_done, g0 + half + 1)
                    nc.vector.tensor_tensor(dst[0:TP, t, :], dst[0:TP, t, :], over_tiles(bias, HT), ALU.add)
            for half in range(2 if len(outs) > 1 else 0):
                dve.wait_ge(xt_ready, xt0 + 2 + half + 1)
                copy_out(nc.vector, outs[1], half, 2)

        @block.gpsimd
        def _(pool):
            for half in range(2):
                t = slice(HT * half, HT * half + HT)
                pool.wait_ge(var_ready, var0 + half + 1)
                nc.gpsimd.tensor_tensor(rstd[0:TP, 1, t], rstd[0:TP, 0, t], K.mhalf12[0:TP, 0:HT],
                                        ALU.pow).then_inc(rstd_ready, 1)
                pool.wait_ge(rstd_ready, rstd0 + half + 1)

        if outs:
            @block.tensor
            def _(pe):
                for o in range(len(outs)):
                    for n in range(NT):
                        if o == 0 and n % 2 == 0:
                            pe.wait_ge(xa_ready, xa0 + n // 2 + 1)
                        last = nc.tensor.transpose(K.ps[:, 2 * o + n // 4, TP * (n % 4):TP * (n % 4) + TP],
                                                   XA[0:TP, n, :], K.ident[0:TP, 0:TP])
                        if n % 4 == 3:
                            last.then_inc(xt_ready, 1)

            @block.scalar
            def _(act):
                for half in range(2):
                    act.wait_ge(xt_ready, xt0 + half + 1)
                    copy_out(nc.scalar, outs[0], half, 0)


def fold_query_weights(nc, K, name, WQ, WK, nchunk, mask, M, WQT, WKT, WKM, bq=None, qbias=None, tmp=None):
    nh = 16 // nchunk
    wt_ready, wt0 = K.shared("fold_wt", 1)
    wk_copied, wk0 = K.shared("fold_wk", 1)
    wkm_ready, wkm0 = K.shared("fold_wkm", nchunk)
    m_ready, m0 = K.shared("fold_m", 2)
    qb_ready = K.sem(f"{name}_qb") if bq is not None else None
    with nc.Block() as block:
        @block.tensor
        def _(pe):
            for c in range(nchunk):
                nc.tensor.transpose(K.ps[:, 0, 128 * c:128 * c + 128], WQ[:, 128 * c:128 * c + 128], K.ident[:, :])
            for c in range(nchunk):
                last = nc.tensor.transpose(K.ps[:, 1, 64 * c:64 * c + 64], WK[0:64, 128 * c:128 * c + 128],
                                           K.ident[0:64, 0:64])
            last.then_inc(wt_ready, 1)
            w = min(512, nh * 64)
            for k in range(16 * 64 // w):
                c = k * w // (nh * 64)
                pe.wait_ge(wkm_ready, wkm0 + c + 1)
                last = nc.tensor.matmul(K.ps[:, 2 + k * w // 512, k * w % 512:k * w % 512 + w], WQT[:, c, :],
                                        WKM[:, :, :].rearrange("p h c -> p (h c)")[:, k * w:k * w + w],
                                        start=True, stop=True, skip_group_check=True)
                if (k + 1) * w % 512 == 0:
                    last.then_inc(m_ready, 1)

        def copy_m(copy, bank):
            for half in range(2):
                copy(M[:, 8 * bank:8 * bank + 8, 64 * half:64 * half + 64],
                     K.ps[:, 2 + bank, :].rearrange("p (h c) -> p h c", h=8))

        @block.vector
        def _(dve):
            dve.wait_ge(wt_ready, wt0 + 1)
            nc.vector.tensor_copy(WQT[:, :, :], K.ps[:, 0, 0:128 * nchunk].rearrange("p (c f) -> p c f", c=nchunk))
            nc.vector.tensor_copy(WKT[:, :, :], K.ps[:, 1, 0:64 * nchunk].rearrange("p (c f) -> p c f", c=nchunk)
                                  ).then_inc(wk_copied, 1)
            dve.wait_ge(wk_copied, wk0 + 1)
            for c in range(nchunk):
                nc.vector.tensor_tensor(WKM[:, nh * c:nh * c + nh, :], over_tiles(WKT[:, c, :], nh),
                                        mask.unsqueeze(2).broadcast_to([128, nh, 64]),
                                        ALU.mult).then_inc(wkm_ready, 1)
            if bq is not None:
                nc.vector.tensor_tensor(tmp, WK, bq, ALU.mult).then_inc(qb_ready, 1)
                dve.wait_ge(qb_ready, 1)
                nc.vector.tensor_reduce(qbias[:, :], tmp.rearrange("p (h d) -> p h d", h=16), axis=AX.X, op=ALU.add)
            dve.wait_ge(m_ready, m0 + 1)
            copy_m(nc.vector.tensor_copy, 0)

        @block.scalar
        def _(act):
            act.wait_ge(m_ready, m0 + 2)
            copy_m(nc.scalar.copy, 1)


def self_attention(nc, K, xT, yT, qT, kT, WQ, WK, WV, oT, bufs, scale, norm):
    QS, KS, YS, VS, E, AT, MX, SM = bufs
    H, D = 16, 32
    proj_done, proj_copied = K.sem("sa_proj"), K.sem("sa_projc")
    with nc.Block() as block:
        @block.sync
        def _(sp):
            for beta in range(2):
                norm.load(sp, beta, beta)

        @block.vector
        def _(dve):
            norm.dve_y_sum1(dve, 0, 0)
            norm.dve_y_sum2(dve, 0, 0)

        @block.gpsimd
        def _(pool):
            o = norm.order(pool, 0)
            norm.pool_ln1(o, 0, 0)
            norm.pool_ln2(o, 0, 0)

        @block.tensor
        def _(pe):
            k = 0
            for W, src in ((WQ, xT), (WK, yT)):
                for c in range(4):
                    for half in range(2):
                        if k >= 8:
                            pe.wait_ge(proj_copied, k - 7)
                        nc.tensor.matmul(K.ps[:, k % 8, 0:448], W[:, 128 * c:128 * c + 128],
                                         src[:, 448 * half:448 * half + 448],
                                         start=True, stop=True).then_inc(proj_done, 1)
                        k += 1

        @block.scalar
        def _(act):
            for k in range(16):
                dst, c, half = (qT, kT)[k // 8], k % 8 // 2, k % 2
                act.wait_ge(proj_done, k + 1)
                nc.scalar.copy(dst[:, c, 448 * half:448 * half + 448], K.ps[:, k % 8, 0:448]
                               ).then_inc(proj_copied, 1)

    q_sliced, y_sliced = K.sem("sa_qs"), K.sem("sa_ys")
    v_done, v_copied = K.sem("sa_v"), K.sem("sa_vc")
    sc_done = K.sem("sa_sc")
    mx_done, sub_done = K.sem("sa_mx"), K.sem("sa_sub")
    ex_done, sum_done, rec_done, mask_done, norm_done = (
        K.sem("sa_ex"), K.sem("sa_sum"), K.sem("sa_rec"), K.sem("sa_mask"), K.sem("sa_norm"))
    tr_done, tr_copied = K.sem("sa_tr"), K.sem("sa_trc")
    o_done, o_copied = K.sem("sa_o"), K.sem("sa_oc")

    def wait_from_second(eng, sem, p, value):
        if not isinstance(p, int) or value > 0:
            eng.wait_ge(sem, value)

    def pairs(eng, emit, after_first=None, after_second=None):
        emit(0, 0, False, True)
        if after_first is not None:
            after_first()
        emit(1, 1, True, True)
        if after_second is not None:
            after_second()
        with eng.Fori(1, NT // 2 - 1) as t:
            emit(2 * t, 0, True, True)
            emit(2 * t + 1, 1, True, True)
        emit(NT - 2, 0, True, True)
        emit(NT - 1, 1, True, True)
        emit(NT, 0, True, False)

    with nc.Block() as block:
        @block.gpsimd
        def _(pool):
            def emit(p, par, lag, cur):
                if cur:
                    e = E[par][0:120, :, 0:SQ]
                    pool.wait_ge(sum_done, p + 1)
                    nc.gpsimd.tensor_tensor(e, e, over_tiles(K.mask[0:120, :], H), ALU.mult).then_inc(mask_done, 1)
                    pool.wait_ge(mask_done, p + 1)
            o = norm.order(pool, 1)
            pairs(pool, emit, lambda: norm.pool_ln1(o, 1, 1), lambda: norm.pool_ln2(o, 1, 1))

        @block.tensor
        def _(pe):
            def emit(p, par, lag, cur):
                if cur:
                    pe.wait_ge(q_sliced, p + 1)
                    if lag:
                        pe.wait_ge(sub_done, p)
                    for c in range(4):
                        for u in range(2):
                            last = nc.tensor.matmul(
                                K.ps[64 * u:64 * u + 64, c // 2, 4 * SQ * (c % 2):4 * SQ * (c % 2) + 4 * SQ],
                                QS[:, c, 64 * u:64 * u + 64],
                                KS[:, c, u, :], start=True, stop=True, skip_group_check=True)
                    last.then_inc(sc_done, 1)
                if lag:
                    pe.wait_ge(y_sliced, p)
                    for u in range(2):
                        wait_from_second(pe, v_copied, p, 2 * p - 3 + u)
                        nc.tensor.matmul(K.ps[0:120, (6, 2)[u], 0:512], YS[:, u, 0:120], WV[:, :],
                                         start=True, stop=True).then_inc(v_done, 1)
                    for b in range(2):
                        pe.wait_ge(proj_copied, 16)
                        pe.wait_ge(norm_done, p)
                        wait_from_second(pe, tr_copied, p, 2 * p - 2 + b)
                        for g in range(4 * b, 4 * b + 4):
                            last = nc.tensor.transpose(
                                K.ps[:, 4 + b, 120 * (g % 4):120 * (g % 4) + 120],
                                E[1 - par][0:120, 2 * g:2 * g + 2, :].rearrange("p h t -> p (h t)"),
                                K.ident[0:120, 0:120])
                        last.then_inc(tr_done, 1)
                    for u in range(2):
                        pe.wait_ge(proj_copied, 16)
                        pe.wait_ge(tr_copied, 2 * p)
                        pe.wait_ge(v_copied, 2 * p)
                        wait_from_second(pe, o_copied, p, 2 * p - 3 + u)
                        for h in range(H):
                            j, c, r = h % 4, h // 4, 64 * (h % 2)
                            last = nc.tensor.matmul(K.ps[32 * j:32 * j + 32, (7, 3)[u], SQ * c:SQ * c + SQ],
                                                    VS[r:r + SQ, u, 32 * h:32 * h + 32],
                                                    AT[r:r + SQ, h // 2, 64 * u:64 * u + SQ],
                                                    start=True, stop=True, skip_group_check=True)
                        last.then_inc(o_done, 1)
            pairs(pe, emit)

        @block.vector
        def _(dve):
            def slices(p):
                for u in range(2):
                    nc.vector.tensor_copy(QS[:, :, 64 * u:64 * u + 64],
                                          qT[:, :, bass.ds(TP * p + SQ * u, 64)])
                for j in range(4):
                    last = nc.vector.tensor_copy(
                        KS[32 * j:32 * j + 32, :, :, SQ * j:SQ * j + SQ],
                        kT[32 * j:32 * j + 32, :, bass.ds(TP * p, TP)].rearrange("p c (u t) -> p c u t", u=2))
                last.then_inc(q_sliced, 1)

            def emit(p, par, lag, cur):
                if lag:
                    wait_from_second(dve, v_done, p, 2 * p - 2)
                    for r in (0, 64):
                        last = nc.vector.tensor_copy(
                            YS[:, :, r:r + SQ], yT[:, bass.ds(TP * (p - 1), TP)].rearrange("p (u t) -> p u t", u=2))
                    last.then_inc(y_sliced, 1)
                if lag:
                    before = E[1 - par][0:120, :, 0:SQ]
                    dve.wait_ge(rec_done, p)
                    dve.wait_ge(mask_done, p)
                    nc.vector.tensor_tensor(before, before, SM[0:120, :].unsqueeze(2).broadcast_to([120, H, SQ]),
                                            ALU.mult).then_inc(norm_done, 1)
                if cur:
                    dve.wait_ge(sc_done, p + 1)
                    sc = K.ps[0:120, 0:2, 0:8 * SQ].rearrange("p b (h t) -> p b h t", h=8)
                    mx = MX[0:120, :].rearrange("p (b h) -> p b h", b=2)
                    nc.vector.tensor_reduce(mx, sc, axis=AX.X, op=ALU.max).then_inc(mx_done, 1)
                    dve.wait_ge(mx_done, p + 1)
                    wait_from_second(dve, tr_done, p, 2 * p - 2)
                    nc.vector.tensor_tensor(E[par][0:120, :, 0:SQ].rearrange("p (b h) t -> p b h t", b=2), sc,
                                            mx.unsqueeze(3).broadcast_to([120, 2, 8, SQ]),
                                            ALU.subtract).then_inc(sub_done, 1)
                    if not isinstance(p, int) or p + 1 < NT:
                        slices(p + 1)
                if cur:
                    dve.wait_ge(ex_done, p + 1)
                    if lag:
                        dve.wait_ge(norm_done, p)
                    nc.vector.tensor_reduce(SM[0:120, :], E[par][0:120, :, 0:SQ], axis=AX.X,
                                            op=ALU.add).then_inc(sum_done, 1)
                    dve.wait_ge(sum_done, p + 1)
                    nc.vector.reciprocal(SM[0:120, :], SM[0:120, :]).then_inc(rec_done, 1)

            norm.dve_y_sum1(dve, 1, 1)
            slices(0)
            pairs(dve, emit, None, lambda: norm.dve_y_sum2(dve, 1, 1))

        @block.scalar
        def _(act):
            def emit(p, par, lag, cur):
                if lag:
                    wait_from_second(act, o_done, p, 2 * p - 2)
                    for u in range(2):
                        act.wait_ge(v_done, 2 * p - 1 + u)
                        nc.scalar.copy(VS[0:120, u, :], K.ps[0:120, (6, 2)[u], 0:512]).then_inc(v_copied, 1)
                if cur:
                    act.wait_ge(sub_done, p + 1)
                    nc.scalar.activation(E[par][0:120, :, 0:SQ], E[par][0:120, :, 0:SQ], ACT.Exp,
                                         scale=scale).then_inc(ex_done, 1)
                if lag:
                    for b in range(2):
                        act.wait_ge(tr_done, 2 * p - 1 + b)
                        last = nc.scalar.copy(AT[:, 4 * b:4 * b + 4, :],
                                              K.ps[:, 4 + b, 0:480].rearrange("p (g s) -> p g s", g=4))
                        last.then_inc(tr_copied, 1)
                    for u in range(2):
                        act.wait_ge(o_done, 2 * p - 1 + u)
                        nc.scalar.copy(oT[:, :, bass.ds(TP * (p - 1) + SQ * u, SQ)],
                                       K.ps[:, (7, 3)[u], 0:4 * SQ].rearrange("p (c s) -> p c s", c=4)).then_inc(o_copied, 1)
            pairs(act, emit)


def normalise_attention(nc, K, name, Zall, oT, sel, vbias, zt, rzt, prefetch=None):
    nchunk = oT.shape[1]
    RH, RL = K.YH[0:16, 0, 0:NTOK], K.YH[0:16, 1, 0:NTOK]
    SEL = K.YL[0:16, 0, 0:128 * nchunk].rearrange("p (c f) -> p c f", c=nchunk)
    sel_done, k0 = K.shared("nrm_sel", 1)
    rh_done, _ = K.shared("nrm_rh", 1)
    rl_done, _ = K.shared("nrm_rl", 1)
    rec_done, _ = K.shared("nrm_rec", 1)
    zt_done, _ = K.shared("nrm_zt", 1)
    zt_copied, _ = K.shared("nrm_ztc", 1)
    z_stored, z0 = K.shared("nrm_zst", 16)
    z_loaded, _ = K.shared("nrm_zld", 16)
    bc_done, bc0 = K.shared("nrm_bc", 2 * nchunk)
    bc_used, _ = K.shared("nrm_bcu", 2 * nchunk)
    with nc.Block() as block:
        @block.sync
        def _(sp):
            if prefetch is not None:
                prefetch(sp)

        @block.scalar
        def _(act):
            act.wait_ge(zt_copied, k0 + 1)
            act.dma_start(K.z_dram, zt[0:112, :]).then_inc(z_stored, 16)
            act.wait_ge(z_stored, z0 + 16)
            act.dma_start(rzt[0:16, :, :], K.z_dram.rearrange("k p -> (k p)").rearrange(
                "(b h s) -> h b s", b=NB, h=16)).then_inc(z_loaded, 16)
            act.wait_ge(z_loaded, z0 + 16)

        @block.tensor
        def _(pe):
            pe.wait_ge(rec_done, k0 + 1)
            nc.tensor.transpose(K.ps[0:112, 0, 0:128], Zall[:, :], K.ident[:, :]).then_inc(zt_done, 1)
            pe.wait_ge(sel_done, k0 + 1)
            pe.wait_ge(rl_done, k0 + 1)
            for k in range(2 * nchunk):
                c, half = k // 2, k % 2
                if k >= 2:
                    pe.wait_ge(bc_used, bc0 + k - 1)
                nc.tensor.matmul(K.ps[:, 1 + k % 2, 0:448], SEL[:, c, :],
                                 RH[:, 448 * half:448 * half + 448], start=True, stop=False)
                nc.tensor.matmul(K.ps[:, 1 + k % 2, 0:448], SEL[:, c, :],
                                 RL[:, 448 * half:448 * half + 448], start=False, stop=True).then_inc(bc_done, 1)

        @block.vector
        def _(dve):
            nc.vector.reciprocal(Zall[:, :], Zall[:, :]).then_inc(rec_done, 1)
            dve.wait_ge(zt_done, k0 + 1)
            nc.vector.tensor_copy(zt[0:112, :], K.ps[0:112, 0, 0:128]).then_inc(zt_copied, 1)
            nc.vector.tensor_copy(SEL, sel[0:16, 0:nchunk, :]).then_inc(sel_done, 1)
            dve.wait_ge(z_loaded, z0 + 16)
            rz = rzt[0:16, :, :].rearrange("h b s -> h (b s)")
            nc.vector.tensor_copy(RH, rz).then_inc(rh_done, 1)
            dve.wait_ge(rh_done, k0 + 1)
            nc.vector.tensor_tensor(RL, rz, RH.bitcast(F32), ALU.subtract).then_inc(rl_done, 1)
            for k in range(2 * nchunk):
                c, half = k // 2, k % 2
                cols = slice(448 * half, 448 * half + 448)
                dve.wait_ge(bc_done, bc0 + k + 1)
                nc.vector.tensor_tensor(oT[:, c, cols], oT[:, c, cols], K.ps[:, 1 + k % 2, 0:448],
                                        ALU.mult).then_inc(bc_used, 1)
                if vbias is not None:
                    dve.wait_ge(bc_used, bc0 + k + 1)
                    nc.vector.tensor_scalar(oT[:, c, cols], oT[:, c, cols], vbias, None, ALU.add)


def project_and_add(nc, K, name, dst, terms, bias, srcT, W):
    nchunk = srcT.shape[1]
    base_done, base0 = K.shared("proj_base", len(terms))
    mm_done, mm0 = K.shared("proj_mm", 2)
    with nc.Block() as block:
        @block.gpsimd
        def _(pool):
            o = Chain(pool, base_done, base0)
            o.then(nc.gpsimd.tensor_tensor(dst[0:TP, :, :], terms[0][0:TP, :, :], over_tiles(bias), ALU.add))
            for t in terms[1:]:
                o.then(nc.gpsimd.tensor_tensor(dst[0:TP, :, :], dst[0:TP, :, :], t[0:TP, :, :], ALU.add))

        @block.tensor
        def _(pe):
            for n in range(NT):
                for c in range(nchunk):
                    last = nc.tensor.matmul(K.ps[0:TP, n // 4, 128 * (n % 4):128 * (n % 4) + 128],
                                            srcT[:, c, TP * n:TP * n + TP], W[:, c, :],
                                            start=c == 0, stop=c == nchunk - 1, skip_group_check=True)
                if n % 4 == 3:
                    last.then_inc(mm_done, 1)

        @block.vector
        def _(dve):
            dve.wait_ge(base_done, base0 + len(terms))
            for half in range(2):
                dve.wait_ge(mm_done, mm0 + half + 1)
                nc.vector.tensor_tensor(dst[0:TP, 4 * half:4 * half + 4, :], dst[0:TP, 4 * half:4 * half + 4, :],
                                        K.ps[0:TP, half, :].rearrange("p (n c) -> p n c", n=4), ALU.add)


def hidden_layer(nc, K, name, xT, W, bias, hT):
    h_done, h0 = K.shared("hidden_h", 2 * NF)
    with nc.Block() as block:
        @block.tensor
        def _(pe):
            for k in range(2 * NF):
                f, half = k % NF, k // NF
                nc.tensor.matmul(K.ps[:, k, 0:448], W[:, 128 * f:128 * f + 128],
                                 xT[:, 448 * half:448 * half + 448], start=True, stop=True).then_inc(h_done, 1)

        @block.scalar
        def _(act):
            for k in range(2 * NF):
                f, half = k % NF, k // NF
                act.wait_ge(h_done, h0 + k + 1)
                nc.scalar.activation(hT[:, f, 448 * half:448 * half + 448], K.ps[:, k, 0:448], ACT.Gelu,
                                     bias=bias[:, f:f + 1])


class ExpertLoader:

    def __init__(self, nc, W1_dram, W2_dram, Wb1, Wb2, w1_loaded, w2_loaded):
        self.W1, self.W2, self.Wb1, self.Wb2 = W1_dram, W2_dram, Wb1, Wb2
        self.w1_loaded, self.w2_loaded = w1_loaded, w2_loaded

    def first(self, sp, e, u):
        sp.dma_start(self.Wb1[:, u, :], self.W1[bass.ds(e, 1), :, :].rearrange("e c h -> (e c) h")
                     ).then_inc(self.w1_loaded[u], 16)

    def second(self, sp, e, u):
        sp.dma_start(self.Wb2[:, u, :, :], self.W2[bass.ds(e, 1), :, :].rearrange("e (f p) d -> (e p) f d", p=128)
                     ).then_inc(self.w2_loaded[u], 16)


def mixture(nc, K, name, X, xT, gate_w, gate_b, top, b1c, b2, load, Wb1, Wb2, hT, bufs):
    G, G2, EQ, SMALL, CW, CWT = bufs
    lg_done, k0 = K.shared("gate_lg", 1)
    sub_done, _ = K.shared("gate_sub", 1)
    ex_done, _ = K.shared("gate_ex", 1)
    cw_done, _ = K.shared("gate_cw", 1)
    cwt_done, _ = K.shared("gate_cwt", 1)
    cwt_copied, _ = K.shared("gate_cwtc", 1)
    b2_done, _ = K.shared("gate_b2", 1)
    xh_done, _ = K.shared("gate_xh", 1)
    XH, XL = K.YH[:, 0, 0:NTOK], K.YH[:, 1, 0:NTOK]
    W1H = K.YL[:, 0, 0:2 * HID].rearrange("p (u h) -> p u h", u=2)
    W1L = K.YL[:, 1, 0:2 * HID].rearrange("p (u h) -> p u h", u=2)
    h_done, g_done = K.sem(f"{name}_h"), K.sem(f"{name}_g")
    out_done, acc_done = K.sem(f"{name}_out"), K.sem(f"{name}_acc")
    col_done = K.sem(f"{name}_col")
    wh_done = K.sem(f"{name}_wh")
    split_done = K.sem(f"{name}_split")
    B1S, CWS = K.b1s, K.cws
    UNITS = 4

    added_done, _ = K.shared("gate_added", 1)

    def pe_logits():
        for n in range(NT):
            last = nc.tensor.matmul(K.ps[0:TP, 6, NE * n:NE * n + NE], xT[:, TP * n:TP * n + TP], gate_w,
                                    start=True, stop=True, skip_group_check=True)
        last.then_inc(lg_done, 1)

    def pe_gates(pe):
        pe.wait_ge(cw_done, k0 + 1)
        for n in range(NT):
            last = nc.tensor.transpose(K.ps[0:NE, 6 + n // 4, TP * (n % 4):TP * (n % 4) + TP],
                                       CW[0:TP, n, :], K.ident[0:TP, 0:TP])
        last.then_inc(cwt_done, 1)
        pe.wait_ge(cwt_copied, k0 + 1)
        for n in range(NT):
            last = nc.tensor.matmul(K.ps[0:TP, 4 + n // 4, 128 * (n % 4):128 * (n % 4) + 128],
                                    CWT[0:NE, TP * n:TP * n + TP], b2, start=True, stop=True,
                                    skip_group_check=True)
        last.then_inc(b2_done, 1)

    def dve_token_parts(dve):
        nc.vector.tensor_copy(XH, xT[:, :]).then_inc(xh_done, 1)
        dve.wait_ge(xh_done, k0 + 1)
        nc.vector.tensor_tensor(XL, xT[:, :], XH.bitcast(F32), ALU.subtract)

    def dve_gates(dve):
        o = K.chain(dve, "gate_chain")
        g, g2, eq, cw = (t[0:TP, :, :] for t in (G, G2, EQ, CW))

        def bc(col):
            return SMALL[0:TP, col, :].unsqueeze(2).broadcast_to([TP, NT, NE])

        def first_largest(src, dst, col):
            o.then(nc.vector.tensor_reduce(SMALL[0:TP, col, :], src, axis=AX.X, op=ALU.max))
            o.then(nc.vector.tensor_tensor(dst, src, bc(col), ALU.is_ge))
            o.then(nc.vector.tensor_tensor(dst, dst, K.expert_m8[0:TP, :, :], ALU.mult))
            o.then(nc.vector.tensor_reduce(SMALL[0:TP, col, :], dst, axis=AX.X, op=ALU.min))
            o.then(nc.vector.tensor_tensor(dst, K.expert_m8[0:TP, :, :], bc(col), ALU.is_equal))

        dve.wait_ge(lg_done, k0 + 1)
        lg = K.ps[0:TP, 6, 0:NT * NE].rearrange("p (n e) -> p n e", e=NE)
        if gate_b is None:
            o.then(nc.vector.tensor_copy(g, lg))
        else:
            o.then(nc.vector.tensor_tensor(g, lg, over_tiles(gate_b), ALU.add))
        o.then(nc.vector.tensor_reduce(SMALL[0:TP, 0, :], g, axis=AX.X, op=ALU.max))
        nc.vector.tensor_tensor(g, g, bc(0), ALU.subtract).then_inc(sub_done, 1)
        dve.wait_ge(ex_done, k0 + 1)
        o.then(nc.vector.tensor_reduce(SMALL[0:TP, 1, :], g, axis=AX.X, op=ALU.add))
        o.then(nc.vector.reciprocal(SMALL[0:TP, 1, :], SMALL[0:TP, 1, :]))
        o.then(nc.vector.tensor_tensor(g, g, bc(1), ALU.mult))
        first_largest(g, eq, 2)
        if top == 1:
            nc.vector.tensor_copy(cw, eq).then_inc(cw_done, 1)
        else:
            o.then(nc.vector.scalar_tensor_tensor(g2, eq, -2.0, g, ALU.mult, ALU.add))
            first_largest(g2, cw, 3)
            o.then(nc.vector.tensor_tensor(cw, cw, eq, ALU.add))
            nc.vector.tensor_tensor(cw, cw, g, ALU.mult).then_inc(cw_done, 1)
        dve.wait_ge(cwt_done, k0 + 1)
        for half in range(2):
            last = nc.vector.tensor_copy(CWT[0:NE, 448 * half:448 * half + 448], K.ps[0:NE, 6 + half, 0:448])
        last.then_inc(cwt_copied, 1)
        dve.wait_ge(b2_done, k0 + 1)
        for half in range(2):
            last = nc.vector.tensor_tensor(X[0:TP, 4 * half:4 * half + 4, :], X[0:TP, 4 * half:4 * half + 4, :],
                                           K.ps[0:TP, 4 + half, :].rearrange("p (n c) -> p n c", n=4), ALU.add)
        last.then_inc(added_done, 1)

    with nc.Block() as block:
        @block.sync
        def _(sp):
            with sp.Fori(0, NE // 2 - 1) as t:
                for u in range(2):
                    sp.wait_ge(split_done, 2 * t + u + 1)
                    load.first(sp, 2 * t + 2 + u, u)
                for u in range(2):
                    sp.wait_ge(out_done, 4 * t + 2 * u + 2)
                    load.second(sp, 2 * t + 2 + u, u)

        @block.tensor
        def _(pe):
            def hidden(t, v):
                u, half = divmod(v, 2)
                if half == 0:
                    pe.wait_ge(split_done, 2 * t + u + 1)
                for f in range(NF):
                    if not (isinstance(t, int) and v == 0):
                        pe.wait_ge(g_done, 16 * t + 4 * v + f - 3)
                    for k, (w, x) in enumerate(((W1H, XH), (W1H, XL), (W1L, XH))):
                        last = nc.tensor.matmul(K.ps[:, f, 0:448], w[:, u, 128 * f:128 * f + 128],
                                                x[:, 448 * half:448 * half + 448], start=k == 0, stop=k == 2)
                    last.then_inc(h_done, 1)

            def output(t, v):
                u, half = divmod(v, 2)
                pe.wait_ge(g_done, 16 * t + 4 * v + 4)
                if half == 0:
                    pe.wait_ge(load.w2_loaded[u], 16 * t + 16)
                if not (isinstance(t, int) and v < 2):
                    pe.wait_ge(acc_done, 4 * t + v - 1)
                for i in range(4):
                    for f in range(NF):
                        last = nc.tensor.matmul(K.ps[0:TP, 4 + v % 2, 128 * i:128 * i + 128],
                                                hT[:, v % 2, f, TP * i:TP * i + TP], Wb2[:, u, f, :],
                                                start=f == 0, stop=f == NF - 1, skip_group_check=True)
                last.then_inc(out_done, 1)

            def turn(t, first_turn=False):
                hidden(t, 0)
                for v in range(1, UNITS):
                    hidden(t, v)
                    if v == 1 and first_turn:
                        pe_gates(pe)
                        pe.wait_ge(added_done, k0 + 1)
                    output(t, v - 1)
                output(t, UNITS - 1)
            pe_logits()
            turn(0, True)
            with pe.Fori(1, NE // 2) as t:
                turn(t)

        @block.scalar
        def _(act):
            def turn(t):
                for v in range(UNITS):
                    u = v // 2
                    if v % 2 == 0:
                        act.wait_ge(split_done, 2 * t + u + 1)
                    if not (isinstance(t, int) and v < 2):
                        act.wait_ge(out_done, 4 * t + v - 1)
                    for f in range(NF):
                        act.wait_ge(h_done, 16 * t + 4 * v + f + 1)
                        nc.scalar.activation(hT[:, v % 2, f, :], K.ps[:, f, 0:448], ACT.Gelu,
                                             bias=B1S[:, u, f:f + 1]).then_inc(g_done, 1)
            act.wait_ge(sub_done, k0 + 1)
            nc.scalar.activation(G[0:TP, :, :], G[0:TP, :, :], ACT.Exp).then_inc(ex_done, 1)
            turn(0)
            with act.Fori(1, NE // 2) as t:
                turn(t)

        @block.vector
        def _(dve):
            def token_weights(t, u):
                nc.vector.tensor_copy(CWS[0:TP, u, :], CW[0:TP, :, bass.ds(2 * t + u, 1)].rearrange(
                    "p n e -> p (n e)")).then_inc(col_done, 1)

            def columns(t, u):
                if not isinstance(t, int) or t > 0:
                    dve.wait_ge(g_done, 16 * t + 8 * u - 8)
                    dve.wait_ge(acc_done, 4 * t + 2 * u - 2)
                nc.vector.tensor_copy(B1S[:, u, :], b1c[:, bass.ds(8 * t + 4 * u, 4)])
                if not (isinstance(t, int) and t == u == 0):
                    token_weights(t, u)
                dve.wait_ge(load.w1_loaded[u], 16 * t + 16)
                nc.vector.tensor_copy(W1H[:, u, :], Wb1[:, u, :]).then_inc(wh_done, 1)
                dve.wait_ge(wh_done, 2 * t + u + 1)
                nc.vector.tensor_tensor(W1L[:, u, :], Wb1[:, u, :], W1H[:, u, :].bitcast(F32),
                                        ALU.subtract).then_inc(split_done, 1)

            def turn(t, last_turn=False):
                for v in range(UNITS):
                    u, half = divmod(v, 2)
                    if v == 0:
                        columns(t, 1)
                    if v == 3 and not last_turn:
                        columns(t + 1, 0)
                    dve.wait_ge(out_done, 4 * t + v + 1)
                    if v % 2 == 0:
                        dve.wait_ge(col_done, 2 * t + u + 1)
                    if not (isinstance(t, int) and v < 2):
                        dve.wait_ge(acc_done, 4 * t + v - 1)
                    for i in range(4):
                        n = 4 * half + i
                        last = nc.vector.scalar_tensor_tensor(
                            X[0:TP, n, :], K.ps[0:TP, 4 + v % 2, 128 * i:128 * i + 128],
                            CWS[0:TP, u, n:n + 1], X[0:TP, n, :], ALU.mult, ALU.add)
                    last.then_inc(acc_done, 1)
            dve_token_parts(dve)
            columns(0, 0)
            dve_gates(dve)
            dve.wait_ge(added_done, k0 + 1)
            token_weights(0, 0)
            turn(0)
            with dve.Fori(1, NE // 2 - 1) as t:
                turn(t)
            turn(NE // 2 - 1, True)
BLOCKS = 7
STEPS = 2 * BLOCKS
GROUPS = 3
GT = 4
TT = 125
NTT = 12
GC = GT * TT
HALF = 448
BANK_V = 7
Q_STEPS = (4, 5, 7, 11)
O_STEP = 6


def score_bank(m, g):
    return 2 if g == 2 else (m % 2) * 3 + g


def t_bank(slot):
    return 5 + slot % 2


def misc_at(m, lag, nxt):
    if m in (1, 2, 3):
        return ("y", 0, m - 1)
    if m in (8, 9, 10) and nxt:
        return ("y", 1, m - 8)
    if m in Q_STEPS and nxt:
        return ("q", 0, Q_STEPS.index(m))
    if m == O_STEP and lag:
        return ("o", 0, 0)
    return None


LN_STEPS = 7


class PoolOrder:
    def __init__(self, pool, step, base):
        self.pool, self.step, self.base, self.k = pool, step, base, 0

    def then(self, ins):
        ins.then_inc(self.step, 1)
        self.k += 1
        self.pool.wait_ge(self.step, self.base + self.k)


class ContextNorm:

    def __init__(self, nc, K, name, ctx_dram, g_bc, b_bc):
        self.nc, self.K, self.g_bc, self.b_bc = nc, K, g_bc, b_bc
        self.LNS, self.yt, self.yraw = K.LNS, K.yt, K.yraw
        self.ctx_v = ctx_dram.rearrange("b (r j) c -> b r j c", j=NTT)
        self.y_loaded = [K.sem(f"{name}_y_loaded0"), K.sem(f"{name}_y_loaded1")]
        self.y_sum1, self.y_sum2 = K.sem(f"{name}_y_sum1"), K.sem(f"{name}_y_sum2")
        self.y_cent, self.y_sq = K.sem(f"{name}_y_cent"), K.sem(f"{name}_y_sq")
        self.yn_done = K.sem(f"{name}_yn_done")
        self.pool_step = K.sem(f"{name}_pool_step")
        self.yT_done = None

    def load(self, sp, k, par):
        src = self.ctx_v[bass.ds(k, 1), :, :, :].rearrange("b r j c -> (b r) j c")
        sp.dma_start(self.yraw[:, par, :, :], src).then_inc(self.y_loaded[par], 16)

    def order(self, pool, beta):
        return PoolOrder(pool, self.pool_step, LN_STEPS * beta)

    def dve_y_sum1(self, dve, beta, par):
        dve.wait_ge(self.y_loaded[par], 8 * (beta - par) + 16)
        if not (isinstance(beta, int) and beta < 2):
            dve.wait_ge(self.yn_done, beta - 1)
        self.nc.vector.tensor_reduce(self.LNS[0:TT, par, 0, :], self.yraw[:, par, :, :], axis=AX.X,
                                op=ALU.add).then_inc(self.y_sum1, 1)

    def dve_y_sum2(self, dve, beta, par):
        dve.wait_ge(self.y_sq, beta + 1)
        self.nc.vector.tensor_reduce(self.LNS[0:TT, par, 1, :], self.yt[:, par, :, 0:64], axis=AX.X,
                                op=ALU.add).then_inc(self.y_sum2, 1)

    def pool_ln1(self, o, beta, par):
        o.pool.wait_ge(self.y_sum1, beta + 1)
        ymean = self.LNS[0:TT, par, 0, :]
        o.then(self.nc.gpsimd.tensor_tensor(self.LNS[0:TT, par, 2, :], ymean, self.K.inv64, ALU.mult))
        self.nc.gpsimd.tensor_tensor(self.yraw[:, par, :, :], self.yraw[:, par, :, :],
                                self.LNS[0:TT, par, 2, :].unsqueeze(2).broadcast_to([TT, NTT, 64]),
                                ALU.subtract).then_inc(self.y_cent, 1)
        o.pool.wait_ge(self.y_cent, beta + 1)
        if self.yT_done is not None:
            o.pool.wait_ge(self.yT_done, 3 * (beta - 2) + 3)
        self.nc.gpsimd.tensor_tensor(self.yt[:, par, :, 0:64], self.yraw[:, par, :, :], self.yraw[:, par, :, :],
                                ALU.mult).then_inc(self.y_sq, 1)
        o.pool.wait_ge(self.y_sq, beta + 1)

    def pool_ln2(self, o, beta, par):
        o.pool.wait_ge(self.y_sum2, beta + 1)
        o.then(self.nc.gpsimd.tensor_tensor(self.LNS[0:TT, par, 1, :], self.LNS[0:TT, par, 1, :], self.K.inv64, ALU.mult))
        o.then(self.nc.gpsimd.tensor_tensor(self.LNS[0:TT, par, 1, :], self.LNS[0:TT, par, 1, :], self.K.eps12, ALU.add))
        o.then(self.nc.gpsimd.tensor_tensor(self.LNS[0:TT, par, 1, :], self.LNS[0:TT, par, 1, :], self.K.mhalf12[0:TT, :], ALU.pow))
        o.then(self.nc.gpsimd.tensor_tensor(self.yraw[:, par, :, :], self.yraw[:, par, :, :],
                                       self.LNS[0:TT, par, 1, :].unsqueeze(2).broadcast_to([TT, NTT, 64]),
                                       ALU.mult))
        o.then(self.nc.gpsimd.tensor_tensor(self.yraw[:, par, :, :], self.yraw[:, par, :, :],
                                       self.g_bc.unsqueeze(1).broadcast_to([TT, NTT, 64]), ALU.mult))
        o.then(self.nc.gpsimd.tensor_tensor(self.yt[:, par, :, 0:64], self.yraw[:, par, :, :],
                                       self.b_bc.unsqueeze(1).broadcast_to([TT, NTT, 64]), ALU.add))
        self.nc.gpsimd.tensor_tensor(self.yt[:, par, :, 64:128], self.yraw[:, par, :, :],
                                self.b_bc.unsqueeze(1).broadcast_to([TT, NTT, 64]),
                                ALU.add).then_inc(self.yn_done, 1)
        o.pool.wait_ge(self.yn_done, beta + 1)


def cross_attention(nc, K, name, ctx_dram, xT, M, qbias, scale, wv, oT, Zall, norm):
    nchunk = oT.shape[1]
    ps, ident = K.ps, K.ident
    PT, P, YH, YL, YF, yt, yv, yraw = K.PT, K.P, K.YH, K.YL, K.YF, K.yt, K.yv, K.yraw
    QF, Q, U, NM, MP, ZP = K.QF, K.Q, K.U, K.NM, K.MP, K.ZP

    def sem(s):
        return K.sem(f"{name}_{s}")

    with_ln = norm is not None
    if with_ln:
        y_loaded, yn_done = norm.y_loaded, norm.yn_done
    else:
        y_loaded = [sem("y_loaded0"), sem("y_loaded1")]
    yv_done = sem("yv_done")
    yT_done, yT_copied = sem("yT_done"), sem("yT_copied")
    if with_ln:
        norm.yT_done = yT_done
    yh_done, yl_done = sem("yh_done"), sem("yl_done")
    q_done, q_copied = sem("q_done"), sem("q_copied")
    qh_done, ql_done = sem("qh_done"), sem("ql_done")
    q_biased = sem("q_biased") if qbias is not None else None
    sc_done = sem("sc_done")
    mxp_done, mx_done = sem("mxp_done"), sem("mx_done")
    ex_shared, ex_done = sem("ex_shared"), sem("ex_done")
    tr_done = sem("tr_done")
    cp = [sem(f"cp{g}") for g in range(GROUPS)]
    pv_done, u_done = sem("pv_done"), sem("u_done")
    o_done, o_copied = sem("o_done"), sem("o_copied")
    z_done = sem("z_done")

    def for_pairs(eng, emit):
        emit(0, False, True, True)
        with eng.Fori(1, 7) as p:
            emit(p, True, True, True)
        emit(7, True, True, False)
        emit(8, True, False, False)

    def pe_free_t_bank(pe, p, m, g, misc, lag, cur, nxt):
        slot = 3 * m + g
        if misc:
            pm, pg = divmod(slot - 1, 3)
            blk = 14 * p + pm - 2
            if pm - 2 >= 0 or lag:
                pe.wait_ge(cp[pg], blk + 1)
            return
        before = misc_at(m - 1, lag, nxt) if g == 0 and m > 0 and cur else None
        if g == 0 and m > 0 and not cur:
            before = None
        if before:
            kind, par, k = before
            if kind == "y":
                pe.wait_ge(yT_copied, 6 * p + 3 * (par + 1) + k + 1)
            elif kind == "q":
                pe.wait_ge(q_copied, 4 * p + 4 + k + 1)
            else:
                pe.wait_ge(o_copied, p)
            return
        pm, pg = divmod(slot - 2, 3)
        if pm - 2 >= 0 or lag:
            pe.wait_ge(cp[pg], 14 * p + pm - 2 + 1)

    def pe_y_transposes(beta, par, g, bank):
        for j in range(GT):
            last = nc.tensor.transpose(ps[:, bank, TT * j:TT * j + TT], yt[:, par, GT * g + j, :],
                                       ident[0:TT, 0:TT])
        last.then_inc(yT_done, 1)

    def pe_q(p_next, k, bank):
        for h in range(4):
            last = nc.tensor.matmul(ps[:, bank, 112 * h:112 * h + 112], M[:, 4 * k + h, :],
                                    xT[:, bass.ds(112 * p_next, 112)], start=True, stop=True)
        last.then_inc(q_done, 1)

    def pe_o(bank):
        for h in range(16):
            if nchunk == 4:
                j, c, first, final = h % 4, h // 4, True, True
            else:
                j, c, first, final = h // 4, 0, h % 4 == 0, h % 4 == 3
            last = nc.tensor.matmul(ps[32 * j:32 * j + 32, bank, 112 * c:112 * c + 112],
                                    wv[:, h, :], U[:, h, :], start=first, stop=final,
                                    skip_group_check=True)
        last.then_inc(o_done, 1)

    def pe_sums(pe, beta, par, w, g):
        if g == 0 or not 6 <= w <= 11:
            return
        half, k = divmod(w - 6, 3)
        first_pair = k == 0 and g == 1
        if first_pair:
            for gg in range(GROUPS):
                pe.wait_ge(cp[gg], 7 * beta + (4 if half == 0 else 7))
            if half == 0:
                pe.wait_ge(yv_done, beta + 1)
        if first_pair and not (isinstance(beta, int) and beta == 0 and half == 0):
            pe.wait_ge(u_done, 2 * beta + half)
        for j in (4 * k + 2 * (g - 1), 4 * k + 2 * (g - 1) + 1):
            rows = slice(64 * (j % 2), 64 * (j % 2) + 64)
            last = nc.tensor.matmul(ps[rows, BANK_V, 0:HALF], yv[:, par, j, :],
                                    PT[0:TT, par, j, HALF * half:HALF * half + HALF],
                                    start=j < 2, stop=j >= NTT - 2, skip_group_check=True)
        if k == 2 and g == 2:
            last.then_inc(pv_done, 1)

    def pe_pair(pe):
        def emit(p, lag, cur, nxt):
            for m in range(STEPS if cur else BLOCKS):
                par, i = divmod(m, BLOCKS)
                n = 14 * p + m
                for g in range(GROUPS):
                    slot = 3 * m + g
                    if (lag and m < 2) or (cur and m >= 2):
                        pe_free_t_bank(pe, p, m, g, False, lag, cur, nxt)
                        if g == 0:
                            pe.wait_ge(ex_done, n - 1)
                        for j in range(GT):
                            last = nc.tensor.transpose(
                                ps[0:TT, t_bank(slot), 128 * j:128 * j + 128],
                                P[:, m % 2, GC * g + TT * j:GC * g + TT * j + TT], ident[:, :])
                        last.then_inc(tr_done, 1)
                    if g == 2:
                        misc = misc_at(m, lag, nxt)
                        if misc and (cur or misc[0] == "o"):
                            kind, mp, k = misc
                            bank = t_bank(3 * m + 3)
                            pe_free_t_bank(pe, p, m, 2, True, lag, cur, nxt) if cur else pe.wait_ge(cp[2], 112)
                            if kind == "y":
                                beta = 2 * p + 1 + mp
                                if with_ln:
                                    pe.wait_ge(yn_done, beta + 1)
                                else:
                                    pe.wait_ge(y_loaded[(1 + mp) % 2], 16 * (beta - (1 + mp) % 2) + 32)
                                pe_y_transposes(beta, (1 + mp) % 2, k, bank)
                            elif kind == "q":
                                pe_q(p + 1, k, bank)
                            else:
                                pe.wait_ge(u_done, 4 * p)
                                pe_o(bank)
                    if cur:
                        if i == 0 and g == 0:
                            pe.wait_ge(ql_done, 2 * p + par + 1)
                            pe.wait_ge(yl_done, 2 * p + par + 1)
                        if g == 0 and (lag or m >= 2):
                            pe.wait_ge(ex_done, n - 1)
                        if g == 2 and (lag or m >= 1):
                            pe.wait_ge(ex_shared, n)
                        bank = score_bank(m, g)
                        rows = Q[:, par, 128 * i:128 * i + 128]
                        nc.tensor.matmul(ps[:, bank, 0:GC], rows, YH[:, par, GC * g:GC * g + GC],
                                         start=True, stop=False)
                        nc.tensor.matmul(ps[:, bank, 0:GC], rows, YL[:, par, GC * g:GC * g + GC],
                                         start=False, stop=True).then_inc(sc_done, 1)
                    if cur:
                        if 6 <= m <= 11:
                            pe_sums(pe, 2 * p, 0, m, g)
                        if m == 13:
                            pe_sums(pe, 2 * p + 1, 1, 6, g)
                    if lag and m <= 4:
                        pe_sums(pe, 2 * p - 1, 1, m + 7, g)
        return emit

    def copy_group(eng, copy, p, m, g, lag):
        slot = 3 * m + g
        n2 = 14 * p + m - 2
        par, i = divmod((m - 2) % STEPS, BLOCKS)
        eng.wait_ge(tr_done, 3 * n2 + g + 1)
        old = not (isinstance(p, int) and 2 * p + (m - 2) // BLOCKS < 2)
        if old:
            beta = 2 * p + (m - 2) // BLOCKS
            eng.wait_ge(pv_done, 2 * beta - 3 + (i >= 3))
        copy(PT[0:TT, par, GT * g:GT * g + GT, 128 * i:128 * i + 128],
             ps[0:TT, t_bank(slot), :].rearrange("p (j c) -> p j c", j=GT)).then_inc(cp[g], 1)

    def act_pair(act):
        def emit(p, lag, cur, nxt):
            for m in range(STEPS if cur else BLOCKS):
                n = 14 * p + m
                t_here = (lag and m < 2) or (cur and m >= 2)
                if t_here:
                    copy_group(act, nc.scalar.copy, p, m, 0, lag)
                if (cur and m >= 1) or (lag and m == 0):
                    pm = (m - 1) % STEPS
                    act.wait_ge(mx_done, n)
                    if lag or m >= 3:
                        act.wait_ge(tr_done, 3 * n - 6)
                    if pm % BLOCKS == 0 and lag:
                        act.wait_ge(z_done, 2 * p + pm // BLOCKS - 1)
                    nc.scalar.activation(P[:, pm % 2, 2 * GC:3 * GC], ps[:, 2, 0:GC], ACT.Exp,
                                         bias=NM[:, pm:pm + 1], scale=scale,
                                         accum_out=ZP[:, pm, 0:1]).then_inc(ex_shared, 1)
                    b = (pm % 2) * 3
                    nc.scalar.activation(P[:, pm % 2, 0:2 * GC].rearrange("p (a b) -> p a b", a=2),
                                         ps[:, b:b + 2, 0:GC], ACT.Exp, bias=NM[:, pm:pm + 1],
                                         scale=scale, accum_out=ZP[:, pm, 1:2]).then_inc(ex_done, 1)
                if t_here:
                    copy_group(act, nc.scalar.copy, p, m, 2, lag)
                misc = misc_at(m, lag, nxt)
                if misc and (cur or misc[0] == "o"):
                    kind, mp, k = misc
                    bank = t_bank(3 * m + 3)
                    if kind == "y":
                        act_y_copy(act, 2 * p + 1 + mp, k, bank, False)
                    elif kind == "q":
                        act_q_copy(act, p + 1, k, bank, False)
                    elif kind == "o":
                        act.wait_ge(o_done, p)
                        nc.scalar.copy(oT[:, :, bass.ds(112 * (p - 1), 112)],
                                       ps[:, bank, 0:112 * nchunk].rearrange("p (c t) -> p c t", c=nchunk)
                                       ).then_inc(o_copied, 1)
                for beta, par, w, live in ((2 * p, 0, m, cur), (2 * p - 1, 1, m + 7, lag)):
                    if live and w in (8, 11):
                        half = 0 if w == 8 else 1
                        act.wait_ge(pv_done, 2 * beta + half + 1)
                        nc.scalar.copy(U[:, 8 * half:8 * half + 8, 56 * par:56 * par + 56],
                                       ps[:, BANK_V, 0:HALF].rearrange("p (h s) -> p h s", h=8)
                                       ).then_inc(u_done, 1)
        return emit

    def act_y_copy(act, beta, k, bank, first):
        act.wait_ge(yT_done, 3 * beta + k + 1)
        if not first:
            act.wait_ge(yl_done, beta)
        nc.scalar.copy(YF[:, GC * k:GC * k + GC], ps[:, bank, 0:GC]).then_inc(yT_copied, 1)

    def act_q_copy(act, p, k, bank, first):
        act.wait_ge(q_done, 4 * p + k + 1)
        if not first:
            act.wait_ge(ql_done, 2 * p)
        nc.scalar.copy(QF[:, 4 * k:4 * k + 4, :],
                       ps[:, bank, 0:448].rearrange("p (h t) -> p h t", h=4)).then_inc(q_copied, 1)

    def dve_q_high(dve, p, par, old):
        dve.wait_ge(q_copied, 4 * p + 4)
        if qbias is not None and par == 0:
            nc.vector.tensor_tensor(QF[:, :, :], QF[:, :, :], qbias[:, :].unsqueeze(2).broadcast_to([128, 16, TP]),
                                    ALU.add).then_inc(q_biased, 1)
            dve.wait_ge(q_biased, p + 1)
        if old:
            dve.wait_ge(sc_done, 42 * p + 21 * par - 21)
        nc.vector.tensor_copy(Q[:, par, :].rearrange("p (h s) -> p h s", h=16),
                              QF[:, :, 56 * par:56 * par + 56]).then_inc(qh_done, 1)

    def dve_y_high(dve, beta, par, old):
        dve.wait_ge(yT_copied, 3 * beta + 3)
        if old:
            dve.wait_ge(sc_done, 21 * (beta - 1))
        nc.vector.tensor_copy(YH[:, par, :], YF[:, :]).then_inc(yh_done, 1)

    def dve_pair(dve):
        def emit(p, lag, cur, nxt):
            for m in range(STEPS if cur else BLOCKS):
                par, i = divmod(m, BLOCKS)
                n = 14 * p + m
                if cur and m == 0:
                    dve_q_high(dve, p, 1, lag)
                if nxt and m == 12:
                    dve_q_high(dve, p + 1, 0, True)
                if cur and m == 4:
                    dve_y_high(dve, 2 * p + 1, 1, lag)
                if nxt and m == 11:
                    dve_y_high(dve, 2 * p + 2, 0, True)
                if with_ln and nxt and i == 1:
                    norm.dve_y_sum1(dve, 2 * p + par + 2, par)
                if with_ln and nxt and i == 3:
                    norm.dve_y_sum2(dve, 2 * p + par + 2, par)
                if (lag and m < 2) or (cur and m >= 2):
                    copy_group(dve, nc.vector.tensor_copy, p, m, 1, lag)
                if cur:
                    b = (m % 2) * 3
                    dve.wait_ge(sc_done, 3 * n + 2)
                    nc.vector.tensor_reduce(MP[:, m, 0:1], ps[:, b:b + 2, 0:GC], axis=AX.XY, op=ALU.max)
                    dve.wait_ge(sc_done, 3 * n + 3)
                    nc.vector.tensor_reduce(MP[:, m, 1:2], ps[:, 2, 0:GC], axis=AX.X,
                                            op=ALU.max).then_inc(mxp_done, 1)
                    dve.wait_ge(mxp_done, n + 1)
                    nc.vector.tensor_scalar(NM[:, m:m + 1], MP[:, m, 0:1], MP[:, m, 1:2], -scale,
                                            ALU.max, ALU.mult).then_inc(mx_done, 1)
        return emit

    def pool_y_low(o, beta, par, old):
        o.pool.wait_ge(yh_done, beta + 1)
        if old:
            o.pool.wait_ge(sc_done, 21 * (beta - 1))
        nc.gpsimd.tensor_tensor(YL[:, par, :], YF[:, :], YH[:, par, :].bitcast(F32),
                                ALU.subtract).then_inc(yl_done, 1)
        o.pool.wait_ge(yl_done, beta + 1)

    def pool_q_low(o, beta, p, par):
        o.pool.wait_ge(qh_done, beta + 1)
        nc.gpsimd.tensor_tensor(Q[64:128, par, :].rearrange("p (h s) -> p h s", h=16),
                                QF[64:128, :, 56 * par:56 * par + 56],
                                Q[64:128, par, :].rearrange("p (h s) -> p h s", h=16).bitcast(F32),
                                ALU.subtract).then_inc(ql_done, 1)
        o.pool.wait_ge(ql_done, beta + 1)

    def pool_yv(o, beta, par, old):
        if with_ln:
            o.pool.wait_ge(yn_done, beta + 1)
        else:
            o.pool.wait_ge(y_loaded[par], 16 * (beta - par) + 32)
        if old:
            o.pool.wait_ge(pv_done, 2 * beta - 2)
        nc.gpsimd.tensor_tensor(yv[:, par, :, :], yt[:, par, :, 0:64], K.zero_bc, ALU.add).then_inc(yv_done, 1)
        o.pool.wait_ge(yv_done, beta + 1)

    def pool_z(o, beta, par):
        o.pool.wait_ge(ex_done, 7 * beta + 7)
        nc.gpsimd.tensor_tensor(Zall[:, bass.ds(7 * beta, 7)], ZP[:, 7 * par:7 * par + 7, 0],
                                ZP[:, 7 * par:7 * par + 7, 1], ALU.add).then_inc(z_done, 1)
        o.pool.wait_ge(z_done, beta + 1)

    PRE = 2 * LN_STEPS if with_ln else 0

    def pool_pair(pool):
        def emit(p, lag, cur, nxt):
            o = PoolOrder(pool, norm.pool_step if with_ln else None, PRE + 2 * LN_STEPS * p)
            for par in range(2 if cur else 1):
                beta = 2 * p + par
                if cur and par == 0:
                    pool_q_low(o, beta + 1, p, 1)
                if cur:
                    pool_yv(o, beta, par, lag)
                if par == 1 or lag:
                    pool_z(o, beta - 1, (par + 1) % 2)
                if with_ln and nxt:
                    norm.pool_ln1(o, beta + 2, par)
                if (par == 0 and cur) or nxt:
                    pool_y_low(o, beta + 1, (par + 1) % 2, lag or par == 1)
                if par == 1 and nxt:
                    pool_q_low(o, beta + 1, p + 1, 0)
                if with_ln and nxt:
                    norm.pool_ln2(o, beta + 2, par)
        return emit

    ctx_v = ctx_dram.rearrange("b (r j) c -> b r j c", j=NTT)

    with nc.Block() as block:
        @block.sync
        def _(sp):
            def load(k, par):
                src = ctx_v[bass.ds(k, 1), :, :, :].rearrange("b r j c -> (b r) j c")
                if with_ln:
                    norm.load(sp, k, par)
                else:
                    for half in range(2):
                        sp.dma_start(yt[:, par, :, 64 * half:64 * half + 64], src).then_inc(y_loaded[par], 16)

            if not with_ln:
                load(0, 0)
                load(1, 1)
            with sp.Fori(0, 7) as p:
                for par in range(2):
                    k = 2 * p + 2 + par
                    if with_ln:
                        sp.wait_ge(yn_done, k - 1)
                    else:
                        sp.wait_ge(yv_done, k - 1)
                        sp.wait_ge(yT_done, 3 * k - 3)
                    load(k, par)

        @block.tensor
        def _(pe):
            for k in range(4):
                if k >= 2:
                    pe.wait_ge(q_copied, k - 1)
                pe_q(0, k, 5 + k % 2)
            if with_ln:
                pe.wait_ge(yn_done, 1)
            else:
                pe.wait_ge(y_loaded[0], 32)
            for g in range(3):
                if g < 2:
                    pe.wait_ge(q_copied, 3 + g)
                else:
                    pe.wait_ge(yT_copied, 1)
                pe_y_transposes(0, 0, g, 5 + g % 2)
            pe.wait_ge(yT_copied, 3)
            for_pairs(pe, pe_pair(pe))

        @block.scalar
        def _(act):
            for k in range(4):
                act_q_copy(act, 0, k, 5 + k % 2, True)
            for g in range(3):
                act_y_copy(act, 0, g, 5 + g % 2, True)
            for_pairs(act, act_pair(act))

        @block.vector
        def _(dve):
            dve_q_high(dve, 0, 0, False)
            dve_y_high(dve, 0, 0, False)
            dve.wait_ge(yh_done, 1)
            nc.vector.tensor_tensor(YL[:, 0, :], YF[:, :], YH[:, 0, :].bitcast(F32),
                                    ALU.subtract).then_inc(yl_done, 1)
            for_pairs(dve, dve_pair(dve))

        @block.gpsimd
        def _(pool):
            pool_q_low(PoolOrder(pool, None, 0), 0, 0, 0)
            for_pairs(pool, pool_pair(pool))


def block_selector(pool_order, nc, t, width, group):
    o = pool_order
    o.then(nc.gpsimd.memset(t, 1.0))
    o.then(nc.gpsimd.affine_select(t, t, pattern=[[1, width]], compare_op=ALU.is_ge, fill=0.0,
                                   base=0, channel_multiplier=-group))
    o.then(nc.gpsimd.affine_select(t, t, pattern=[[-1, width]], compare_op=ALU.is_ge, fill=0.0,
                                   base=group - 1, channel_multiplier=group))


def group_mask(pool_order, nc, t, heads, group):
    o = pool_order
    o.then(nc.gpsimd.memset(t, 1.0))
    o.then(nc.gpsimd.affine_select(t, t, pattern=[[-group, heads]], compare_op=ALU.is_ge, fill=0.0,
                                   base=0, channel_multiplier=1))
    o.then(nc.gpsimd.affine_select(t, t, pattern=[[group, heads]], compare_op=ALU.is_ge, fill=0.0,
                                   base=group - 1, channel_multiplier=-1))


class Arena:

    def __init__(self, flat):
        self.flat, self.at = flat, 0

    def take(self, *shape, parts=128):
        n = 1
        for s in shape:
            n *= s
        v = self.flat[0:parts, self.at:self.at + n]
        self.at += n
        assert self.at <= self.flat.shape[1]
        if len(shape) == 2:
            v = v.rearrange("p (a b) -> p a b", a=shape[0])
        elif len(shape) == 3:
            v = v.rearrange("p (a b c) -> p a b c", a=shape[0], b=shape[1])
        return v


def decoder_kernel(nc, d, out):
    with ExitStack() as ctx:
        build(nc, d, out, Kit(nc, ctx))


def build(nc, d, out, K):
    xin = d["x"].rearrange("b s c -> (b s) c")
    yout = out.rearrange("b s c -> (b s) c")

    K.ps = K.ctx.enter_context(nc.psum_tensor("ps", [128, 8, 512], F32))
    arena = K.sb("arena", [128, 2 * NTT * 896])
    K.PT = arena[:, :].rearrange("p (u j c) -> p u j c", u=2, j=NTT)
    K.P = K.sb("P", [128, 2, NTT * TT])
    K.YH, K.YL = K.sb("YH", [128, 2, NTT * TT], F32R), K.sb("YL", [128, 2, NTT * TT], F32R)
    K.YF = K.sb("YF", [128, NTT * TT])
    K.yt = K.sb("yt", [TT, 2, NTT, 128])
    K.yv, K.yraw = K.sb("yv", [TT, 2, NTT, 64]), K.sb("yraw", [TT, 2, NTT, 64])
    K.QF, K.Q = K.sb("QF", [128, 16, TP]), K.sb("Q", [128, 2, 16 * SQ], F32R)
    K.U = K.sb("U", [128, 16, TP])
    K.NM, K.MP, K.ZP = K.sb("NM", [128, STEPS]), K.sb("MP", [128, STEPS, 2]), K.sb("ZP", [128, STEPS, 2])
    K.LNS = K.sb("LNS", [128, 2, 3, NTT])
    K.b1s, K.cws = K.sb("b1s", [128, 2, NF]), K.sb("cws", [TP, 2, NT])
    K.ln_stats, K.ln_mv = K.sb("ln_stats", [TP, NT, 6]), K.sb("ln_mv", [TP, NT, 2])
    K.ln_rstd = K.sb("ln_rstd", [TP, 2, NT])
    X = K.sb("X", [TP, NT, CH])
    xnT = K.sb("xnT", [128, NTOK])
    oT = K.sb("oT", [128, 4, NTOK])
    Zall = K.sb("Zall", [128, BLOCKS * NB])
    M = K.sb("M", [128, 16, 128])
    wv = K.sb("wv", [128, 16, 32])
    qbias = K.sb("qbias", [128, 16])
    K.ident = K.sb("ident", [128, 128])
    K.mhalf12, inv64 = K.sb("mhalf12", [128, NTT]), K.sb("inv64", [TT, NTT])
    eps12, zero = K.sb("eps12", [TT, NTT]), K.sb("zero", [TT, 1])
    K.inv64, K.eps12 = inv64[:, :], eps12[:, :]
    K.zero_bc = zero[:, :].unsqueeze(2).broadcast_to([TT, NTT, CTX_C])
    K.expert_m8 = K.sb("expert_m8", [TP, NT, NE])
    hm0, hm1 = K.sb("hm0", [128, 4]), K.sb("hm1", [128, 16])
    lny = K.sb("lny", [TT, 2, CTX_C])
    VECS = ["L0_xattn_a1_lnx_g", "L0_xattn_a1_lnx_b", "L0_xattn_a1_lny_g", "L0_xattn_a1_lny_b",
            "L0_xattn_a1_ln3_g", "L0_xattn_a1_ln3_b", "L0_xattn_a2_lnx_g", "L0_xattn_a2_lnx_b",
            "L0_xattn_a2_ln3_g", "L0_xattn_a2_ln3_b", "L1_xattn_bv"]
    MATS = [("L0_xattn_a1_li2_b", NF), ("L0_xattn_a2_li2_b", NF), ("L0_ffn_b1", NE * NF),
            ("L1_ffn_b1", NE * NF), ("L0_ffn_w_gate", NE)]
    at, ncols = {}, 0
    for v, n in [(v, 1) for v in VECS] + MATS:
        at[v] = (ncols, ncols + n)
        ncols += n
    cols = K.sb("cols", [128, ncols])

    def col(v):
        a, b = at[v]
        return cols[:, a:b]

    K.z_dram = nc.dram_tensor("z_scratch", [BLOCKS * NB, 128], F32).ap()

    A = Arena(arena)
    XA, XO = A.take(NT, CH), A.take(NT, CH)
    ynT = A.take(NTOK)
    qT_at = A.at
    qT, kT = A.take(4, NTOK + 8), A.take(4, NTOK)
    hT = arena[:, qT_at:qT_at + NF * NTOK].rearrange("p (f t) -> p f t", f=NF)
    a1 = {k: A.take(512) for k in ("wq", "wk", "wv")}
    li1, li2, li3 = A.take(4, CH), A.take(HID), A.take(NF, CH)
    QS, KS, YS, VS = A.take(4, CH), A.take(4, 2, 4 * SQ), A.take(2, CH), A.take(2, 512)
    E, AT, MX, SM = A.take(16, 64), A.take(8, 120), A.take(16), A.take(16)
    E2 = arena[:, NT * CH:NT * CH + 16 * 64].rearrange("p (h s) -> p h s", h=16)
    WQ2, WK2 = A.take(512), A.take(512)
    F = Arena(arena)
    F.at = qT_at
    WQT, WKT, WKM = F.take(4, CH), F.take(4, CTX_C), F.take(16, CTX_C)
    rows = {k: A.take(CH, parts=TP) for k in ("ln1_g", "ln1_b", "ln2_g", "ln2_b", "a1_li1_b", "a1_li3_b")}
    stage = A.take(CH)
    mask, mask_b = A.take(SQ), A.take(SQ)
    K.mask = mask

    A1, A2 = "L0_xattn_a1_", "L0_xattn_a2_"
    x_loaded, rows_loaded, vecs_loaded = K.sem("x_loaded"), K.sem("rows_loaded"), K.sem("vecs_loaded")
    a1_loaded, a2_loaded = K.sem("a1_loaded"), K.sem("a2_loaded")
    const_step = K.sem("const_step")
    cols_done = K.sem("cols_done")

    def bcast(v, n=TP):
        return v.unsqueeze(0).broadcast_to([n, v.shape[0]])

    def by_head(w):
        return w.rearrange("h c d -> c h d")

    def heads_of(t, parts=128):
        return t[0:parts, :].rearrange("p (h d) -> p h d", h=16)

    def load_vectors(sp):
        for v in VECS:
            sp.dma_start(stage[at[v][0]:at[v][1], :], d[v].unsqueeze(0)).then_inc(vecs_loaded, 16)
        for v, n in MATS:
            src = d[v]
            if len(src.shape) == 1:
                src = src.rearrange("(f p) -> f p", p=128)
            elif src.shape[1] == HID:
                src = src.rearrange("e (f p) -> (e f) p", p=128)
            sp.dma_start(stage[at[v][0]:at[v][1], :], src).then_inc(vecs_loaded, 16)
        sp.wait_ge(rows_loaded, 32)

    def load_a1(sp):
        for k in ("wq", "wk", "wv"):
            sp.dma_start(heads_of(a1[k]), by_head(d[A1 + k])).then_inc(a1_loaded, 16)
        sp.dma_start(li1, d[A1 + "li1_w"].rearrange("(c p) o -> p c o", p=128)).then_inc(a1_loaded, 16)
        sp.dma_start(li2, d[A1 + "li2_w"]).then_inc(a1_loaded, 16)
        sp.dma_start(li3, d[A1 + "li3_w"].rearrange("(c p) o -> p c o", p=128)).then_inc(a1_loaded, 16)
        sp.wait_ge(vecs_loaded, 16 * (len(VECS) + len(MATS)))

    def load_a2(sp):
        for k in ("ln2_g", "ln2_b", "a1_li1_b", "a1_li3_b"):
            sp.dma_start(rows[k], bcast(d["L0_xattn_" + k])).then_inc(rows_loaded, 16)
        for i, k in enumerate(("g", "b")):
            sp.dma_start(lny[:, i, :], bcast(d[A2 + "lny_" + k], TT)).then_inc(rows_loaded, 16)
        sp.dma_start(heads_of(WQ2), by_head(d[A2 + "wq"])).then_inc(a2_loaded, 16)
        sp.dma_start(heads_of(WK2, 64), by_head(d[A2 + "wk"])).then_inc(a2_loaded, 16)
        for half in range(2):
            sp.dma_start(wv[64 * half:64 * half + 64, :, :], by_head(d[A2 + "wv"])).then_inc(a2_loaded, 16)
        sp.wait_ge(a1_loaded, 96)
        sp.wait_ge(rows_loaded, 128)

    with nc.Block() as block:
        @block.sync
        def _(sp):
            sp.dma_start(X[:, :, :], row_tiles(xin)).then_inc(x_loaded, 16)
            for k in ("ln1_g", "ln1_b"):
                sp.dma_start(rows[k], bcast(d["L0_xattn_" + k])).then_inc(rows_loaded, 16)
            sp.wait_ge(x_loaded, 16)

        @block.vector
        def _(dve):
            nc.vector.memset(K.mhalf12[:, :], -0.5)
            nc.vector.memset(inv64[:, :], 1.0 / CTX_C)
            nc.vector.memset(eps12[:, :], EPS)
            nc.vector.memset(zero[:, :], 0.0)
            nc.vector.memset(QS, 0.0)
            nc.vector.memset(KS, 0.0)
            nc.vector.memset(YS, 0.0)
            nc.vector.memset(E, 0.0)
            nc.vector.memset(E2, 0.0)
            nc.vector.memset(qT[:, :, NTOK:NTOK + 8], 0.0)
            for e in range(NE):
                nc.vector.memset(K.expert_m8[:, :, e:e + 1], float(e - NE))

        @block.gpsimd
        def _(pool):
            o = Chain(pool, const_step)
            o.then(nc.gpsimd.memset(K.ident[:, :], 1.0))
            o.then(nc.gpsimd.affine_select(K.ident[:, :], K.ident[:, :], pattern=[[-1, 128]],
                                           compare_op=ALU.is_equal, fill=0.0, base=0, channel_multiplier=1))
            for t, base in ((mask, 0), (mask_b, 64)):
                o.then(nc.gpsimd.memset(t, 1.0))
                o.then(nc.gpsimd.affine_select(t, t, pattern=[[1, SQ]], compare_op=ALU.is_gt, fill=0.0,
                                               base=base, channel_multiplier=-1))
            o.then(nc.gpsimd.affine_select(mask_b, mask_b, pattern=[[0, SQ]], compare_op=ALU.is_ge, fill=0.0,
                                           base=-64, channel_multiplier=1))
            o.then(nc.gpsimd.tensor_tensor(mask, mask, mask_b, ALU.add))
            group_mask(o, nc, hm0[:, :], 4, 32)
            group_mask(o, nc, hm1[:, :], 16, 8)

    norm = ContextNorm(nc, K, "xa0", d["ctx_512"], lny[:, 0, :], lny[:, 1, :])
    layer_norm(nc, K, "ln_in", X, XA, prefetch=load_vectors)
    layer_norm(nc, K, "ln1", XA, XA, affine=(X, rows["ln1_g"], rows["ln1_b"]),
               prefetch=load_a1)
    with nc.Block() as block:
        @block.tensor
        def _(pe):
            nc.tensor.transpose(K.ps[:, 0, 0:ncols], stage[0:ncols, :], K.ident[0:ncols, 0:ncols]
                                ).then_inc(cols_done, 1)

        @block.vector
        def _(dve):
            dve.wait_ge(cols_done, 1)
            nc.vector.tensor_copy(cols[:, :], K.ps[:, 0, 0:ncols])

    layer_norm(nc, K, "ln_xy", X, XA,
               outs=[(xnT, col(A1 + "lnx_g"), col(A1 + "lnx_b")), (ynT, col(A1 + "lny_g"), col(A1 + "lny_b"))],
               prefetch=load_a2)
    self_attention(nc, K, xnT, ynT, qT, kT, a1["wq"], a1["wk"], a1["wv"], oT,
                   (QS, KS, YS, VS, (E, E2), AT, MX, SM), 32 ** -0.5, norm)
    project_and_add(nc, K, "sa_out", XO, [X], rows["a1_li1_b"], oT, li1)
    layer_norm(nc, K, "ln3a", XO, XA, outs=[(xnT, col(A1 + "ln3_g"), col(A1 + "ln3_b"))])
    hidden_layer(nc, K, "ff1", xnT, li2, col(A1 + "li2_b"), hT)
    project_and_add(nc, K, "ff1_out", X, [X, XO], rows["a1_li3_b"], hT, li3)
    layer_norm(nc, K, "ln2", X, XA, affine=(X, rows["ln2_g"], rows["ln2_b"]))

    layer_norm(nc, K, "ln_x2", X, XA, outs=[(xnT, col(A2 + "lnx_g"), col(A2 + "lnx_b"))],
               prefetch=lambda sp: sp.wait_ge(a2_loaded, 64))
    fold_query_weights(nc, K, "fold0", WQ2, WK2, 4, hm0[:, :], M, WQT, WKT, WKM)
    cross_attention(nc, K, "xa0", d["ctx_512"], xnT, M, None, 32 ** -0.5, wv, oT, Zall, norm)

    B = Arena(arena)
    XA, XO, XI = B.take(NT, CH), B.take(NT, CH), B.take(NT, CH)
    hT = B.take(NF, NTOK)
    li1, li2, li3 = B.take(4, CH), B.take(HID), B.take(NF, CH)
    li1_b, li3_b = B.take(CH, parts=TP), B.take(CH, parts=TP)
    zt, rzt = B.take(CH), B.take(16, SQ)
    sel = B.take(4, CH)
    Wb1, Wb2, hM = B.take(2, HID), B.take(2, NF, CH), B.take(2, NF, 448)
    b2, gw, bg = B.take(CH, parts=NE), B.take(NE), B.take(NE, parts=TP)
    moe = (B.take(NT, NE), B.take(NT, NE), B.take(NT, NE), B.take(4, NT), B.take(NT, NE), B.take(NTOK, parts=NE))
    WQ1, WK1, Wo = B.take(CH), B.take(CH), B.take(1, CH)
    WQT1, WKT1, WKM1 = B.take(1, CH), B.take(1, CTX_C), B.take(16, CTX_C)
    bq_row, bq_tmp = B.take(CH), B.take(CH)

    def selector(name, nchunk, group):
        with nc.Block() as block:
            @block.gpsimd
            def _(pool):
                block_selector(K.chain(pool, "sel_chain"), nc, sel[0:16, 0:nchunk, :].rearrange("p c f -> p (c f)"),
                               128 * nchunk, group)

    post_loaded = K.sem("post_loaded")

    def load_post(sp):
        for dst, src in ((li1, d[A2 + "li1_w"].rearrange("(c p) o -> p c o", p=128)),
                         (li1_b, bcast(d[A2 + "li1_b"])), (li3_b, bcast(d[A2 + "li3_b"])),
                         (li2, d[A2 + "li2_w"]),
                         (li3, d[A2 + "li3_w"].rearrange("(c p) o -> p c o", p=128)),
                         (XI[0:TP, :, :], row_tiles(xin))):
            sp.dma_start(dst, src).then_inc(post_loaded, 16)
        sp.wait_ge(post_loaded, 96)

    selector("sel0", 4, 32)
    normalise_attention(nc, K, "nrm0", Zall, oT, sel, None, zt, rzt, prefetch=load_post)
    project_and_add(nc, K, "xa0_out", XO, [X], li1_b, oT, li1)
    layer_norm(nc, K, "ln3b", XO, XA, outs=[(xnT, col(A2 + "ln3_g"), col(A2 + "ln3_b"))])
    hidden_layer(nc, K, "ff2", xnT, li2, col(A2 + "li2_b"), hT)
    project_and_add(nc, K, "ff2_out", X, [X, XO, XI], li3_b, hT, li3)

    m0_small, small0 = K.shared("small_loaded", 16)
    load0 = ExpertLoader(nc, d["L0_ffn_W1"], d["L0_ffn_W2"], Wb1, Wb2,
                         [K.sem("m0_w1_even"), K.sem("m0_w1_odd")], [K.sem("m0_w2_even"), K.sem("m0_w2_odd")])

    def load_m0(sp):
        sp.dma_start(b2, d["L0_ffn_b2"]).then_inc(m0_small, 16)
        for u in range(2):
            load0.first(sp, u, u)
            load0.second(sp, u, u)
        sp.wait_ge(m0_small, 16)

    layer_norm(nc, K, "ln_m0", X, XA, outs=[(xnT, None, None)], prefetch=load_m0)
    mixture(nc, K, "moe0", X, xnT, col("L0_ffn_w_gate"), None, 2, col("L0_ffn_b1"), b2, load0,
            Wb1, Wb2, hM, moe)

    l1_loaded, wv_zero = K.sem("l1_loaded"), K.sem("wv_zero")
    with nc.Block() as block:
        @block.vector
        def _(dve):
            nc.vector.memset(wv[:, :, :], 0.0).then_inc(wv_zero, 1)

        @block.sync
        def _(sp):
            sp.dma_start(WQ1, d["L1_xattn_Wq"]).then_inc(l1_loaded, 16)
            for half in range(2):
                sp.dma_start(WK1[64 * half:64 * half + 64, :], d["L1_xattn_Wk"]).then_inc(l1_loaded, 16)
            sp.dma_start(bq_row, bcast(d["L1_xattn_bq"], 128)).then_inc(l1_loaded, 16)
            sp.wait_ge(wv_zero, 1)
            src = d["L1_xattn_Wv"].rearrange("c (a j k) -> c a j k", j=4, k=8)
            dst = wv[:, :, :].rearrange("p (a j) k -> p a j k", j=4)
            for half in range(2):
                for j in range(4):
                    sp.dma_start(dst[64 * half:64 * half + 64, :, j, 8 * j:8 * j + 8], src[:, :, j, :]
                                 ).then_inc(l1_loaded, 16)
    layer_norm(nc, K, "ln_x3", X, XA, outs=[(xnT, None, None)], prefetch=lambda sp: sp.wait_ge(l1_loaded, 192))
    fold_query_weights(nc, K, "fold1", WQ1, WK1, 1, hm1[:, :], M, WQT1, WKT1, WKM1, bq_row, qbias, bq_tmp)
    oT1 = oT[:, 0:1, :]
    cross_attention(nc, K, "xa1", d["ctx_512"], xnT, M, qbias, 8 ** -0.5, wv, oT1, Zall, None)

    wo_loaded = K.sem("wo_loaded")

    def load_wo(sp):
        sp.dma_start(Wo[:, 0, :], d["L1_xattn_Wo"]).then_inc(wo_loaded, 16)
        sp.dma_start(li1_b, bcast(d["L1_xattn_bo"])).then_inc(wo_loaded, 16)
        sp.wait_ge(wo_loaded, 32)

    selector("sel1", 1, 8)
    normalise_attention(nc, K, "nrm1", Zall, oT1, sel, col("L1_xattn_bv"), zt, rzt, prefetch=load_wo)
    project_and_add(nc, K, "xa1_out", X, [X], li1_b, oT1, Wo)

    m1_small, small0 = K.shared("small_loaded", 48)
    load1 = ExpertLoader(nc, d["L1_ffn_W1"], d["L1_ffn_W2"], Wb1, Wb2,
                         [K.sem("m1_w1_even"), K.sem("m1_w1_odd")], [K.sem("m1_w2_even"), K.sem("m1_w2_odd")])

    def load_m1(sp):
        sp.dma_start(b2, d["L1_ffn_b2"]).then_inc(m1_small, 16)
        sp.dma_start(gw, d["L1_ffn_Wg"]).then_inc(m1_small, 16)
        sp.dma_start(bg, bcast(d["L1_ffn_bg"])).then_inc(m1_small, 16)
        for u in range(2):
            load1.first(sp, u, u)
            load1.second(sp, u, u)
        sp.wait_ge(m1_small, small0 + 48)

    layer_norm(nc, K, "ln_m1", X, XA, outs=[(xnT, None, None)], prefetch=load_m1)
    mixture(nc, K, "moe1", X, xnT, gw, bg, 1, col("L1_ffn_b1"), b2, load1, Wb1, Wb2, hM, moe)

    out_stored = K.sem("out_stored")
    with nc.Block() as block:
        @block.sync
        def _(sp):
            sp.dma_start(row_tiles(yout), X[:, :, :]).then_inc(out_stored, 16)
            sp.wait_ge(out_stored, 16)


def kernel(**inputs):
    import numpy as _np
    import concourse.bacc as _bacc
    from concourse import mybir as _mybir
    from concourse.bass_utils import run_bass_kernel_spmd as _run

    nc = _bacc.Bacc("TRN2", target_bir_lowering=False, num_devices=1)
    arrays, d = {}, {}
    for name in inputs:
        a = _np.ascontiguousarray(inputs[name])
        arrays[f"in_{name}_dram"] = a
        d[name] = nc.dram_tensor(f"in_{name}_dram", a.shape, _mybir.dt.from_np(a.dtype), kind="ExternalInput").ap()
    out = nc.dram_tensor("out_0_dram", (NB, SQ, CH), _mybir.dt.float32, kind="ExternalOutput").ap()
    decoder_kernel(nc, d, out)
    r = _run(nc, [arrays], core_ids=[0])
    return r.results[0]["out_0_dram"]
```
